# Optimizing a Trainium2 kernel written in Bass

```python
import numpy as np
import jax
import jax.numpy as jnp

def _softmax(x, axis=-1):
    return jax.nn.softmax(x, axis=axis)

def _gelu(x):
    return jax.nn.gelu(x, approximate=True)

def _silu(x):
    return jax.nn.silu(x)

def _sigmoid(x):
    return jax.nn.sigmoid(x)

def _layernorm(x, axis=-1, eps=1e-05):
    m = jnp.mean(x, axis=axis, keepdims=True)
    v = jnp.var(x, axis=axis, keepdims=True)
    return (x - m) / jnp.sqrt(v + eps)

def _scatter_add(tgt, idx, src, axis=0):
    return tgt.at[idx].add(src)

def _segment_sum(src, seg, n):
    return jax.ops.segment_sum(src, seg, n)
kernel_name = 'mk_gnn_ffn_d1_gnn_r8_512a59'

def setup_inputs(seed: int=0):
    np.random.seed(seed)
    _w = jnp.asarray

    def _rec_inputs():
        import jax
        import jax.numpy as jnp
        _gk = jax.random.key(seed)
        x = -0.0001126 + 1 * jax.random.normal(jax.random.fold_in(_gk, 1), (3750, 256), jnp.float32)
        _s = jax.random.randint(jax.random.fold_in(_gk, 2), (60000,), 0, 3750, jnp.int32)
        _d = jax.random.randint(jax.random.fold_in(_gk, 3), (60000,), 0, 3750, jnp.int32)
        _loop = jnp.arange(3750, dtype=jnp.int32)
        src = jnp.concatenate([_s, _d, _loop])
        dst = jnp.concatenate([_d, _s, _loop])
        _o = jnp.argsort(dst, stable=True)
        src = src[_o]
        dst = dst[_o]
        edge_type_8 = jax.random.randint(jax.random.fold_in(_gk, 12), (123750,), 0, 8, jnp.int32)
        return (x, src, dst, edge_type_8)
    x, src, dst, edge_type_8 = _rec_inputs()

    def _L0_gnn_setup():
        import jax, jax.numpy as jnp
        import numpy as np
        N_NODES = 3750
        N_EDGES = 60000
        IN_FEAT = 256
        OUT_FEAT = 256
        N_RELS = 8
        N_HEADS = 4
        HEAD_DIM = OUT_FEAT // N_HEADS
        LEAKY_SLOPE = 0.2
        key = jax.random.key(seed)
        ks = jax.random.split(key, 8)
        inputs = jax.random.normal(ks[0], (N_NODES, IN_FEAT), dtype=jnp.float32)
        conv_weights = jax.random.normal(ks[1], (N_RELS, N_HEADS, IN_FEAT, HEAD_DIM), dtype=jnp.float32) * (1.0 / np.sqrt(IN_FEAT))
        attn_l = jax.random.normal(ks[2], (N_RELS, N_HEADS, HEAD_DIM), dtype=jnp.float32) * 0.1
        attn_r = jax.random.normal(ks[3], (N_RELS, N_HEADS, HEAD_DIM), dtype=jnp.float32) * 0.1
        h_bias = jax.random.normal(ks[4], (OUT_FEAT,), dtype=jnp.float32) * 0.02
        edge_src = jax.random.randint(ks[5], (N_EDGES,), 0, N_NODES, dtype=jnp.int32)
        edge_dst = jax.random.randint(ks[6], (N_EDGES,), 0, N_NODES, dtype=jnp.int32)
        edge_type = jax.random.randint(ks[7], (N_EDGES,), 0, N_RELS, dtype=jnp.int32)
        return {'inputs': inputs, 'conv_weights': conv_weights, 'attn_l': attn_l, 'attn_r': attn_r, 'h_bias': h_bias, 'edge_src': edge_src, 'edge_dst': edge_dst, 'edge_type': edge_type}
    _L0_gnn_all = _L0_gnn_setup()
    _L0_gnn_in = {k: v for k, v in _L0_gnn_all.items() if k in ('conv_weights', 'attn_l', 'attn_r', 'h_bias')}
    del _L0_gnn_all

    def _L0_ffn_setup():
        import jax, jax.numpy as jnp
        import numpy as np
        B, N, D = (16, 512, 256)
        NUM_EXPERTS, TOP_K, HEADS = (4, 2, 4)
        N_EDGES = 131072
        LN_EPS = 1e-05

        def _layernorm(x, g, b):
            mu = x.mean(-1, keepdims=True)
            var = ((x - mu) ** 2).mean(-1, keepdims=True)
            return (x - mu) * jax.lax.rsqrt(var + LN_EPS) * g + b

        def _forward(x, edge_index, W_gat, att_src, att_dst, b_gat, ln_gamma, ln_beta, W1, b1, W2, b2):
            Bc, Nc, Dc = x.shape
            M = Bc * Nc
            x_flat = x.reshape(M, Dc)
            h = (x_flat @ W_gat).reshape(M, HEADS, NUM_EXPERTS)
            loops = jnp.arange(M, dtype=edge_index.dtype)
            src = jnp.concatenate([edge_index[0], loops])
            dst = jnp.concatenate([edge_index[1], loops])
            a_src = (h * att_src).sum(-1)
            a_dst = (h * att_dst).sum(-1)
            e = jax.nn.leaky_relu(a_src[src] + a_dst[dst], negative_slope=0.2)
            e_max = jax.ops.segment_max(e, dst, num_segments=M)
            ee = jnp.exp(e - e_max[dst])
            denom = jax.ops.segment_sum(ee, dst, num_segments=M)
            alpha = ee / (denom[dst] + 1e-16)
            msg = h[src] * alpha[:, :, None]
            agg = jax.ops.segment_sum(msg, dst, num_segments=M).reshape(M, HEADS * NUM_EXPERTS) + b_gat
            scores = _layernorm(agg, ln_gamma, ln_beta).reshape(M, HEADS, NUM_EXPERTS).mean(1)
            scores = scores.reshape(Bc, Nc, NUM_EXPERTS)
            topk_s, topk_i = jax.lax.top_k(scores, TOP_K)
            w = jax.nn.softmax(topk_s, axis=-1)
            out = jnp.zeros_like(x)
            for ei in range(NUM_EXPERTS):
                g = jnp.where(topk_i == ei, w, 0.0).sum(-1)
                hh = jax.nn.gelu(x @ W1[ei] + b1[ei], approximate=False)
                out = out + g[..., None] * (hh @ W2[ei] + b2[ei])
            return out
        key = jax.random.key(seed)
        ks = jax.random.split(key, 8)
        s = 0.05
        return {'x': jax.random.normal(ks[0], (B, N, D), jnp.float32), 'W_gat': jax.random.normal(ks[1], (D, HEADS * NUM_EXPERTS), jnp.float32) * s, 'att_src': jax.random.normal(ks[2], (HEADS, NUM_EXPERTS), jnp.float32) * s, 'att_dst': jax.random.normal(ks[3], (HEADS, NUM_EXPERTS), jnp.float32) * s, 'b_gat': jnp.zeros((HEADS * NUM_EXPERTS,), jnp.float32), 'ln_gamma': jnp.ones((HEADS * NUM_EXPERTS,), jnp.float32), 'ln_beta': jnp.zeros((HEADS * NUM_EXPERTS,), jnp.float32), 'W1': jax.random.normal(ks[4], (NUM_EXPERTS, D, 2 * D), jnp.float32) * s, 'b1': jnp.zeros((NUM_EXPERTS, 2 * D), jnp.float32), 'W2': jax.random.normal(ks[5], (NUM_EXPERTS, 2 * D, D), jnp.float32) * s, 'b2': jnp.zeros((NUM_EXPERTS, D), jnp.float32), 'edge_index': jax.random.randint(ks[6], (2, N_EDGES), 0, B * N, jnp.int32)}
    _L0_ffn_all = _L0_ffn_setup()
    _L0_ffn_in = {k: v for k, v in _L0_ffn_all.items() if k in ('W_gat', 'att_src', 'att_dst', 'b_gat', 'ln_gamma', 'ln_beta', 'W1', 'b1', 'W2', 'b2', 'edge_index')}
    del _L0_ffn_all
    return {'x': x, 'src': src, 'dst': dst, 'edge_type_8': edge_type_8, 'L0_gnn_conv_weights': _L0_gnn_in['conv_weights'], 'L0_gnn_attn_l': _L0_gnn_in['attn_l'], 'L0_gnn_attn_r': _L0_gnn_in['attn_r'], 'L0_gnn_h_bias': _L0_gnn_in['h_bias'], 'L0_ffn_W_gat': _L0_ffn_in['W_gat'], 'L0_ffn_att_src': _L0_ffn_in['att_src'], 'L0_ffn_att_dst': _L0_ffn_in['att_dst'], 'L0_ffn_b_gat': _L0_ffn_in['b_gat'], 'L0_ffn_ln_gamma': _L0_ffn_in['ln_gamma'], 'L0_ffn_ln_beta': _L0_ffn_in['ln_beta'], 'L0_ffn_W1': _L0_ffn_in['W1'], 'L0_ffn_b1': _L0_ffn_in['b1'], 'L0_ffn_W2': _L0_ffn_in['W2'], 'L0_ffn_b2': _L0_ffn_in['b2'], 'L0_ffn_edge_index': _L0_ffn_in['edge_index']}

def reference(x, src, dst, edge_type_8, L0_gnn_conv_weights, L0_gnn_attn_l, L0_gnn_attn_r, L0_gnn_h_bias, L0_ffn_W_gat, L0_ffn_att_src, L0_ffn_att_dst, L0_ffn_b_gat, L0_ffn_ln_gamma, L0_ffn_ln_beta, L0_ffn_W1, L0_ffn_b1, L0_ffn_W2, L0_ffn_b2, L0_ffn_edge_index):
    import jax
    import jax.numpy as jnp

    def _L0_gnn_ref(inputs, conv_weights, attn_l, attn_r, h_bias, edge_src, edge_dst, edge_type):
        import jax, jax.numpy as jnp
        import numpy as np
        N_NODES = 3750
        N_EDGES = 60000
        IN_FEAT = 256
        OUT_FEAT = 256
        N_RELS = 8
        N_HEADS = 4
        HEAD_DIM = OUT_FEAT // N_HEADS
        LEAKY_SLOPE = 0.2
        feat_all = jnp.einsum('ni,rhid->rnhd', inputs, conv_weights)
        feat_src_e = feat_all[edge_type, edge_src]
        feat_dst_e = feat_all[edge_type, edge_dst]
        el = jnp.sum(feat_src_e * attn_l[edge_type], axis=-1)
        er = jnp.sum(feat_dst_e * attn_r[edge_type], axis=-1)
        e = jax.nn.leaky_relu(el + er, negative_slope=LEAKY_SLOPE)
        m = jax.ops.segment_max(e, edge_dst, num_segments=N_NODES)
        ex = jnp.exp(e - m[edge_dst])
        denom = jax.ops.segment_sum(ex, edge_dst, num_segments=N_NODES)
        alpha = ex / denom[edge_dst]
        h = jax.ops.segment_sum(alpha[..., None] * feat_src_e, edge_dst, num_segments=N_NODES)
        h = h.reshape(N_NODES, OUT_FEAT) + h_bias
        return h

    def _L0_ffn_ref(x, W_gat, att_src, att_dst, b_gat, ln_gamma, ln_beta, W1, b1, W2, b2, edge_index):
        import jax, jax.numpy as jnp
        import numpy as np
        B, N, D = (16, 512, 256)
        NUM_EXPERTS, TOP_K, HEADS = (4, 2, 4)
        N_EDGES = 131072
        LN_EPS = 1e-05

        def _layernorm(x, g, b):
            mu = x.mean(-1, keepdims=True)
            var = ((x - mu) ** 2).mean(-1, keepdims=True)
            return (x - mu) * jax.lax.rsqrt(var + LN_EPS) * g + b

        def _forward(x, edge_index, W_gat, att_src, att_dst, b_gat, ln_gamma, ln_beta, W1, b1, W2, b2):
            Bc, Nc, Dc = x.shape
            M = Bc * Nc
            x_flat = x.reshape(M, Dc)
            h = (x_flat @ W_gat).reshape(M, HEADS, NUM_EXPERTS)
            loops = jnp.arange(M, dtype=edge_index.dtype)
            src = jnp.concatenate([edge_index[0], loops])
            dst = jnp.concatenate([edge_index[1], loops])
            a_src = (h * att_src).sum(-1)
            a_dst = (h * att_dst).sum(-1)
            e = jax.nn.leaky_relu(a_src[src] + a_dst[dst], negative_slope=0.2)
            e_max = jax.ops.segment_max(e, dst, num_segments=M)
            ee = jnp.exp(e - e_max[dst])
            denom = jax.ops.segment_sum(ee, dst, num_segments=M)
            alpha = ee / (denom[dst] + 1e-16)
            msg = h[src] * alpha[:, :, None]
            agg = jax.ops.segment_sum(msg, dst, num_segments=M).reshape(M, HEADS * NUM_EXPERTS) + b_gat
            scores = _layernorm(agg, ln_gamma, ln_beta).reshape(M, HEADS, NUM_EXPERTS).mean(1)
            scores = scores.reshape(Bc, Nc, NUM_EXPERTS)
            topk_s, topk_i = jax.lax.top_k(scores, TOP_K)
            w = jax.nn.softmax(topk_s, axis=-1)
            out = jnp.zeros_like(x)
            for ei in range(NUM_EXPERTS):
                g = jnp.where(topk_i == ei, w, 0.0).sum(-1)
                hh = jax.nn.gelu(x @ W1[ei] + b1[ei], approximate=False)
                out = out + g[..., None] * (hh @ W2[ei] + b2[ei])
            return out
        return _forward(x, edge_index, W_gat, att_src, att_dst, b_gat, ln_gamma, ln_beta, W1, b1, W2, b2)
    x = x + _L0_gnn_ref(_layernorm(x, axis=-1), L0_gnn_conv_weights, L0_gnn_attn_l, L0_gnn_attn_r, L0_gnn_h_bias, src, dst, edge_type_8)
    x = x + _L0_ffn_ref(_layernorm(x, axis=-1)[None], L0_ffn_W_gat, L0_ffn_att_src, L0_ffn_att_dst, L0_ffn_b_gat, L0_ffn_ln_gamma, L0_ffn_ln_beta, L0_ffn_W1, L0_ffn_b1, L0_ffn_W2, L0_ffn_b2, L0_ffn_edge_index)[0]
    return x

_drawn_inputs = setup_inputs


def setup_inputs(seed=0):
    import zlib

    import numpy as np

    out = dict(_drawn_inputs(seed))
    spreads = {'L0_ffn_b_gat': (0.0, 0.1),
     'L0_ffn_ln_gamma': (1.0, 0.2),
     'L0_ffn_ln_beta': (0.0, 0.1),
     'L0_ffn_b1': (0.0, 0.1),
     'L0_ffn_b2': (0.0, 0.1)}
    factors = {}
    for name, (base, spread) in spreads.items():
        noise = np.random.default_rng([zlib.crc32(name.encode()), seed]).standard_normal(out[name].shape)
        drawn = base * np.exp(spread * noise) if base else spread * noise
        out[name] = jnp.asarray(drawn.astype(out[name].dtype))
    for name, factor in factors.items():
        out[name] = (out[name] * factor).astype(out[name].dtype)
    return out
```

```python
from contextlib import ExitStack, contextmanager

import concourse.bass as bass
from concourse import mybir

F32, BF16, I32, U16 = mybir.dt.float32, mybir.dt.bfloat16, mybir.dt.int32, mybir.dt.uint16
ALU = mybir.AluOpType
ACT = mybir.ActivationFunctionType
AX = mybir.AxisListType.X

P = 128
N = 3750
NB = -(-N // P)
NBP = 32
D = 256
KC = D // P
H = 4
R = 8
HD = D // H
E1 = 123750
E2 = 131072
X = 4
FF = 2 * D
U = 8
G2 = 2 * U
EPS = 1e-5
SLOPE = 0.2
BIG = 1.0e30
FREE_LO, FREE_HI = 255, 31


class Graph:

    def __init__(self, name, chunks, types, row, feats):
        self.name = name
        self.raw = -(-chunks // G2) * G2
        self.raw_tiles = -(-self.raw // P)
        self.slots = -(-(self.raw + NB) // G2) * G2
        self.tiles = -(-self.slots // P)
        self.lane = self.tiles * P
        self.rels = types
        self.er = types * H
        self.row = row
        self.feats = feats
        self.out = feats + H


REL = Graph("rel", -(-E1 // P), R, H, D)
ROUTE = Graph("route", E2 // P + NB, 1, X * H + H, X * H)


def row_bcast(ap, parts=P):
    return bass.AP(ap.tensor, ap.offset, [[0, parts]] + [list(x) for x in ap.ap])


class Chain:

    def __init__(self, eng, sem, step=None, per_step=0, before=0):
        self.eng, self.sem, self.step, self.per_step, self.before, self.n = eng, sem, step, per_step, before, 0

    def link(self, ins):
        ins.then_inc(self.sem, 1)
        self.n += 1
        at = self.before + self.n
        self.eng.wait_ge(self.sem, at if self.step is None else self.step * self.per_step + at)

    def end(self):
        assert self.step is None or self.n == self.per_step, (self.n, self.per_step)


@contextmanager
def stage(nc, name=""):
    sems = []
    with ExitStack() as ctx:
        def sb(label, shape, dt=F32):
            return ctx.enter_context(nc.sbuf_tensor(name + label, shape, dt))

        def ps(label, shape, dt=F32):
            return ctx.enter_context(nc.psum_tensor(name + label, shape, dt))

        def sem(label):
            sems.append(nc.alloc_semaphore(name + label))
            return sems[-1]

        yield sb, ps, sem
        if sems:
            nc.clear_and_free_semaphores(sems)
            nc.all_engine_barrier()


def each_step(eng, steps, body):
    body(0)
    with eng.Fori(1, steps) as i:
        body(i)


def wait_before_reuse(eng, sem, step, per_step, at=0):
    if not isinstance(step, int):
        eng.wait_ge(sem, step * per_step + at)


def bc(ap, *dims):
    return bass.AP(ap.tensor, ap.offset, [list(ap.ap[0])] + [list(x) for x in dims])


def turns(tiles, arrays):
    return [(k, t, min(4, tiles - t)) for k in range(arrays) for t in range(0, tiles, 4)]


def constants(nc, C):
    with stage(nc) as (_, _, sem):
        filled = sem("const_filled")
        made = sem("const_made")
        with nc.Block() as block:
            @block.gpsimd
            def _(pool):
                nc.gpsimd.memset(C.ident[:, :], 0.0).then_inc(filled, 1)
                nc.gpsimd.memset(C.before[:, :], 1.0).then_inc(filled, 1)
                nc.gpsimd.memset(C.after[:, :], 1.0).then_inc(filled, 1)
                nc.gpsimd.memset(C.ones[:, :], 1.0).then_inc(filled, 1)
                nc.gpsimd.memset(C.zero_bf[:, :], 0.0).then_inc(filled, 1)
                pool.wait_ge(filled, 5)
                nc.gpsimd.affine_select(out=C.ident[:, :], in_=C.ident[:, :], compare_op=ALU.not_equal, fill=1.0,
                                        base=0, pattern=[[-1, P]], channel_multiplier=1).then_inc(made, 1)
                nc.gpsimd.affine_select(out=C.before[:, :], in_=C.before[:, :], compare_op=ALU.is_gt, fill=0.0,
                                        base=0, pattern=[[-1, P]], channel_multiplier=1).then_inc(made, 1)
                nc.gpsimd.affine_select(out=C.after[:, :], in_=C.after[:, :], compare_op=ALU.is_gt, fill=0.0,
                                        base=0, pattern=[[1, P]], channel_multiplier=-1).then_inc(made, 1)
                nc.gpsimd.iota(C.count_i[:, :], [[1, P]], base=0, channel_multiplier=0).then_inc(made, 1)
                nc.gpsimd.iota(C.part_i[:, :], [[0, 1]], base=0, channel_multiplier=1).then_inc(made, 1)
                pool.wait_ge(made, 5)

            @block.vector
            def _(dve):
                dve.wait_ge(made, 5)
                nc.vector.tensor_copy(C.count[:, :], C.count_i[:, :]).then_inc(filled, 1)
                nc.vector.tensor_copy(C.part[:, :], C.part_i[:, :]).then_inc(filled, 1)


def prepare_edges(nc, C, g, S, src_in, dst_in, type_in):
    T = g.raw_tiles
    W = T * P
    with stage(nc, g.name + "_") as (sb, ps, sem):
        src = sb("pe_src", [P, W], I32)
        dst = sb("pe_dst", [P, W], I32)
        typ = sb("pe_typ", [P, W], I32)
        lo_i = sb("pe_lo_i", [P, W], I32)
        hi_i = sb("pe_hi_i", [P, W], I32)
        a_f = sb("pe_a", [P, W])
        lo_f = sb("pe_lo", [P, W])
        hi_f = sb("pe_hi", [P, W])
        rows = sb("pe_rows", [P, T, 2, P], U16)
        a_ci = sb("pe_a_ci", [P, W], I32)
        k_ci = sb("pe_k_ci", [P, W], I32)
        turned = [ps(f"pe_turned{i}", [P, 512]) for i in range(6)]
        filled = sem("pe_filled")
        loaded = sem("pe_loaded")
        split = sem("pe_split")
        rows_out = sem("pe_rows_out")
        turn_done = sem("pe_turn_done")
        turn_used = sem("pe_turn_used")
        chain = sem("pe_chain")
        n_loads = []

        with nc.Block() as block:
            @block.gpsimd
            def _(pool):
                nc.gpsimd.memset(typ[:, :], 0).then_inc(filled, 1)
                if g is REL:
                    nc.gpsimd.memset(src[:, :], 0).then_inc(filled, 1)
                    nc.gpsimd.memset(dst[:, :], N).then_inc(filled, 1)
                else:
                    nc.gpsimd.iota(src[:, W - P:W], [[1, P]], base=0, channel_multiplier=P).then_inc(filled, 1)
                    nc.gpsimd.iota(dst[:, W - P:W], [[1, P]], base=0, channel_multiplier=P).then_inc(filled, 1)

            @block.sync
            def _(sp):
                sp.wait_ge(filled, 3)
                pairs = [(src, src_in), (dst, dst_in)] + ([(typ, type_in)] if g is REL else [])
                for sbuf, dram in pairs:
                    edges = E1 if g is REL else E2
                    tiles, rest = divmod(edges, P * P)
                    sp.dma_start(sbuf[:, 0:tiles * P].rearrange("p (t e) -> p t e", e=P),
                                 dram[0:tiles * P * P].rearrange("(t p e) -> p t e", p=P, e=P)).then_inc(loaded, 16)
                    n_loads.append(1)
                    full, last = divmod(rest, P)
                    if full:
                        sp.dma_start(sbuf[0:full, tiles * P:tiles * P + P],
                                     dram[tiles * P * P:tiles * P * P + full * P].rearrange(
                                         "(p e) -> p e", e=P)).then_inc(loaded, 16)
                        n_loads.append(1)
                    if last:
                        at = edges - last
                        sp.dma_start(sbuf[full:full + 1, tiles * P:tiles * P + last],
                                     dram[at:edges].rearrange("(p e) -> p e", p=1)).then_inc(loaded, 16)
                        n_loads.append(1)
                sp.wait_ge(split, 1)
                sp.dma_start(S.key_rows.rearrange("(t p) k e -> p t k e", p=P), rows[:, :, :, :]).then_inc(rows_out, 16)
                sp.wait_ge(rows_out, 16)

            @block.vector
            def _(dve):
                ch = Chain(dve, chain)
                dve.wait_ge(loaded, 16 * len(n_loads))
                dve.wait_ge(filled, 3)
                nc.vector.tensor_scalar(src[:, :], src[:, :], float(N - 1), None, ALU.min)
                ch.link(nc.vector.tensor_scalar(dst[:, :], dst[:, :], float(N), None, ALU.min))
                nc.vector.tensor_scalar(lo_i[:, :], dst[:, :], P - 1, None, ALU.bitwise_and)
                nc.vector.tensor_scalar(hi_i[:, :], dst[:, :], 7, None, ALU.logical_shift_right)
                ch.link(nc.vector.scalar_tensor_tensor(a_f[:, :], src[:, :], float(g.rels), typ[:, :], ALU.mult,
                                                       ALU.add))
                nc.vector.tensor_copy(lo_f[:, :], lo_i[:, :])
                ch.link(nc.vector.tensor_copy(hi_f[:, :], hi_i[:, :]))
                lo3 = lo_f[:, :].rearrange("p (t e) -> p t e", e=P)
                hi3 = hi_f[:, :].rearrange("p (t e) -> p t e", e=P)
                nc.vector.scalar_tensor_tensor(rows[:, :, 0, :], hi3, 256.0, lo3, ALU.mult, ALU.add)
                ch.link(nc.vector.tensor_copy(rows[:, :, 1, :], lo3))
                nc.vector.engine_nop().then_inc(split, 1)
                for q, (k, t0, n) in enumerate(turns(T, 3)):
                    dve.wait_ge(turn_done, q + 1)
                    out = (S.lo, S.hi, a_ci)[k][:, t0 * P:(t0 + n) * P]
                    nc.vector.tensor_copy(out, turned[q % 6][:, 0:n * P]).then_inc(turn_used, 1)
                dve.wait_ge(turn_used, len(turns(T, 3)))
                ch.link(nc.vector.scalar_tensor_tensor(S.key[:, :], S.hi[:, :], 256.0, S.lo[:, :], ALU.mult, ALU.add))
                ch.link(nc.vector.tensor_copy(k_ci[:, :], S.key[:, :]))
                ch.link(nc.vector.tensor_scalar(k_ci[:, :], k_ci[:, :], 15, None, ALU.logical_shift_left))
                ch.link(nc.vector.tensor_tensor(S.packed[:, :], k_ci[:, :], a_ci[:, :], ALU.bitwise_or))

            @block.tensor
            def _(pe):
                pe.wait_ge(split, 1)
                for q, (k, t0, n) in enumerate(turns(T, 3)):
                    if q >= 6:
                        pe.wait_ge(turn_used, q - 5)
                    for i in range(n):
                        last = nc.tensor.transpose(turned[q % 6][:, i * P:(i + 1) * P],
                                                   (lo_f, hi_f, a_f)[k][:, (t0 + i) * P:(t0 + i + 1) * P],
                                                   C.ident[:, :])
                    last.then_inc(turn_done, 1)


def onehot(nc, C, out, values, width):
    return nc.vector.tensor_tensor(out, bc(values, [1, U], [0, width]), bc(C.count[:, 0:1], [0, U], [1, width]),
                                   ALU.is_equal)


def count_edges(nc, C, g, S):
    steps = g.raw // G2
    with stage(nc, g.name + "_") as (sb, ps, sem):
        low = [sb(f"ce_low{h}", [P, U, P], BF16) for h in range(2)]
        blk = [sb(f"ce_blk{h}", [P, U, NBP], BF16) for h in range(2)]
        size = sb("ce_size", [P, NBP])
        size_i = sb("ce_size_i", [P, NBP], I32)
        ends = sb("ce_ends", [P, NBP])
        zeros = sb("ce_zeros", [P, NBP])
        starts = sb("ce_starts", [P, NBP])
        chunk_i = sb("ce_chunk_i", [P, g.tiles], I32)
        chunk_f = sb("ce_chunk_f", [P, g.tiles])
        past = sb("ce_past", [P, g.tiles, NBP])
        blocks = sb("ce_blocks", [P, g.tiles])
        blocks_i = sb("ce_blocks_i", [P, g.tiles], I32)
        free = sb("ce_free", [P, g.tiles * P], I32)
        counts_ps = ps("ce_counts", [P, 512])
        sums_ps = ps("ce_sums", [P, 512])
        one = sem("ce_onehot_ready")
        used = [sem(f"ce_onehot_used{h}") for h in range(2)]
        cleared = sem("ce_cleared")
        counted = sem("ce_counted")
        copied = sem("ce_copied")
        summed = sem("ce_summed")
        chain = sem("ce_chain")
        stored = sem("ce_stored")
        numbered = sem("ce_numbered")
        numbers_ready = sem("ce_numbers_ready")
        with nc.Block() as block:
            @block.gpsimd
            def _(pool):
                nc.gpsimd.memset(free[:, :], (FREE_LO + 256 * FREE_HI) << 15).then_inc(numbered, 1)
                nc.gpsimd.iota(chunk_i[:, :], [[P * P, g.tiles]], base=0, channel_multiplier=P).then_inc(numbered, 1)

            @block.sync
            def _(sp):
                sp.wait_ge(numbered, 2)
                sp.dma_start(S.sorted.rearrange("(p l) o -> p (l o)", p=P), free[:, :]).then_inc(stored, 16)
                sp.wait_ge(numbers_ready, 1)
                sp.dma_start(S.block_dram.rearrange("(t p) -> p t", p=P), blocks_i[:, :],
                             allow_slow_non_contiguous=True).then_inc(stored, 16)
                sp.wait_ge(stored, 32)
                sp.dma_start(S.block_row[0:1, :], S.block_dram.rearrange("(o c) -> o c", o=1)).then_inc(stored, 16)
                sp.wait_ge(stored, 48)

            @block.vector
            def _(dve):
                def step(i):
                    for h in range(2):
                        wait_before_reuse(dve, used[h], i, 1)
                        at = i * G2 + h * U
                        onehot(nc, C, low[h][:, :, :], S.lo[:, bass.ds(at, 1)], P)
                        onehot(nc, C, blk[h][:, :, :], S.hi[:, bass.ds(at, 1)], NBP).then_inc(one, 1)

                each_step(dve, steps, step)
                ch = Chain(dve, chain)
                dve.wait_ge(counted, 1)
                ch.link(nc.vector.tensor_copy(S.counts[:, :], counts_ps[:, 0:NBP]))
                dve.wait_ge(summed, 1)
                ch.link(nc.vector.tensor_scalar(size_i[:, :], sums_ps[:, NBP:2 * NBP], float(P - 1), None, ALU.add))
                ch.link(nc.vector.tensor_scalar(size_i[:, :], size_i[:, :], 7, 7, ALU.logical_shift_right,
                                                ALU.logical_shift_left))
                nc.vector.memset(zeros[:, :], 0.0)
                ch.link(nc.vector.tensor_copy(size[:, :], size_i[:, :]))
                ch.link(nc.vector.tensor_tensor_scan(ends[:, :], size[:, :], zeros[:, :], 0.0, ALU.add, ALU.add))
                ch.link(nc.vector.tensor_tensor(starts[:, :], ends[:, :], size[:, :], ALU.subtract))
                ch.link(nc.vector.tensor_tensor(S.start[:, :], sums_ps[:, 0:NBP], starts[:, :], ALU.add))
                ch.link(nc.vector.scalar_tensor_tensor(size[:, :], S.start[:, :], -1.0, S.counts[:, :], ALU.add,
                                                       ALU.add))
                ch.link(nc.vector.tensor_scalar(S.last[:, :], size[:, :], 0.0, None, ALU.max))
                dve.wait_ge(numbered, 2)
                ch.link(nc.vector.tensor_copy(chunk_f[:, :], chunk_i[:, :]))
                ch.link(nc.vector.tensor_tensor(past[:, :, :], bc(ends[:, 0:1], [0, g.tiles], [1, NBP]),
                                                bc(chunk_f[:, 0:1], [1, g.tiles], [0, NBP]), ALU.is_le))
                ch.link(nc.vector.tensor_reduce(blocks[:, :], past[:, :, 0:NB], AX, ALU.add))
                nc.vector.tensor_scalar(blocks_i[:, :], blocks[:, :], float(NB - 1), None,
                                        ALU.min).then_inc(numbers_ready, 1)

            @block.tensor
            def _(pe):
                nc.tensor.matmul(counts_ps[:, 0:NBP], C.zero_bf[:, :], C.zero_bf[:, 0:NBP], start=True, stop=False)

                def step(i):
                    for h in range(2):
                        pe.wait_ge(one, i * 2 + h + 1)
                        for u in range(U):
                            last = nc.tensor.matmul(counts_ps[:, 0:NBP], low[h][:, u, :], blk[h][:, u, :],
                                                    start=False, stop=False)
                        last.then_inc(used[h], 1)

                each_step(pe, steps, step)
                nc.tensor.matmul(counts_ps[:, 0:NBP], C.zero_bf[:, :], C.zero_bf[:, 0:NBP], start=False,
                                 stop=True).then_inc(counted, 1)
                pe.wait_ge(chain, 1)
                nc.tensor.matmul(sums_ps[:, 0:NBP], C.after[:, :], S.counts[:, :], start=True, stop=True)
                nc.tensor.matmul(sums_ps[:, NBP:2 * NBP], C.ones[:, :], S.counts[:, :], start=True,
                                 stop=True).then_inc(summed, 1)


def scatter_edges(nc, C, g, S):
    steps = g.raw // G2
    with stage(nc, g.name + "_") as (sb, ps, sem):
        low = [sb(f"se_low{h}", [P, U, P], BF16) for h in range(2)]
        blk = [sb(f"se_blk{h}", [P, U, NBP], BF16) for h in range(2)]
        low_t = [sb(f"se_low_t{h}", [P, U, P]) for h in range(2)]
        rows = [sb(f"se_rows{h}", [P, U, 2, P], U16) for h in range(2)]
        table = [sb(f"se_table{h}", [P, U + 1, NBP]) for h in range(2)]
        match = [sb(f"se_match{h}", [P, U, P], BF16) for h in range(2)]
        rank = [sb(f"se_rank{h}", [P, U]) for h in range(2)]
        pick = [sb(f"se_pick{h}", [P, U, NBP]) for h in range(2)]
        base = [sb(f"se_base{h}", [P, U]) for h in range(2)]
        slot = [sb(f"se_slot{h}", [P, U], I32) for h in range(2)]
        load = [sb(f"se_load{h}", [P, U], I32) for h in range(2)]
        grow = [ps(f"se_grow{h}", [P, 512]) for h in range(2)]
        look = [ps(f"se_look{h}", [P, 512]) for h in range(2)]
        rows_in = [sem(f"se_rows_in{h}") for h in range(2)]
        rows_used = [sem(f"se_rows_used{h}") for h in range(2)]
        one = sem("se_onehot_ready")
        grown = sem("se_grown")
        tables = sem("se_table_ready")
        looked = sem("se_looked")
        picked = sem("se_picked")
        slots = sem("se_slots_ready")
        chain = sem("se_chain")
        begun = sem("se_scatter_begun")
        sent = [sem(f"se_sent{h}") for h in range(2)]
        with nc.Block() as block:
            @block.sync
            def _(sp):
                def step(i):
                    for h in range(2):
                        wait_before_reuse(sp, rows_used[h], i, 1)
                        chunk = S.key_rows[bass.ds(i * G2 + h * U, U), :, :]
                        sp.dma_start(rows[h][:, :, :, :].rearrange("p u k e -> p (u k e)"),
                                     row_bcast(chunk.rearrange("u k e -> (u k e)"))).then_inc(rows_in[h], 16)

                each_step(sp, steps, step)

            @block.vector
            def _(dve):
                Chain(dve, chain).link(nc.vector.tensor_copy(table[0][:, 0, :], S.start[:, :]))

                def step(i):
                    ch = Chain(dve, chain, i, 4, 1)
                    for h in range(2):
                        at = i * G2 + h * U
                        onehot(nc, C, low[h][:, :, :], S.lo[:, bass.ds(at, 1)], P)
                        onehot(nc, C, blk[h][:, :, :], S.hi[:, bass.ds(at, 1)], NBP)
                        dve.wait_ge(rows_in[h], i * 16 + 16)
                        nc.vector.tensor_scalar(low_t[h][:, :, :], rows[h][:, :, 1, :], C.part[:, 0:1], None,
                                                ALU.is_equal).then_inc(one, 1)
                        for u in range(U):
                            ins = nc.vector.scalar_tensor_tensor(
                                match[h][:, u, :], rows[h][:, u, 0, :], S.key[:, bass.ds(at + u, 1)],
                                C.before[:, :], ALU.is_equal, ALU.mult, accum_out=rank[h][:, u:u + 1])
                        ins.then_inc(rows_used[h], 1)
                        dve.wait_ge(grown, i * 2 + h + 1)
                        ch.link(nc.vector.tensor_tensor(
                            table[h][:, 1:, :], grow[h][:, 0:U * NBP].rearrange("p (u b) -> p u b", b=NBP),
                            bc(table[h][:, 0, 0:1], [0, U], [1, NBP]), ALU.add))
                        nc.vector.tensor_copy(table[1 - h][:, 0, :], table[h][:, U, :]).then_inc(tables, 1)
                        dve.wait_ge(looked, i * 2 + h + 1)
                        nc.vector.tensor_tensor(
                            pick[h][:, :, :], look[h][:, 0:U * NBP].rearrange("p (u b) -> p u b", b=NBP),
                            blk[h][:, :, :], ALU.mult).then_inc(picked, 1)
                        dve.wait_ge(picked, i * 2 + h + 1)
                        ch.link(nc.vector.tensor_reduce(base[h][:, :], pick[h][:, :, :], AX, ALU.add))
                        wait_before_reuse(dve, sent[h], i, 16 * U)
                        nc.vector.tensor_tensor(slot[h][:, :], base[h][:, :], rank[h][:, :], ALU.add)
                        nc.vector.tensor_copy(load[h][:, :], S.packed[:, bass.ds(at, U)]).then_inc(slots, 1)
                    ch.end()

                each_step(dve, steps, step)

            @block.tensor
            def _(pe):
                def step(i):
                    for h in range(2):
                        pe.wait_ge(one, i * 2 + h + 1)
                        for u in range(U):
                            last = nc.tensor.matmul(grow[h][:, u * NBP:U * NBP], low[h][:, u, :],
                                                    bc(blk[h][:, u, 0:1], [0, U - u], [1, NBP]),
                                                    start=(u == 0), stop=(u == U - 1))
                        last.then_inc(grown, 1)
                        pe.wait_ge(tables, i * 2 + h + 1)
                        for u in range(U):
                            last = nc.tensor.matmul(look[h][:, u * NBP:(u + 1) * NBP], low_t[h][:, u, :],
                                                    table[h][:, u, :], start=True, stop=True)
                        last.then_inc(looked, 1)

                each_step(pe, steps, step)

            @block.gpsimd
            def _(pool):
                def step(i):
                    for h in range(2):
                        pool.wait_ge(slots, i * 2 + h + 1)
                        pool.sem_inc(begun, 1)
                        for u in range(U):
                            nc.gpsimd.indirect_dma_start(
                                S.sorted, bass.IndirectOffsetOnAxis(ap=slot[h][:, u:u + 1], axis=0),
                                load[h][:, u:u + 1], None).then_inc(sent[h], 16)

                each_step(pool, steps, step)
                for h in range(2):
                    pool.wait_ge(sent[h], steps * U * 16)


def read_slots(nc, C, g, S):
    T = g.tiles
    W = T * P
    with stage(nc, g.name + "_") as (sb, ps, sem):
        packed = sb("rs_packed", [P, W], I32)
        row_i = sb("rs_row_i", [P, W], I32)
        key_i = sb("rs_key_i", [P, W], I32)
        typ_i = sb("rs_typ_i", [P, W], I32)
        row_f = sb("rs_row", [P, W])
        low_f = sb("rs_low", [P, W])
        typ_f = sb("rs_typ", [P, W])
        low_u = sb("rs_low_u", [P, T, P], U16)
        turned = [ps(f"rs_turned{i}", [P, 512]) for i in range(6)]
        loaded = sem("rs_loaded")
        chain = sem("rs_chain")
        split = sem("rs_split")
        stored = sem("rs_stored")
        turn_done = sem("rs_turn_done")
        turn_used = sem("rs_turn_used")
        groups = turns(T, 3 if g is REL else 2)
        with nc.Block() as block:
            @block.sync
            def _(sp):
                sp.dma_start(packed[:, :].rearrange("p (t e) -> p t e", e=P),
                             S.sorted.rearrange("(t p e) o -> p t (e o)", p=P, e=P)).then_inc(loaded, 16)
                sp.wait_ge(split, 1)
                sp.dma_start(S.low_rows.rearrange("(t p) e -> p t e", p=P), low_u[:, :, :]).then_inc(stored, 16)
                sp.wait_ge(stored, 16)

            @block.vector
            def _(dve):
                ch = Chain(dve, chain)
                dve.wait_ge(loaded, 16)
                nc.vector.tensor_scalar(row_i[:, :], packed[:, :], 0x7fff, None, ALU.bitwise_and)
                ch.link(nc.vector.tensor_scalar(key_i[:, :], packed[:, :], 15, 255, ALU.logical_shift_right,
                                                ALU.bitwise_and))
                nc.vector.tensor_scalar(typ_i[:, :], row_i[:, :], g.rels - 1, None, ALU.bitwise_and)
                nc.vector.tensor_copy(row_f[:, :], row_i[:, :])
                nc.vector.tensor_copy(low_u[:, :, :], key_i[:, :].rearrange("p (t e) -> p t e", e=P))
                ch.link(nc.vector.tensor_copy(low_f[:, :], key_i[:, :]))
                nc.vector.tensor_copy(typ_f[:, :], typ_i[:, :]).then_inc(split, 1)
                for q, (k, t0, n) in enumerate(groups):
                    dve.wait_ge(turn_done, q + 1)
                    out = (S.slot_row, S.slot_low, S.slot_type)[k][:, t0 * P:(t0 + n) * P]
                    nc.vector.tensor_copy(out, turned[q % 6][:, 0:n * P]).then_inc(turn_used, 1)

            @block.tensor
            def _(pe):
                pe.wait_ge(split, 1)
                for q, (k, t0, n) in enumerate(groups):
                    if q >= 6:
                        pe.wait_ge(turn_used, q - 5)
                    for i in range(n):
                        last = nc.tensor.transpose(turned[q % 6][:, i * P:(i + 1) * P],
                                                   (row_f, low_f, typ_f)[k][:, (t0 + i) * P:(t0 + i + 1) * P],
                                                   C.ident[:, :])
                    last.then_inc(turn_done, 1)


def score_edges(nc, C, g, S):
    steps = g.slots // G2
    with stage(nc, g.name + "_") as (sb, ps, sem):
        index = [sb(f"sc_index{h}", [P, U], I32) for h in range(2)]
        got = [sb(f"sc_got{h}", [P, U, g.row]) for h in range(2)]
        rows = [sb(f"sc_rows{h}", [P, U, P], U16) for h in range(2)]
        low_t = [sb(f"sc_low_t{h}", [P, U, P]) for h in range(2)]
        type1 = [sb(f"sc_type{h}", [P, U, R]) for h in range(2)]
        pick = [sb(f"sc_pick{h}", [P, U, g.rels, H]) for h in range(2)]
        dest = [sb(f"sc_dest{h}", [P, U, H]) for h in range(2)]
        both = [sb(f"sc_sum{h}", [P, U, H]) for h in range(2)]
        score = [sb(f"sc_score{h}", [P, U * H]) for h in range(2)]
        turned = [sb(f"sc_turned{h}", [U * H, P]) for h in range(2)]
        look = [ps(f"sc_look{h}", [P, 512]) for h in range(2)]
        turn = [ps(f"sc_turn{h}", [P, 512]) for h in range(2)]
        index_ready = sem("sc_index_ready")
        begun = sem("sc_begun")
        gathered = [sem(f"sc_gathered{h}") for h in range(2)]
        got_used = [sem(f"sc_got_used{h}") for h in range(2)]
        rows_in = [sem(f"sc_rows_in{h}") for h in range(2)]
        low_ready = sem("sc_low_ready")
        looked = sem("sc_looked")
        chain = sem("sc_chain")
        scored = sem("sc_scored")
        turn_done = sem("sc_turn_done")
        kept = sem("sc_kept")
        turn_copied = sem("sc_turn_copied")
        stored = [sem(f"sc_stored{h}") for h in range(2)]
        with nc.Block() as block:
            @block.sync
            def _(sp):
                def step(i):
                    for h in range(2):
                        wait_before_reuse(sp, low_ready, i, 2, h - 1)
                        sp.dma_start(rows[h][:, :, :].rearrange("p u e -> p (u e)"), row_bcast(
                            S.low_rows[bass.ds(i * G2 + h * U, U), :].rearrange("u e -> (u e)"))).then_inc(
                                rows_in[h], 16)

                each_step(sp, steps, step)

            @block.gpsimd
            def _(pool):
                def step(i):
                    for h in range(2):
                        wait_before_reuse(pool, got_used[h], i, 1)
                        pool.sem_inc(begun, 1)
                        nc.gpsimd.tensor_copy(index[h][:, :],
                                              S.slot_row[:, bass.ds(i * G2 + h * U, U)]).then_inc(index_ready, 1)
                        pool.wait_ge(index_ready, i * 2 + h + 1)
                        pool.sem_inc(begun, 1)
                        for u in range(U):
                            nc.gpsimd.indirect_dma_start(
                                got[h][:, u, :], None, S.score_table,
                                bass.IndirectOffsetOnAxis(ap=index[h][:, u:u + 1], axis=0)).then_inc(gathered[h], 16)

                each_step(pool, steps, step)

            @block.vector
            def _(dve):
                def step(i):
                    ch = Chain(dve, chain, i, 4)
                    for h in range(2):
                        at = i * G2 + h * U
                        if g is REL:
                            onehot(nc, C, type1[h][:, :, :], S.slot_type[:, bass.ds(at, 1)], R)
                        dve.wait_ge(rows_in[h], i * 16 + 16)
                        nc.vector.tensor_scalar(low_t[h][:, :, :], rows[h][:, :, :], C.part[:, 0:1], None,
                                                ALU.is_equal).then_inc(low_ready, 1)
                        dve.wait_ge(looked, i * 2 + h + 1)
                        found = look[h][:, 0:U * g.er]
                        if g is REL:
                            ch.link(nc.vector.tensor_tensor(
                                pick[h][:, :, :, :], found.rearrange("p (u r h) -> p u r h", r=R, h=H),
                                bc(type1[h][:, 0, 0:1], [R, U], [1, R], [0, H]), ALU.mult))
                            ch.link(nc.vector.tensor_reduce(
                                dest[h][:, :, :], pick[h][:, :, :, :].rearrange("p u r h -> p u h r"), AX, ALU.add))
                            found = dest[h][:, :, :]
                        else:
                            found = found.rearrange("p (u h) -> p u h", h=H)
                        dve.wait_ge(gathered[h], (i * 16 + 16) * U)
                        if g is ROUTE:
                            nc.vector.tensor_copy(S.kept[:, bass.ds(at, U), :], got[h][:, :, 0:g.feats])
                        nc.vector.tensor_tensor(both[h][:, :, :], found, got[h][:, :, g.row - H:g.row],
                                                ALU.add).then_inc(got_used[h], 1)
                        dve.wait_ge(got_used[h], i + 1)
                        wait_before_reuse(dve, turn_done, i, 2, h - 1)
                        wait_before_reuse(dve, kept, i, 2, h - 1)
                        nc.vector.scalar_tensor_tensor(
                            score[h][:, :], both[h][:, :, :].rearrange("p u h -> p (u h)"), SLOPE,
                            both[h][:, :, :].rearrange("p u h -> p (u h)"), ALU.mult, ALU.max).then_inc(scored, 1)
                    if g is REL:
                        ch.end()

                each_step(dve, steps, step)

            @block.tensor
            def _(pe):
                def step(i):
                    for h in range(2):
                        at = i * G2 + h * U
                        pe.wait_ge(low_ready, i * 2 + h + 1)
                        for u in range(U):
                            b = pe.value_load(S.block_row[0:1, bass.ds(at + u, 1)], min_val=0, max_val=NB - 1)
                            last = nc.tensor.matmul(look[h][:, u * g.er:(u + 1) * g.er], low_t[h][:, u, :],
                                                    S.dest_table[:, bass.ds(b * g.er, g.er)], start=True, stop=True)
                        last.then_inc(looked, 1)
                        pe.wait_ge(scored, i * 2 + h + 1)
                        wait_before_reuse(pe, turn_copied, i, 2, h - 1)
                        nc.tensor.transpose(turn[h][0:U * H, 0:P], score[h][:, :], C.ident[:, :]).then_inc(turn_done, 1)

                each_step(pe, steps, step)

            @block.scalar
            def _(act):
                def step(i):
                    for h in range(2):
                        at = i * G2 + h * U
                        act.wait_ge(scored, i * 2 + h + 1)
                        nc.scalar.copy(S.score[:, bass.ds(at * H, U * H)], score[h][:, :]).then_inc(kept, 1)
                        act.wait_ge(turn_done, i * 2 + h + 1)
                        wait_before_reuse(act, stored[h], i, 16)
                        nc.scalar.copy(turned[h][:, :], turn[h][0:U * H, 0:P]).then_inc(turn_copied, 1)
                        act.wait_ge(turn_copied, i * 2 + h + 1)
                        act.dma_start(S.score_rows[bass.ds(at, U), :, :].rearrange("u h e -> (u h) e"),
                                      turned[h][:, :]).then_inc(stored[h], 16)

                each_step(act, steps, step)
                for h in range(2):
                    act.wait_ge(stored[h], steps * 16)


def node_maxima(nc, C, g, S):
    T, L = g.tiles, g.lane
    full, part = divmod(g.slots, T)
    with stage(nc, g.name + "_") as (sb, ps, sem):
        packed = sb("nm_packed", [P, L], I32)
        key = sb("nm_key", [P, L])
        fresh = sb("nm_fresh", [P, L])
        score = sb("nm_score", [P, H, L])
        peak = sb("nm_peak", [P, L, H])
        ends = sb("nm_ends", [P, H + 1])
        diag = sb("nm_diag", [P, H + 1, P])
        same = sb("nm_same", [P, P])
        reach = sb("nm_reach", [P, H, P])
        carry = sb("nm_carry", [P, H])
        index = sb("nm_index", [P, NBP], I32)
        across = [ps(f"nm_across{i}", [P, 512]) for i in range(2)]
        cleared = sem("nm_cleared")
        loaded = sem("nm_loaded")
        chain = sem("nm_chain")
        diag_ready = sem("nm_diag_ready")
        spread = sem("nm_spread")
        peaks = sem("nm_peaks_ready")
        stored = sem("nm_stored")
        gathered = sem("nm_gathered")
        with nc.Block() as block:
            @block.gpsimd
            def _(pool):
                nc.gpsimd.memset(score[:, :, :], 0.0).then_inc(cleared, 1)
                pool.wait_ge(stored, 16)
                for b in range(NB):
                    nc.gpsimd.indirect_dma_start(
                        S.peak[:, b * H:(b + 1) * H], None, S.peak_table,
                        bass.IndirectOffsetOnAxis(ap=S.last[:, b:b + 1], axis=0)).then_inc(gathered, 16)
                pool.wait_ge(gathered, NB * 16)

            @block.sync
            def _(sp):
                sp.dma_start(packed[:, :], S.sorted.rearrange("(p l) o -> p (l o)", p=P)).then_inc(loaded, 16)
                sp.wait_ge(cleared, 1)
                for h in range(H):
                    sp.dma_start(score[0:full, h, :].rearrange("p (t e) -> p t e", e=P),
                                 S.score_rows[0:full * T, h, :].rearrange("(p t) e -> p t e", t=T)).then_inc(loaded, 16)
                    if part:
                        sp.dma_start(score[full:full + 1, h, 0:part * P].rearrange("p (t e) -> p t e", e=P),
                                     S.score_rows[full * T:g.slots, h, :].rearrange(
                                         "(p t) e -> p t e", p=1)).then_inc(loaded, 16)
                sp.wait_ge(peaks, 1)
                sp.dma_start(S.peak_table.rearrange("(p l) h -> p (l h)", p=P),
                             peak[:, :, :].rearrange("p l h -> p (l h)")).then_inc(stored, 16)

            @block.vector
            def _(dve):
                ch = Chain(dve, chain)
                dve.wait_ge(loaded, 16 * (1 + H * (2 if part else 1)))
                ch.link(nc.vector.tensor_scalar(packed[:, :], packed[:, :], 15, None, ALU.logical_shift_right))
                ch.link(nc.vector.tensor_copy(key[:, :], packed[:, :]))
                ch.link(nc.vector.tensor_tensor(fresh[:, 1:L], key[:, 1:L], key[:, 0:L - 1], ALU.is_equal))
                ch.link(nc.vector.memset(fresh[:, 0:1], 0.0))
                ch.link(nc.vector.tensor_scalar(fresh[:, :], fresh[:, :], 1.0, BIG, ALU.subtract, ALU.mult))
                for h in range(H):
                    ins = nc.vector.tensor_tensor_scan(peak[:, :, h], fresh[:, :], score[:, h, :], -BIG, ALU.add,
                                                       ALU.max)
                ch.link(ins)
                nc.vector.tensor_copy(ends[:, H:H + 1], key[:, L - 1:L])
                ch.link(nc.vector.tensor_copy(ends[:, 0:H], peak[:, L - 1, :]))
                nc.vector.tensor_tensor(diag[:, :, :], bc(ends[:, 0:1], [1, H + 1], [0, P]),
                                        bc(C.ident[:, 0:1], [0, H + 1], [1, P]), ALU.mult).then_inc(diag_ready, 1)
                dve.wait_ge(spread, 1)
                ch.link(nc.vector.scalar_tensor_tensor(same[:, :], across[1][:, 0:P], key[:, 0:1], C.before[:, :],
                                                       ALU.is_equal, ALU.mult))
                ch.link(nc.vector.tensor_scalar(same[:, :], same[:, :], 1.0, BIG, ALU.subtract, ALU.mult))
                ch.link(nc.vector.tensor_tensor(reach[:, :, :], across[0][:, :].rearrange("p (h q) -> p h q", h=H),
                                                bc(same[:, 0:1], [0, H], [1, P]), ALU.add))
                ch.link(nc.vector.memset(fresh[:, 0:1], 0.0))
                ch.link(nc.vector.tensor_reduce(carry[:, :], reach[:, :, :], AX, ALU.max))
                for h in range(H):
                    ins = nc.vector.tensor_tensor_scan(peak[:, :, h], fresh[:, :], score[:, h, :],
                                                       carry[:, h:h + 1], ALU.add, ALU.max)
                ins.then_inc(peaks, 1)

            @block.tensor
            def _(pe):
                pe.wait_ge(diag_ready, 1)
                nc.tensor.matmul(across[0][:, :], C.ones[:, :], diag[:, 0:H, :].rearrange("p h q -> p (h q)"),
                                 start=True, stop=True)
                nc.tensor.matmul(across[1][:, 0:P], C.ones[:, :], diag[:, H, :], start=True,
                                 stop=True).then_inc(spread, 1)


def sum_edges(nc, C, g, S):
    steps = g.slots // G2
    banks = 4
    hd = g.feats // H
    with stage(nc, g.name + "_") as (sb, ps, sem):
        index = [sb(f"su_index{h}", [P, U], I32) for h in range(2)]
        got = [sb(f"su_got{h}", [P, U, g.feats]) for h in range(2)] if g is REL else None
        rows = [sb(f"su_rows{h}", [P, U, P], U16) for h in range(2)]
        low_t = [sb(f"su_low_t{h}", [P, U, P]) for h in range(2)]
        low = [sb(f"su_low{h}", [P, U, P]) for h in range(2)]
        under = [sb(f"su_under{h}", [P, U * H]) for h in range(2)]
        weight = [sb(f"su_weight{h}", [P, U, H]) for h in range(2)]
        terms = [sb(f"su_terms{h}", [P, U, g.out]) for h in range(2)]
        look = [ps(f"su_look{h}", [P, 512]) for h in range(2)]
        total = [ps(f"su_total{b}", [P, 512]) for b in range(banks)]
        index_ready = sem("su_index_ready")
        begun = sem("su_begun")
        gathered = [sem(f"su_gathered{h}") for h in range(2)]
        rows_in = [sem(f"su_rows_in{h}") for h in range(2)]
        low_ready = sem("su_low_ready")
        looked = sem("su_looked")
        chain = sem("su_chain")
        lowered = sem("su_lowered")
        weighed = sem("su_weighed")
        ready = sem("su_terms_ready")
        totalled = sem("su_totalled")
        added = sem("su_added")
        cleared = sem("su_cleared")
        with nc.Block() as block:
            @block.sync
            def _(sp):
                def step(i):
                    for h in range(2):
                        wait_before_reuse(sp, low_ready, i, 2, h - 1)
                        sp.dma_start(rows[h][:, :, :].rearrange("p u e -> p (u e)"), row_bcast(
                            S.low_rows[bass.ds(i * G2 + h * U, U), :].rearrange("u e -> (u e)"))).then_inc(
                                rows_in[h], 16)

                each_step(sp, steps, step)

            @block.gpsimd
            def _(pool):
                nc.gpsimd.memset(S.sums[:, :], 0.0).then_inc(cleared, 1)

                def step(i):
                    for h in range(2):
                        wait_before_reuse(pool, ready, i, 2, h - 1)
                        pool.sem_inc(begun, 1)
                        nc.gpsimd.tensor_copy(index[h][:, :],
                                              S.slot_row[:, bass.ds(i * G2 + h * U, U)]).then_inc(index_ready, 1)
                        pool.wait_ge(index_ready, i * 2 + h + 1)
                        pool.sem_inc(begun, 1)
                        for u in range(U):
                            nc.gpsimd.indirect_dma_start(
                                got[h][:, u, :], None, S.feature_table,
                                bass.IndirectOffsetOnAxis(ap=index[h][:, u:u + 1], axis=0)).then_inc(gathered[h], 16)

                if g is REL:
                    each_step(pool, steps, step)

            @block.vector
            def _(dve):
                dve.wait_ge(cleared, 1)

                def step(i):
                    ch = Chain(dve, chain, i, 2)
                    for h in range(2):
                        at = i * G2 + h * U
                        dve.wait_ge(rows_in[h], i * 16 + 16)
                        nc.vector.tensor_scalar(low_t[h][:, :, :], rows[h][:, :, :], C.part[:, 0:1], None,
                                                ALU.is_equal).then_inc(low_ready, 1)
                        onehot(nc, C, low[h][:, :, :], S.slot_low[:, bass.ds(at, 1)], P)
                        dve.wait_ge(looked, i * 2 + h + 1)
                        ch.link(nc.vector.tensor_tensor(under[h][:, :], S.score[:, bass.ds(at * H, U * H)],
                                                        look[h][:, 0:U * H], ALU.subtract))
                        nc.vector.tensor_scalar(under[h][:, :], under[h][:, :], 0.0, None, ALU.min).then_inc(lowered, 1)
                        if g is REL:
                            dve.wait_ge(gathered[h], (i * 16 + 16) * U)
                            feats = got[h][:, :, :].rearrange("p u (h d) -> p u h d", h=H)
                        else:
                            feats = S.kept[:, bass.ds(at, U), :].rearrange("p u (h d) -> p u h d", h=H)
                        dve.wait_ge(weighed, i * 2 + h + 1)
                        nc.vector.tensor_copy(terms[h][:, :, g.feats:g.out], weight[h][:, :, :])
                        nc.vector.tensor_tensor(
                            terms[h][:, :, 0:g.feats].rearrange("p u (h d) -> p u h d", h=H), feats,
                            bc(weight[h][:, 0, 0:1], [H, U], [1, H], [0, hd]), ALU.mult).then_inc(ready, 1)
                        for u in range(U):
                            n = h * U + u
                            b = dve.value_load(S.block_row[0:1, bass.ds(at + u, 1)], min_val=0, max_val=NB - 1)
                            dve.wait_ge(totalled, i * G2 + n + 1)
                            wait_after(dve, added, i, n)
                            block_sums = S.sums[:, bass.ds(b * g.out, g.out)]
                            nc.vector.tensor_tensor(block_sums, block_sums, total[n % banks][:, 0:g.out],
                                                    ALU.add).then_inc(added, 1)

                def wait_after(eng, sem_, i, n):
                    if not isinstance(i, int) or n:
                        eng.wait_ge(sem_, i * G2 + n)

                each_step(dve, steps, step)

            @block.tensor
            def _(pe):
                def step(i):
                    for h in range(2):
                        at = i * G2 + h * U
                        pe.wait_ge(low_ready, i * 2 + h + 1)
                        blocks = []
                        for u in range(U):
                            b = pe.value_load(S.block_row[0:1, bass.ds(at + u, 1)], min_val=0, max_val=NB - 1)
                            last = nc.tensor.matmul(look[h][:, u * H:(u + 1) * H], low_t[h][:, u, :],
                                                    S.peak[:, bass.ds(b * H, H)], start=True, stop=True)
                        last.then_inc(looked, 1)
                        pe.wait_ge(ready, i * 2 + h + 1)
                        for u in range(U):
                            n = h * U + u
                            if not isinstance(i, int) or n >= banks:
                                pe.wait_ge(added, i * G2 + n - banks + 1)
                            nc.tensor.matmul(total[n % banks][:, 0:g.out], low[h][:, u, :], terms[h][:, u, :],
                                             start=True, stop=True).then_inc(totalled, 1)

                each_step(pe, steps, step)

            @block.scalar
            def _(act):
                def step(i):
                    for h in range(2):
                        act.wait_ge(lowered, i * 2 + h + 1)
                        nc.scalar.activation(weight[h][:, :, :].rearrange("p u h -> p (u h)"), under[h][:, :],
                                             ACT.Exp).then_inc(weighed, 1)

                each_step(act, steps, step)


def normalise(nc, C, S, name):
    with stage(nc) as (sb, ps, sem):
        square = sb(f"{name}_square", [P, NB, D])
        mean = sb(f"{name}_mean", [P, NB])
        var = sb(f"{name}_var", [P, NB])
        std = sb(f"{name}_std", [P, NB])
        chain = sem(f"{name}_chain")
        var_ready = sem(f"{name}_var_ready")
        std_ready = sem(f"{name}_std_ready")
        with nc.Block() as block:
            @block.vector
            def _(dve):
                ch = Chain(dve, chain)
                ch.link(nc.vector.tensor_reduce(mean[:, :], S.x[:, :, :], AX, ALU.add))
                ch.link(nc.vector.tensor_scalar(mean[:, :], mean[:, :], 1.0 / D, None, ALU.mult))
                ch.link(nc.vector.tensor_tensor(S.normed[:, :, :], S.x[:, :, :], bc(mean[:, 0:1], [1, NB], [0, D]),
                                                ALU.subtract))
                ch.link(nc.vector.tensor_tensor(square[:, :, :], S.normed[:, :, :], S.normed[:, :, :], ALU.mult))
                ch.link(nc.vector.tensor_reduce(var[:, :], square[:, :, :], AX, ALU.add))
                nc.vector.tensor_scalar(var[:, :], var[:, :], 1.0 / D, EPS, ALU.mult, ALU.add).then_inc(var_ready, 1)
                dve.wait_ge(std_ready, 1)
                ch.link(nc.vector.reciprocal(var[:, :], std[:, :]))
                ch.link(nc.vector.tensor_tensor(S.normed[:, :, :], S.normed[:, :, :], bc(var[:, 0:1], [1, NB], [0, D]),
                                                ALU.mult))

            @block.scalar
            def _(act):
                act.wait_ge(var_ready, 1)
                nc.scalar.activation(std[:, :], var[:, :], ACT.Sqrt).then_inc(std_ready, 1)


def load_nodes(nc, S, x_in):
    last = N - (NB - 1) * P
    with stage(nc) as (_, _, sem):
        cleared = sem("ln_cleared")
        loaded = sem("ln_loaded")
        with nc.Block() as block:
            @block.gpsimd
            def _(pool):
                nc.gpsimd.memset(S.x[:, NB - 1, :], 0.0).then_inc(cleared, 1)

            @block.sync
            def _(sp):
                sp.dma_start(S.x[:, 0:NB - 1, :],
                             x_in[0:(NB - 1) * P, :].rearrange("(t p) d -> p t d", p=P)).then_inc(loaded, 16)
                sp.wait_ge(cleared, 1)
                sp.dma_start(S.x[0:last, NB - 1, :], x_in[(NB - 1) * P:N, :]).then_inc(loaded, 16)
                sp.wait_ge(loaded, 32)


def relation_features(nc, C, S, w_in, left_in, right_in):
    RH = R * H
    with stage(nc) as (sb, ps, sem):
        w = sb("rf_w", [P, KC, R, H, HD])
        att = [sb(f"rf_att{s}", [P, R * D]) for s in range(2)]
        prod = sb("rf_prod", [P, KC, R * D])
        w_att = sb("rf_w_att", [P, KC, 2 * RH])
        tile = [sb(f"rf_tile{h}", [P, D]) for h in range(2)]
        turned = [sb(f"rf_turned{h}", [P, KC, P]) for h in range(2)]
        feats = [sb(f"rf_feats{h}", [P, R * D]) for h in range(2)]
        parts = [sb(f"rf_parts{h}", [P, RH]) for h in range(2)]
        turn = ps("rf_turn", [P, 512])
        banks = [ps(f"rf_bank{q}", [P, 512]) for q in range(4)]
        part = ps("rf_part", [P, 512])
        loaded = sem("rf_loaded")
        chain = sem("rf_chain")
        w_ready = sem("rf_w_ready")
        tile_ready = sem("rf_tile_ready")
        turn_done = sem("rf_turn_done")
        turn_copied = sem("rf_turn_copied")
        bank_done = sem("rf_bank_done")
        act_copied = sem("rf_act_copied")
        dve_copied = sem("rf_dve_copied")
        part_copied = sem("rf_part_copied")
        part_kept = sem("rf_part_kept")
        stored = [sem(f"rf_stored{h}") for h in range(2)]
        n_loads = KC + 2
        with nc.Block() as block:
            @block.sync
            def _(sp):
                for kc in range(KC):
                    sp.dma_start(w[:, kc, :, :, :].rearrange("p r h d -> p (r h) d"),
                                 w_in[:, :, kc * P:(kc + 1) * P, :].rearrange(
                                     "r h k d -> k (r h) d")).then_inc(loaded, 16)
                for s, a in enumerate((left_in, right_in)):
                    sp.dma_start(att[s][:, :], row_bcast(a.rearrange("r h d -> (r h d)"))).then_inc(loaded, 16)

                def step(i):
                    for h in range(2):
                        t = i * 2 + h
                        sp.wait_ge(act_copied, i * 4 + 2 * h + 2)
                        sp.wait_ge(dve_copied, i * 4 + 2 * h + 2)
                        sp.dma_start(S.feature_table[bass.ds(t * P * R, P * R), :].rearrange("(p r) d -> p (r d)", r=R),
                                     feats[h][:, :]).then_inc(stored[h], 16)
                        sp.wait_ge(part_copied, i * 2 + h + 1)
                        sp.dma_start(S.score_table[bass.ds(t * P * R, P * R), :].rearrange("(p r) h -> p (r h)", r=R),
                                     parts[h][:, :]).then_inc(stored[h], 16)

                each_step(sp, NB // 2, step)
                for h in range(2):
                    sp.wait_ge(stored[h], NB // 2 * 32)

            @block.gpsimd
            def _(pool):
                def step(i):
                    for h in range(2):
                        wait_before_reuse(pool, turn_done, i, 2, h - 1)
                        nc.gpsimd.tensor_copy(tile[h][:, :], S.normed[:, bass.ds(i * 2 + h, 1), :].rearrange(
                            "p t d -> p (t d)")).then_inc(tile_ready, 1)

                each_step(pool, NB // 2, step)

            @block.tensor
            def _(pe):
                pe.wait_ge(w_ready, 1)

                def step(i):
                    for h in range(2):
                        t = i * 2 + h
                        if not isinstance(t, int) or t:
                            pe.wait_ge(turn_copied, i * 2 + h)
                        pe.wait_ge(tile_ready, i * 2 + h + 1)
                        for kc in range(KC):
                            last = nc.tensor.transpose(turn[:, kc * P:(kc + 1) * P], tile[h][:, kc * P:(kc + 1) * P],
                                                       C.ident[:, :])
                        last.then_inc(turn_done, 1)
                        pe.wait_ge(turn_copied, i * 2 + h + 1)
                        for q in range(5):
                            if not isinstance(t, int) or t:
                                used, n = ((act_copied, 2), (dve_copied, 2), (part_kept, 1))[q // 2]
                                pe.wait_ge(used, i * 2 * n + n * h + (q % 2 + 1 - n if q < 4 else 0))
                            out = banks[q][:, :] if q < 4 else part[:, 0:2 * RH]
                            for kc in range(KC):
                                rhs = (w[:, kc, 2 * q:2 * q + 2, :, :].rearrange("p r h d -> p (r h d)") if q < 4
                                       else w_att[:, kc, :])
                                last = nc.tensor.matmul(out, turned[h][:, kc, :], rhs, start=(kc == 0),
                                                        stop=(kc == KC - 1))
                            last.then_inc(bank_done, 1)

                each_step(pe, NB // 2, step)

            @block.scalar
            def _(act):
                def step(i):
                    for h in range(2):
                        act.wait_ge(turn_done, i * 2 + h + 1)
                        nc.scalar.copy(turned[h][:, :, :].rearrange("p k n -> p (k n)"),
                                       turn[:, 0:KC * P]).then_inc(turn_copied, 1)
                        wait_before_reuse(act, stored[h], i, 32)
                        for q in range(2):
                            act.wait_ge(bank_done, i * 10 + 5 * h + q + 1)
                            nc.scalar.copy(feats[h][:, q * 512:(q + 1) * 512], banks[q][:, :]).then_inc(act_copied, 1)

                each_step(act, NB // 2, step)

            @block.vector
            def _(dve):
                ch = Chain(dve, chain)
                dve.wait_ge(loaded, 16 * n_loads)
                for s in range(2):
                    ch.link(nc.vector.tensor_tensor(prod[:, :, :], w[:, :, :, :, :].rearrange("p k r h d -> p k (r h d)"),
                                                    bc(att[s][:, 0:1], [0, KC], [1, R * D]), ALU.mult))
                    ch.link(nc.vector.tensor_reduce(w_att[:, :, s * RH:(s + 1) * RH],
                                                    prod[:, :, :].rearrange("p k (g d) -> p k g d", d=HD), AX, ALU.add))
                nc.vector.tensor_copy(parts[0][:, 0:1], w_att[:, 0, 0:1]).then_inc(w_ready, 1)

                def step(i):
                    for h in range(2):
                        wait_before_reuse(dve, stored[h], i, 32)
                        for q in range(2, 4):
                            dve.wait_ge(bank_done, i * 10 + 5 * h + q + 1)
                            nc.vector.tensor_copy(feats[h][:, q * 512:(q + 1) * 512],
                                                  banks[q][:, :]).then_inc(dve_copied, 1)
                        dve.wait_ge(bank_done, i * 10 + 5 * h + 5)
                        nc.vector.tensor_copy(parts[h][:, :], part[:, 0:RH]).then_inc(part_copied, 1)
                        nc.vector.tensor_copy(S.dest_table[:, bass.ds((i * 2 + h) * RH, RH)],
                                              part[:, RH:2 * RH]).then_inc(part_kept, 1)

                each_step(dve, NB // 2, step)


def add_attention(nc, C, S, bias_in):
    with stage(nc) as (sb, ps, sem):
        bias = sb("aa_bias", [P, D])
        inverse = sb("aa_inverse", [P, NB, H])
        loaded = sem("aa_loaded")
        chain = sem("aa_chain")
        with nc.Block() as block:
            @block.sync
            def _(sp):
                sp.dma_start(bias[:, :], row_bcast(bias_in)).then_inc(loaded, 16)

            @block.vector
            def _(dve):
                ch = Chain(dve, chain)
                sums = S.sums[:, :].rearrange("p (b c) -> p b c", b=NB)
                ch.link(nc.vector.tensor_scalar(inverse[:, :, :], sums[:, :, D:D + H], 0.5, None, ALU.max))
                ch.link(nc.vector.reciprocal(inverse[:, :, :], inverse[:, :, :]))
                heads = sums[:, :, 0:D].rearrange("p b (h d) -> p b h d", h=H)
                ch.link(nc.vector.tensor_tensor(heads, heads, bc(inverse[:, 0, 0:1], [H, NB], [1, H], [0, HD]), ALU.mult))
                dve.wait_ge(loaded, 16)
                ch.link(nc.vector.tensor_tensor(sums[:, :, 0:D], sums[:, :, 0:D], bc(bias[:, 0:1], [0, NB], [1, D]),
                                                ALU.add))
                ch.link(nc.vector.tensor_tensor(S.x[:, :, :], S.x[:, :, :], sums[:, :, 0:D], ALU.add))


def routing_features(nc, C, S, w_in, src_in, dst_in):
    XH = X * H
    WIDTH = XH + 2 * H
    with stage(nc) as (sb, ps, sem):
        w = sb("gf_w", [P, KC, WIDTH])
        att = sb("gf_att", [P, 2, XH])
        prod = sb("gf_prod", [P, KC, XH])
        tile = [sb(f"gf_tile{h}", [P, D]) for h in range(2)]
        turned = [sb(f"gf_turned{h}", [P, KC, P]) for h in range(2)]
        feats = [sb(f"gf_feats{h}", [P, XH + H]) for h in range(2)]
        turn = [ps(f"gf_turn{h}", [P, 512]) for h in range(2)]
        out = [ps(f"gf_out{h}", [P, 512]) for h in range(2)]
        loaded = sem("gf_loaded")
        chain = sem("gf_chain")
        w_ready = sem("gf_w_ready")
        tile_ready = sem("gf_tile_ready")
        turn_done = sem("gf_turn_done")
        turn_copied = sem("gf_turn_copied")
        out_done = sem("gf_out_done")
        copied = sem("gf_copied")
        kept = sem("gf_kept")
        stored = [sem(f"gf_stored{h}") for h in range(2)]
        with nc.Block() as block:
            @block.sync
            def _(sp):
                sp.dma_start(w[:, :, 0:XH], w_in.rearrange("(k p) c -> p k c", p=P)).then_inc(loaded, 16)
                for s, a in enumerate((src_in, dst_in)):
                    sp.dma_start(att[:, s, :], row_bcast(a.rearrange("h x -> (h x)"))).then_inc(loaded, 16)

                def step(i):
                    for h in range(2):
                        sp.wait_ge(copied, i * 2 + h + 1)
                        sp.dma_start(S.score_table[bass.ds((i * 2 + h) * P, P), :], feats[h][:, :]).then_inc(stored[h], 16)

                each_step(sp, NB // 2, step)
                for h in range(2):
                    sp.wait_ge(stored[h], NB // 2 * 16)

            @block.gpsimd
            def _(pool):
                def step(i):
                    for h in range(2):
                        wait_before_reuse(pool, turn_done, i, 2, h - 1)
                        nc.gpsimd.tensor_copy(tile[h][:, :], S.normed[:, bass.ds(i * 2 + h, 1), :].rearrange(
                            "p t d -> p (t d)")).then_inc(tile_ready, 1)

                each_step(pool, NB // 2, step)

            @block.tensor
            def _(pe):
                pe.wait_ge(w_ready, 1)

                def step(i):
                    for h in range(2):
                        wait_before_reuse(pe, turn_copied, i, 2, h - 1)
                        pe.wait_ge(tile_ready, i * 2 + h + 1)
                        for kc in range(KC):
                            last = nc.tensor.transpose(turn[h][:, kc * P:(kc + 1) * P],
                                                       tile[h][:, kc * P:(kc + 1) * P], C.ident[:, :])
                        last.then_inc(turn_done, 1)
                        pe.wait_ge(turn_copied, i * 2 + h + 1)
                        wait_before_reuse(pe, kept, i, 2, h - 1)
                        for kc in range(KC):
                            last = nc.tensor.matmul(out[h][:, 0:WIDTH], turned[h][:, kc, :], w[:, kc, :],
                                                    start=(kc == 0), stop=(kc == KC - 1))
                        last.then_inc(out_done, 1)

                each_step(pe, NB // 2, step)

            @block.scalar
            def _(act):
                def step(i):
                    for h in range(2):
                        act.wait_ge(turn_done, i * 2 + h + 1)
                        nc.scalar.copy(turned[h][:, :, :].rearrange("p k n -> p (k n)"),
                                       turn[h][:, 0:KC * P]).then_inc(turn_copied, 1)

                each_step(act, NB // 2, step)

            @block.vector
            def _(dve):
                ch = Chain(dve, chain)
                dve.wait_ge(loaded, 48)
                for s in range(2):
                    ch.link(nc.vector.tensor_tensor(prod[:, :, :], w[:, :, 0:XH], bc(att[:, s, 0:1], [0, KC], [1, XH]),
                                                    ALU.mult))
                    ch.link(nc.vector.tensor_reduce(w[:, :, XH + s * H:XH + (s + 1) * H],
                                                    prod[:, :, :].rearrange("p k (h x) -> p k h x", x=X), AX, ALU.add))
                nc.vector.tensor_copy(prod[:, 0, 0:1], w[:, 0, 0:1]).then_inc(w_ready, 1)

                def step(i):
                    for h in range(2):
                        dve.wait_ge(out_done, i * 2 + h + 1)
                        wait_before_reuse(dve, stored[h], i, 16)
                        nc.vector.tensor_copy(feats[h][:, :], out[h][:, 0:XH + H]).then_inc(copied, 1)
                        nc.vector.tensor_copy(S.dest_table[:, bass.ds((i * 2 + h) * H, H)],
                                              out[h][:, XH + H:WIDTH]).then_inc(kept, 1)

                each_step(dve, NB // 2, step)


def route(nc, C, S, bias_in, gamma_in, beta_in):
    XH = X * H
    with stage(nc) as (sb, ps, sem):
        rows = sb("ro_rows", [P, 3, XH])
        agg = sb("ro_agg", [P, NB, XH])
        square = sb("ro_square", [P, NB, XH])
        inverse = sb("ro_inverse", [P, NB, H])
        mean = sb("ro_mean", [P, NB])
        var = sb("ro_var", [P, NB])
        std = sb("ro_std", [P, NB])
        score = sb("ro_score", [P, NB, X])
        better = sb("ro_better", [P, NB, X])
        worse = sb("ro_worse", [P, NB])
        rank = sb("ro_rank", [P, NB, X])
        best = sb("ro_best", [P, NB])
        power = sb("ro_power", [P, NB, X])
        loaded = sem("ro_loaded")
        chain = sem("ro_chain")
        var_ready = sem("ro_var_ready")
        std_ready = sem("ro_std_ready")
        shifted = sem("ro_shifted")
        powered = sem("ro_powered")
        with nc.Block() as block:
            @block.sync
            def _(sp):
                for s, a in enumerate((bias_in, gamma_in, beta_in)):
                    sp.dma_start(rows[:, s, :], row_bcast(a)).then_inc(loaded, 16)

            @block.scalar
            def _(act):
                act.wait_ge(var_ready, 1)
                nc.scalar.activation(std[:, :], var[:, :], ACT.Sqrt).then_inc(std_ready, 1)
                act.wait_ge(shifted, 1)
                nc.scalar.activation(power[:, :, :].rearrange("p b x -> p (b x)"),
                                     score[:, :, :].rearrange("p b x -> p (b x)"), ACT.Exp).then_inc(powered, 1)

            @block.vector
            def _(dve):
                ch = Chain(dve, chain)
                sums = S.sums[:, :].rearrange("p (b c) -> p b c", b=NB)

                def row(s):
                    return bc(rows[:, s, 0:1], [0, NB], [1, XH])

                def per_node(ap, n=XH):
                    return bc(ap[:, 0:1], [1, NB], [0, n])

                ch.link(nc.vector.tensor_scalar(inverse[:, :, :], sums[:, :, XH:XH + H], 1e-16, None, ALU.add))
                ch.link(nc.vector.reciprocal(inverse[:, :, :], inverse[:, :, :]))
                ch.link(nc.vector.tensor_tensor(agg[:, :, :].rearrange("p b (h x) -> p b h x", h=H),
                                                sums[:, :, 0:XH].rearrange("p b (h x) -> p b h x", h=H),
                                                bc(inverse[:, 0, 0:1], [H, NB], [1, H], [0, X]), ALU.mult))
                dve.wait_ge(loaded, 48)
                ch.link(nc.vector.tensor_tensor(agg[:, :, :], agg[:, :, :], row(0), ALU.add))
                ch.link(nc.vector.tensor_reduce(mean[:, :], agg[:, :, :], AX, ALU.add))
                ch.link(nc.vector.tensor_scalar(mean[:, :], mean[:, :], 1.0 / XH, None, ALU.mult))
                ch.link(nc.vector.tensor_tensor(agg[:, :, :], agg[:, :, :], per_node(mean), ALU.subtract))
                ch.link(nc.vector.tensor_tensor(square[:, :, :], agg[:, :, :], agg[:, :, :], ALU.mult))
                ch.link(nc.vector.tensor_reduce(var[:, :], square[:, :, :], AX, ALU.add))
                nc.vector.tensor_scalar(var[:, :], var[:, :], 1.0 / XH, EPS, ALU.mult, ALU.add).then_inc(var_ready, 1)
                dve.wait_ge(std_ready, 1)
                ch.link(nc.vector.reciprocal(var[:, :], std[:, :]))
                ch.link(nc.vector.tensor_tensor(agg[:, :, :], agg[:, :, :], per_node(var), ALU.mult))
                ch.link(nc.vector.tensor_tensor(agg[:, :, :], agg[:, :, :], row(1), ALU.mult))
                ch.link(nc.vector.tensor_tensor(agg[:, :, :], agg[:, :, :], row(2), ALU.add))
                ch.link(nc.vector.tensor_reduce(score[:, :, :], agg[:, :, :].rearrange("p b (h x) -> p b x h", h=H), AX,
                                                ALU.add))
                ch.link(nc.vector.tensor_scalar(score[:, :, :], score[:, :, :], 1.0 / H, None, ALU.mult))
                for x in range(X):
                    one = bc(score[:, 0, x:x + 1], [X, NB], [0, X])
                    ch.link(nc.vector.tensor_tensor(better[:, :, :], score[:, :, :], one, ALU.is_gt))
                    if x:
                        ch.link(nc.vector.tensor_tensor(better[:, :, 0:x], score[:, :, 0:x],
                                                        bc(score[:, 0, x:x + 1], [X, NB], [0, x]), ALU.is_ge))
                    ch.link(nc.vector.tensor_reduce(rank[:, :, x], better[:, :, :], AX, ALU.add))
                ch.link(nc.vector.tensor_reduce(best[:, :], score[:, :, :], AX, ALU.max))
                nc.vector.tensor_tensor(score[:, :, :], score[:, :, :], per_node(best, X),
                                        ALU.subtract).then_inc(shifted, 1)
                dve.wait_ge(powered, 1)
                ch.link(nc.vector.tensor_scalar(rank[:, :, :], rank[:, :, :], 1.5, None, ALU.is_lt))
                ch.link(nc.vector.tensor_tensor(power[:, :, :], power[:, :, :], rank[:, :, :], ALU.mult))
                ch.link(nc.vector.tensor_reduce(worse[:, :], power[:, :, :], AX, ALU.add))
                ch.link(nc.vector.reciprocal(worse[:, :], worse[:, :]))
                ch.link(nc.vector.tensor_tensor(S.gate[:, :, :], power[:, :, :], per_node(worse, X), ALU.mult))


GT = 3


def experts(nc, C, S, w1_in, b1_in, w2_in, b2_in, out):
    FT = FF // P
    XF = X * FT
    GN = GT * P
    groups = NB // GT
    last = N - (NB - 1) * P
    with stage(nc) as (sb, ps, sem):
        w1 = sb("ex_w1", [P, KC, X, FF])
        w2 = sb("ex_w2", [P, XF, D])
        b1 = sb("ex_b1", [P, XF])
        b1_rows = sb("ex_b1_rows", [XF, P])
        b2 = sb("ex_b2", [1, X, D])
        tiles = sb("ex_tiles", [P, GT, D])
        turned = sb("ex_turned", [P, KC, GN])
        hidden = sb("ex_hidden", [P, XF, GN])
        turn = ps("ex_turn", [P, 512])
        up = [ps(f"ex_up{q}", [P, 512]) for q in range(3)]
        down = [ps(f"ex_down{q}", [P, 512]) for q in range(4)]
        loaded = sem("ex_loaded")
        b1_turned = sem("ex_b1_turned")
        b1_ready = sem("ex_b1_ready")
        tiles_ready = sem("ex_tiles_ready")
        turn_done = sem("ex_turn_done")
        turn_copied = sem("ex_turn_copied")
        up_done = sem("ex_up_done")
        gelu_done = sem("ex_gelu_done")
        down_done = sem("ex_down_done")
        added = sem("ex_added")
        stored = sem("ex_stored")
        with nc.Block() as block:
            @block.sync
            def _(sp):
                for kc in range(KC):
                    sp.dma_start(w1[:, kc, :, :], w1_in[:, kc * P:(kc + 1) * P, :].rearrange(
                        "x k f -> k x f")).then_inc(loaded, 16)
                sp.dma_start(w2[:, :, :], w2_in.rearrange("x (f p) d -> p (x f) d", p=P)).then_inc(loaded, 16)
                sp.dma_start(b1_rows[:, :], b1_in.rearrange("x (f p) -> (x f) p", p=P)).then_inc(loaded, 16)
                sp.dma_start(b2[:, :, :], b2_in.rearrange("(o x) d -> o x d", o=1)).then_inc(loaded, 16)
                sp.wait_ge(added, NB * X)
                sp.dma_start(out[0:(NB - 1) * P, :].rearrange("(t p) d -> p t d", p=P),
                             S.x[:, 0:NB - 1, :]).then_inc(stored, 16)
                sp.dma_start(out[(NB - 1) * P:N, :], S.x[0:last, NB - 1, :]).then_inc(stored, 16)
                sp.wait_ge(stored, 32)

            @block.gpsimd
            def _(pool):
                def step(i):
                    wait_before_reuse(pool, turn_done, i, KC)
                    nc.gpsimd.tensor_copy(tiles[:, :, :], S.normed[:, bass.ds(i * GT, GT), :]).then_inc(tiles_ready, 1)

                each_step(pool, groups, step)

            @block.tensor
            def _(pe):
                pe.wait_ge(loaded, 16 * (KC + 3))
                nc.tensor.transpose(turn[:, 0:XF], b1_rows[:, :], C.ident[0:XF, 0:XF]).then_inc(b1_turned, 1)
                pe.wait_ge(b1_ready, 1)

                def step(i):
                    pe.wait_ge(tiles_ready, i + 1)
                    for kc in range(KC):
                        if not (isinstance(i, int) and kc == 0):
                            pe.wait_ge(turn_copied, i * KC + kc)
                        for t in range(GT):
                            ins = nc.tensor.transpose(turn[:, t * P:(t + 1) * P], tiles[:, t, kc * P:(kc + 1) * P],
                                                      C.ident[:, :])
                        ins.then_inc(turn_done, 1)
                    pe.wait_ge(turn_copied, i * KC + KC)
                    for xf in range(XF):
                        if not (isinstance(i, int) and xf < 3):
                            pe.wait_ge(gelu_done, i * XF + xf - 2)
                        x, f = divmod(xf, FT)
                        for kc in range(KC):
                            ins = nc.tensor.matmul(up[xf % 3][:, 0:GN], w1[:, kc, x, f * P:(f + 1) * P],
                                                   turned[:, kc, :], start=(kc == 0), stop=(kc == KC - 1))
                        ins.then_inc(up_done, 1)
                    pe.wait_ge(gelu_done, i * XF + XF)
                    for n in range(GT * X):
                        t, x = divmod(n, X)
                        if not (isinstance(i, int) and n < 4):
                            pe.wait_ge(added, i * GT * X + n - 3)
                        for f in range(FT):
                            nc.tensor.matmul(down[n % 4][:, 0:D], hidden[:, x * FT + f, t * P:(t + 1) * P],
                                             w2[:, x * FT + f, :], start=(f == 0), stop=False)
                        nc.tensor.matmul(down[n % 4][:, 0:D], C.ones[0:1, :], b2[0:1, x, :], start=False,
                                         stop=True).then_inc(down_done, 1)

                each_step(pe, groups, step)

            @block.scalar
            def _(act):
                act.wait_ge(b1_turned, 1)
                nc.scalar.copy(b1[:, :], turn[:, 0:XF]).then_inc(b1_ready, 1)
                act.wait_ge(b1_ready, 1)

                def step(i):
                    for kc in range(KC):
                        act.wait_ge(turn_done, i * KC + kc + 1)
                        nc.scalar.copy(turned[:, kc, :], turn[:, 0:GN]).then_inc(turn_copied, 1)
                    for xf in range(XF):
                        act.wait_ge(up_done, i * XF + xf + 1)
                        nc.scalar.activation(hidden[:, xf, :], up[xf % 3][:, 0:GN], ACT.Gelu,
                                             bias=b1[:, xf:xf + 1]).then_inc(gelu_done, 1)

                each_step(act, groups, step)

            @block.vector
            def _(dve):
                def step(i):
                    for n in range(GT * X):
                        t, x = divmod(n, X)
                        dve.wait_ge(down_done, i * GT * X + n + 1)
                        if not (isinstance(i, int) and n == 0):
                            dve.wait_ge(added, i * GT * X + n)
                        row = S.x[:, bass.ds(i * GT + t, 1), :].rearrange("p t d -> p (t d)")
                        gate = S.gate[:, bass.ds(i * GT + t, 1), x:x + 1].rearrange("p t o -> p (t o)")
                        nc.vector.scalar_tensor_tensor(row, down[n % 4][:, 0:D], gate, row, ALU.mult,
                                                       ALU.add).then_inc(added, 1)

                each_step(dve, groups, step)


class Space:
    pass


def graph_space(nc, g):
    S = Space()

    def dram(name, shape, dt=F32):
        return nc.dram_tensor(f"{g.name}_{name}", shape, dt, kind="Internal").ap()

    S.key_rows = dram("key_rows", [g.raw_tiles * P, 2, P], U16)
    S.sorted = dram("sorted", [g.tiles * P * P, 1], I32)
    S.low_rows = dram("low_rows", [g.tiles * P, P], U16)
    S.block_dram = dram("block", [g.tiles * P], I32)
    S.score_table = dram("score_table", [NB * P * g.rels, g.row])
    S.feature_table = dram("feature_table", [NB * P * g.rels, g.feats]) if g is REL else None
    S.score_rows = dram("score_rows", [g.slots, H, P])
    S.peak_table = dram("peak_table", [g.tiles * P * P, H])
    return S


def attend(nc, C, g, S, src, dst, typ, features, finish):
    with stage(nc, g.name + "_") as (sb, _, _):
        S.counts = sb(f"counts", [P, NBP])
        S.start = sb(f"start", [P, NBP])
        S.last = sb(f"last", [P, NBP], I32)
        S.block_row = sb(f"block_row", [1, g.tiles * P], I32)
        S.dest_table = sb(f"dest_table", [P, NB * g.er])
        S.sums = sb(f"sums", [P, NB * g.out])
        with stage(nc, g.name + "_") as (sb, _, _):
            W = g.raw_tiles * P
            S.lo, S.hi, S.key = (sb(f"{name}", [P, W]) for name in ("lo", "hi", "key"))
            S.packed = sb(f"packed", [P, W], I32)
            prepare_edges(nc, C, g, S, src, dst, typ)
            count_edges(nc, C, g, S)
            scatter_edges(nc, C, g, S)
        features(S)
        with stage(nc, g.name + "_") as (sb, _, _):
            W = g.tiles * P
            S.slot_row = sb(f"slot_row", [P, W], I32)
            S.slot_low = sb(f"slot_low", [P, W])
            S.slot_type = sb(f"slot_type", [P, W]) if g is REL else None
            S.score = sb(f"score", [P, g.slots * H])
            S.peak = sb(f"peak", [P, NB * H])
            S.kept = sb(f"kept", [P, g.slots, g.feats]) if g is ROUTE else None
            read_slots(nc, C, g, S)
            score_edges(nc, C, g, S)
            node_maxima(nc, C, g, S)
            sum_edges(nc, C, g, S)
        finish(S)


def gnn_moe_kernel(nc, x, src, dst, edge_type, conv_w, attn_l, attn_r, h_bias, w_gat, att_src, att_dst, b_gat,
                   ln_gamma, ln_beta, w1, b1, w2, b2, edge_index, out):
    rel, routing = graph_space(nc, REL), graph_space(nc, ROUTE)
    with stage(nc) as (sb, _, _):
        C = Space()
        C.ident = sb("ident", [P, P])
        C.before = sb("before", [P, P])
        C.after = sb("after", [P, P])
        C.ones = sb("ones", [P, P])
        C.zero_bf = sb("zero_bf", [P, P], BF16)
        C.count_i = sb("count_i", [P, P], I32)
        C.part_i = sb("part_i", [P, 1], I32)
        C.count = sb("count", [P, P])
        C.part = sb("part", [P, 1])
        nodes = Space()
        nodes.x = sb("x_nodes", [P, NB, D])
        nodes.gate = sb("gate", [P, NB, X])
        constants(nc, C)
        load_nodes(nc, nodes, x)

        def with_normed(name, then):
            with ExitStack() as inner:
                nodes.normed = inner.enter_context(nc.sbuf_tensor(f"{name}_normed", [P, NB, D], F32))
                normalise(nc, C, nodes, name)
                then()

        def relation_stage(S):
            S.normed = nodes.normed
            relation_features(nc, C, S, conv_w, attn_l, attn_r)

        def routing_stage(S):
            S.normed = nodes.normed
            routing_features(nc, C, S, w_gat, att_src, att_dst)

        def finish_relations(S):
            S.x = nodes.x
            add_attention(nc, C, S, h_bias)

        def finish_routing(S):
            S.gate = nodes.gate
            route(nc, C, S, b_gat, ln_gamma, ln_beta)

        attend(nc, C, REL, rel, src, dst, edge_type,
               lambda S: with_normed("norm1", lambda: relation_stage(S)), finish_relations)
        attend(nc, C, ROUTE, routing, edge_index[0], edge_index[1], None,
               lambda S: with_normed("norm2", lambda: routing_stage(S)), finish_routing)
        with_normed("norm3", lambda: experts(nc, C, nodes, w1, b1, w2, b2, out))


_INS = ["x", "src", "dst", "edge_type_8", "L0_gnn_conv_weights", "L0_gnn_attn_l", "L0_gnn_attn_r", "L0_gnn_h_bias",
        "L0_ffn_W_gat", "L0_ffn_att_src", "L0_ffn_att_dst", "L0_ffn_b_gat", "L0_ffn_ln_gamma", "L0_ffn_ln_beta",
        "L0_ffn_W1", "L0_ffn_b1", "L0_ffn_W2", "L0_ffn_b2", "L0_ffn_edge_index"]


def kernel(**inputs):
    import numpy as _np
    import concourse.bacc as _bacc
    from concourse import mybir as _mybir
    from concourse.bass_utils import run_bass_kernel_spmd as _run

    nc = _bacc.Bacc("TRN2", target_bir_lowering=False, num_devices=1)
    arrays, args = {}, []
    for name in _INS:
        a = _np.ascontiguousarray(inputs[name])
        arrays[f"in_{name}_dram"] = a
        args.append(nc.dram_tensor(f"in_{name}_dram", a.shape, _mybir.dt.from_np(a.dtype), kind="ExternalInput").ap())
    out = nc.dram_tensor("out_0_dram", (N, D), F32, kind="ExternalOutput").ap()
    gnn_moe_kernel(nc, *args, out)
    r = _run(nc, [arrays], core_ids=[0])
    return r.results[0]["out_0_dram"]
```

```python
from contextlib import ExitStack, contextmanager

import concourse.bass as bass
from concourse import mybir

F32, BF16, I32, U16 = mybir.dt.float32, mybir.dt.bfloat16, mybir.dt.int32, mybir.dt.uint16
ALU = mybir.AluOpType
ACT = mybir.ActivationFunctionType
AX = mybir.AxisListType.X

P = 128
N = 3750
NB = -(-N // P)
NBP = 32
D = 256
KC = D // P
H = 4
R = 8
HD = D // H
E1 = 123750
E2 = 131072
X = 4
FF = 2 * D
U = 8
G2 = 2 * U
EPS = 1e-5
SLOPE = 0.2
BIG = 1.0e30
FREE_LO, FREE_HI = 255, 31


class Graph:

    def __init__(self, name, chunks, types, row, feats):
        self.name = name
        self.raw = -(-chunks // G2) * G2
        self.raw_tiles = -(-self.raw // P)
        self.slots = -(-(self.raw + NB) // G2) * G2
        self.tiles = -(-self.slots // P)
        self.lane = self.tiles * P
        self.rels = types
        self.er = types * H
        self.row = row
        self.feats = feats
        self.out = feats + H


REL = Graph("rel", -(-E1 // P), R, H, D)
ROUTE = Graph("route", E2 // P + NB, 1, X * H + H, X * H)


def row_bcast(ap, parts=P):
    return bass.AP(ap.tensor, ap.offset, [[0, parts]] + [list(x) for x in ap.ap])


class Chain:

    def __init__(self, eng, sem, step=None, per_step=0, before=0):
        self.eng, self.sem, self.step, self.per_step, self.before, self.n = eng, sem, step, per_step, before, 0

    def link(self, ins):
        ins.then_inc(self.sem, 1)
        self.n += 1
        at = self.before + self.n
        self.eng.wait_ge(self.sem, at if self.step is None else self.step * self.per_step + at)

    def end(self):
        assert self.step is None or self.n == self.per_step, (self.n, self.per_step)


@contextmanager
def stage(nc, name=""):
    sems = []
    with ExitStack() as ctx:
        def sb(label, shape, dt=F32):
            return ctx.enter_context(nc.sbuf_tensor(name + label, shape, dt))

        def ps(label, shape, dt=F32):
            return ctx.enter_context(nc.psum_tensor(name + label, shape, dt))

        def sem(label):
            sems.append(nc.alloc_semaphore(name + label))
            return sems[-1]

        yield sb, ps, sem
        if sems:
            nc.clear_and_free_semaphores(sems)
            nc.all_engine_barrier()


def each_step(eng, steps, body, live=None):
    body(0)
    with eng.Fori(1, steps) as i:
        if live is None:
            body(i)
        else:
            with eng.If(i < live):
                body(i)


def live_steps(eng, S, steps):
    return eng.value_load(S.live[0:1, 0:1], min_val=1, max_val=steps)


def wait_before_reuse(eng, sem, step, per_step, at=0):
    if not (isinstance(step, int) and step == 0):
        eng.wait_ge(sem, step * per_step + at)


def bc(ap, *dims):
    return bass.AP(ap.tensor, ap.offset, [list(ap.ap[0])] + [list(x) for x in dims])


def ahead(i, h):
    return (i, 1) if h == 0 else (i + 1, 0)


def places(eng, S, what, first, width):
    row = S.place_row[0:1, what, bass.ds(first, U)]
    _, values = eng.bass.values_load_multi_w_load_instructions(
        row, engines=[eng.engine], min_val=0, max_val=(NB - 1) * width,
        skip_runtime_bounds_check_because="count_edges makes them from blocks that it holds below NB")
    return values


def turns(tiles, arrays):
    return [(k, t, min(4, tiles - t)) for k in range(arrays) for t in range(0, tiles, 4)]


def constants(nc, C):
    with stage(nc) as (_, _, sem):
        filled = sem("const_filled")
        made = sem("const_made")
        with nc.Block() as block:
            @block.gpsimd
            def _(pool):
                nc.gpsimd.memset(C.ident[:, :], 0.0).then_inc(filled, 1)
                nc.gpsimd.memset(C.before[:, :], 1.0).then_inc(filled, 1)
                nc.gpsimd.memset(C.after[:, :], 1.0).then_inc(filled, 1)
                nc.gpsimd.memset(C.ones[:, :], 1.0).then_inc(filled, 1)
                nc.gpsimd.memset(C.zero_bf[:, :], 0.0).then_inc(filled, 1)
                nc.gpsimd.memset(C.zero_wide[:, :], 0.0).then_inc(filled, 1)
                pool.wait_ge(filled, 6)
                nc.gpsimd.affine_select(out=C.ident[:, :], in_=C.ident[:, :], compare_op=ALU.not_equal, fill=1.0,
                                        base=0, pattern=[[-1, P]], channel_multiplier=1).then_inc(made, 1)
                nc.gpsimd.affine_select(out=C.before[:, :], in_=C.before[:, :], compare_op=ALU.is_gt, fill=0.0,
                                        base=0, pattern=[[-1, P]], channel_multiplier=1).then_inc(made, 1)
                nc.gpsimd.affine_select(out=C.after[:, :], in_=C.after[:, :], compare_op=ALU.is_gt, fill=0.0,
                                        base=0, pattern=[[1, P]], channel_multiplier=-1).then_inc(made, 1)
                nc.gpsimd.iota(C.count_i[:, :], [[1, P]], base=0, channel_multiplier=0).then_inc(made, 1)
                nc.gpsimd.iota(C.part_i[:, :], [[0, 1]], base=0, channel_multiplier=1).then_inc(made, 1)
                pool.wait_ge(made, 5)

            @block.vector
            def _(dve):
                dve.wait_ge(made, 5)
                nc.vector.tensor_copy(C.count[:, :], C.count_i[:, :]).then_inc(filled, 1)
                nc.vector.tensor_copy(C.part[:, :], C.part_i[:, :]).then_inc(filled, 1)


def prepare_edges(nc, C, g, S, src_in, dst_in, type_in):
    T = g.raw_tiles
    W = T * P
    with stage(nc, g.name + "_") as (sb, ps, sem):
        src = sb("pe_src", [P, W], I32)
        dst = sb("pe_dst", [P, W], I32)
        typ = sb("pe_typ", [P, W], I32)
        lo_i = sb("pe_lo_i", [P, W], I32)
        hi_i = sb("pe_hi_i", [P, W], I32)
        a_f = sb("pe_a", [P, W])
        lo_f = sb("pe_lo", [P, W])
        hi_f = sb("pe_hi", [P, W])
        rows = sb("pe_rows", [P, T, 2, P], U16)
        a_ci = sb("pe_a_ci", [P, W], I32)
        k_ci = sb("pe_k_ci", [P, W], I32)
        turned = [ps(f"pe_turned{i}", [P, 512]) for i in range(6)]
        filled = sem("pe_filled")
        loaded = sem("pe_loaded")
        split = sem("pe_split")
        rows_out = sem("pe_rows_out")
        turn_done = sem("pe_turn_done")
        turn_used = sem("pe_turn_used")
        chain = sem("pe_chain")
        n_loads = []

        with nc.Block() as block:
            @block.gpsimd
            def _(pool):
                nc.gpsimd.memset(typ[:, :], 0).then_inc(filled, 1)
                if g is REL:
                    nc.gpsimd.memset(src[:, :], 0).then_inc(filled, 1)
                    nc.gpsimd.memset(dst[:, :], N).then_inc(filled, 1)
                else:
                    nc.gpsimd.iota(src[:, W - P:W], [[1, P]], base=0, channel_multiplier=P).then_inc(filled, 1)
                    nc.gpsimd.iota(dst[:, W - P:W], [[1, P]], base=0, channel_multiplier=P).then_inc(filled, 1)

            @block.sync
            def _(sp):
                sp.wait_ge(filled, 3)
                pairs = [(src, src_in), (dst, dst_in)] + ([(typ, type_in)] if g is REL else [])
                for sbuf, dram in pairs:
                    edges = E1 if g is REL else E2
                    tiles, rest = divmod(edges, P * P)
                    sp.dma_start(sbuf[:, 0:tiles * P].rearrange("p (t e) -> p t e", e=P),
                                 dram[0:tiles * P * P].rearrange("(t p e) -> p t e", p=P, e=P)).then_inc(loaded, 16)
                    n_loads.append(1)
                    full, last = divmod(rest, P)
                    if full:
                        sp.dma_start(sbuf[0:full, tiles * P:tiles * P + P],
                                     dram[tiles * P * P:tiles * P * P + full * P].rearrange(
                                         "(p e) -> p e", e=P)).then_inc(loaded, 16)
                        n_loads.append(1)
                    if last:
                        at = edges - last
                        sp.dma_start(sbuf[full:full + 1, tiles * P:tiles * P + last],
                                     dram[at:edges].rearrange("(p e) -> p e", p=1)).then_inc(loaded, 16)
                        n_loads.append(1)
                sp.wait_ge(split, 1)
                sp.dma_start(S.key_rows.rearrange("(t p) k e -> p t k e", p=P), rows[:, :, :, :]).then_inc(rows_out, 16)
                sp.wait_ge(rows_out, 16)

            @block.vector
            def _(dve):
                ch = Chain(dve, chain)
                dve.wait_ge(loaded, 16 * len(n_loads))
                dve.wait_ge(filled, 3)
                nc.vector.tensor_scalar(src[:, :], src[:, :], float(N - 1), None, ALU.min)
                ch.link(nc.vector.tensor_scalar(dst[:, :], dst[:, :], float(N), None, ALU.min))
                nc.vector.tensor_scalar(lo_i[:, :], dst[:, :], P - 1, None, ALU.bitwise_and)
                nc.vector.tensor_scalar(hi_i[:, :], dst[:, :], 7, None, ALU.logical_shift_right)
                ch.link(nc.vector.scalar_tensor_tensor(a_f[:, :], src[:, :], float(g.rels), typ[:, :], ALU.mult,
                                                       ALU.add))
                nc.vector.tensor_copy(lo_f[:, :], lo_i[:, :])
                ch.link(nc.vector.tensor_copy(hi_f[:, :], hi_i[:, :]))
                lo3 = lo_f[:, :].rearrange("p (t e) -> p t e", e=P)
                hi3 = hi_f[:, :].rearrange("p (t e) -> p t e", e=P)
                nc.vector.scalar_tensor_tensor(rows[:, :, 0, :], hi3, 256.0, lo3, ALU.mult, ALU.add)
                ch.link(nc.vector.tensor_copy(rows[:, :, 1, :], lo3))
                nc.vector.engine_nop().then_inc(split, 1)
                for q, (k, t0, n) in enumerate(turns(T, 3)):
                    dve.wait_ge(turn_done, q + 1)
                    out = (S.lo, S.hi, a_ci)[k][:, t0 * P:(t0 + n) * P]
                    nc.vector.tensor_copy(out, turned[q % 6][:, 0:n * P]).then_inc(turn_used, 1)
                dve.wait_ge(turn_used, len(turns(T, 3)))
                ch.link(nc.vector.scalar_tensor_tensor(S.key[:, :], S.hi[:, :], 256.0, S.lo[:, :], ALU.mult, ALU.add))
                ch.link(nc.vector.tensor_copy(k_ci[:, :], S.key[:, :]))
                ch.link(nc.vector.tensor_scalar(k_ci[:, :], k_ci[:, :], 15, None, ALU.logical_shift_left))
                ch.link(nc.vector.tensor_tensor(S.packed[:, :], k_ci[:, :], a_ci[:, :], ALU.bitwise_or))

            @block.tensor
            def _(pe):
                pe.wait_ge(split, 1)
                for q, (k, t0, n) in enumerate(turns(T, 3)):
                    if q >= 6:
                        pe.wait_ge(turn_used, q - 5)
                    for i in range(n):
                        last = nc.tensor.transpose(turned[q % 6][:, i * P:(i + 1) * P],
                                                   (lo_f, hi_f, a_f)[k][:, (t0 + i) * P:(t0 + i + 1) * P],
                                                   C.ident[:, :])
                    last.then_inc(turn_done, 1)


def onehot(nc, C, out, values, width):
    return nc.vector.tensor_tensor(out, bc(values, [1, U], [0, width]), bc(C.count[:, 0:1], [0, U], [1, width]),
                                   ALU.is_equal)


def count_edges(nc, C, g, S):
    steps = g.raw // G2
    with stage(nc, g.name + "_") as (sb, ps, sem):
        low = [sb(f"ce_low{h}", [P, U, P], BF16) for h in range(2)]
        blk = [sb(f"ce_blk{h}", [P, U, NBP], BF16) for h in range(2)]
        size = sb("ce_size", [P, NBP])
        size_i = sb("ce_size_i", [P, NBP], I32)
        ends = sb("ce_ends", [P, NBP])
        zeros = sb("ce_zeros", [P, NBP])
        starts = sb("ce_starts", [P, NBP])
        chunk_i = sb("ce_chunk_i", [P, g.tiles], I32)
        chunk_f = sb("ce_chunk_f", [P, g.tiles])
        past = sb("ce_past", [P, g.tiles, NBP])
        blocks = sb("ce_blocks", [P, g.tiles])
        places_i = sb("ce_places_i", [P, 3, g.tiles], I32)
        free = sb("ce_free", [P, g.tiles * P], I32)
        no_scores = sb("ce_no_scores", [P, g.slots * H])
        live_i = sb("ce_live_i", [P, NBP], I32)
        counts_ps = ps("ce_counts", [P, 512])
        sums_ps = ps("ce_sums", [P, 512])
        one = sem("ce_onehot_ready")
        used = [sem(f"ce_onehot_used{h}") for h in range(2)]
        cleared = sem("ce_cleared")
        counted = sem("ce_counted")
        copied = sem("ce_copied")
        summed = sem("ce_summed")
        chain = sem("ce_chain")
        stored = sem("ce_stored")
        numbered = sem("ce_numbered")
        numbers_ready = sem("ce_numbers_ready")
        with nc.Block() as block:
            @block.gpsimd
            def _(pool):
                nc.gpsimd.memset(free[:, :], (FREE_LO + 256 * FREE_HI) << 15).then_inc(numbered, 1)
                nc.gpsimd.iota(chunk_i[:, :], [[P * P, g.tiles]], base=0, channel_multiplier=P).then_inc(numbered, 1)
                nc.gpsimd.memset(no_scores[:, :], 0.0).then_inc(numbered, 1)

            @block.sync
            def _(sp):
                sp.wait_ge(numbered, 3)
                sp.dma_start(S.score_rows.rearrange("c h e -> (c h e)").rearrange("(p x) -> p x", p=P),
                             no_scores[:, :]).then_inc(stored, 16)
                sp.dma_start(S.sorted.rearrange("(p l) o -> p (l o)", p=P), free[:, :]).then_inc(stored, 16)
                sp.wait_ge(numbers_ready, 1)
                sp.dma_start(S.place_dram.rearrange("k (t p) -> p k t", p=P), places_i[:, :, :],
                             allow_slow_non_contiguous=True).then_inc(stored, 16)
                sp.dma_start(S.live_dram, live_i[N % P:N % P + 1, N // P:N // P + 1]).then_inc(stored, 16)
                sp.wait_ge(stored, 64)
                sp.dma_start(S.place_row[0:1, :, :],
                             S.place_dram.rearrange("(o k) c -> o k c", o=1)).then_inc(stored, 16)
                sp.dma_start(S.live[0:1, 0:1], S.live_dram).then_inc(stored, 16)
                sp.wait_ge(stored, 96)

            @block.vector
            def _(dve):
                def step(i):
                    for h in range(2):
                        wait_before_reuse(dve, used[h], i, 1)
                        at = i * G2 + h * U
                        onehot(nc, C, low[h][:, :, :], S.lo[:, bass.ds(at, 1)], P)
                        onehot(nc, C, blk[h][:, :, :], S.hi[:, bass.ds(at, 1)], NBP).then_inc(one, 1)

                each_step(dve, steps, step)
                ch = Chain(dve, chain)
                dve.wait_ge(counted, 1)
                ch.link(nc.vector.tensor_copy(S.counts[:, :], counts_ps[:, 0:NBP]))
                dve.wait_ge(summed, 1)
                ch.link(nc.vector.tensor_scalar(size_i[:, :], sums_ps[:, NBP:2 * NBP], float(P - 1), None, ALU.add))
                ch.link(nc.vector.tensor_scalar(size_i[:, :], size_i[:, :], 7, 7, ALU.logical_shift_right,
                                                ALU.logical_shift_left))
                nc.vector.memset(zeros[:, :], 0.0)
                ch.link(nc.vector.tensor_copy(size[:, :], size_i[:, :]))
                ch.link(nc.vector.tensor_tensor_scan(ends[:, :], size[:, :], zeros[:, :], 0.0, ALU.add, ALU.add))
                ch.link(nc.vector.tensor_tensor(starts[:, :], ends[:, :], size[:, :], ALU.subtract))
                ch.link(nc.vector.tensor_tensor(S.start[:, :], sums_ps[:, 0:NBP], starts[:, :], ALU.add))
                ch.link(nc.vector.scalar_tensor_tensor(size[:, :], S.start[:, :], -1.0, S.counts[:, :], ALU.add,
                                                       ALU.add))
                ch.link(nc.vector.tensor_scalar(S.last[:, :], size[:, :], 0.0, None, ALU.max))
                ch.link(nc.vector.tensor_scalar(live_i[:, :], S.start[:, :], float(G2 * P - 1), None, ALU.add))
                ch.link(nc.vector.tensor_scalar(live_i[:, :], live_i[:, :], (G2 * P).bit_length() - 1, None,
                                                ALU.logical_shift_right))
                ch.link(nc.vector.tensor_scalar(live_i[:, :], live_i[:, :], 1.0, None, ALU.max))
                dve.wait_ge(numbered, 3)
                ch.link(nc.vector.tensor_copy(chunk_f[:, :], chunk_i[:, :]))
                ch.link(nc.vector.tensor_tensor(past[:, :, :], bc(ends[:, 0:1], [0, g.tiles], [1, NBP]),
                                                bc(chunk_f[:, 0:1], [1, g.tiles], [0, NBP]), ALU.is_le))
                ch.link(nc.vector.tensor_reduce(blocks[:, :], past[:, :, 0:NB], AX, ALU.add))
                for k, width in enumerate((g.er, H, g.out if g is REL else PLACE)):
                    ins = nc.vector.tensor_scalar(places_i[:, k, :], blocks[:, :], float(NB - 1), float(width), ALU.min,
                                                  ALU.mult)
                ins.then_inc(numbers_ready, 1)

            @block.tensor
            def _(pe):
                nc.tensor.matmul(counts_ps[:, 0:NBP], C.zero_bf[:, :], C.zero_bf[:, 0:NBP], start=True, stop=False)

                def step(i):
                    for h in range(2):
                        pe.wait_ge(one, i * 2 + h + 1)
                        for u in range(U):
                            last = nc.tensor.matmul(counts_ps[:, 0:NBP], low[h][:, u, :], blk[h][:, u, :],
                                                    start=False, stop=False)
                        last.then_inc(used[h], 1)

                each_step(pe, steps, step)
                nc.tensor.matmul(counts_ps[:, 0:NBP], C.zero_bf[:, :], C.zero_bf[:, 0:NBP], start=False,
                                 stop=True).then_inc(counted, 1)
                pe.wait_ge(chain, 1)
                nc.tensor.matmul(sums_ps[:, 0:NBP], C.after[:, :], S.counts[:, :], start=True, stop=True)
                nc.tensor.matmul(sums_ps[:, NBP:2 * NBP], C.ones[:, :], S.counts[:, :], start=True,
                                 stop=True).then_inc(summed, 1)


def scatter_edges(nc, C, g, S):
    steps = g.raw // G2
    with stage(nc, g.name + "_") as (sb, ps, sem):
        low = [sb(f"se_low{h}", [P, U, P], BF16) for h in range(2)]
        blk = [sb(f"se_blk{h}", [P, U, NBP], BF16) for h in range(2)]
        low_t = [sb(f"se_low_t{h}", [P, U, P]) for h in range(2)]
        rows = [sb(f"se_rows{h}", [P, U, 2, P], U16) for h in range(2)]
        table = [sb(f"se_table{h}", [P, U + 1, NBP]) for h in range(2)]
        match = [sb(f"se_match{h}", [P, U, P], BF16) for h in range(2)]
        rank = [sb(f"se_rank{h}", [P, U]) for h in range(2)]
        pick = [sb(f"se_pick{h}", [P, U, NBP]) for h in range(2)]
        base = [sb(f"se_base{h}", [P, U]) for h in range(2)]
        slot = [sb(f"se_slot{h}", [P, U], I32) for h in range(2)]
        load = [sb(f"se_load{h}", [P, U], I32) for h in range(2)]
        grow = [ps(f"se_grow{h}", [P, 512]) for h in range(2)]
        look = [ps(f"se_look{h}", [P, 512]) for h in range(2)]
        rows_in = [sem(f"se_rows_in{h}") for h in range(2)]
        one = sem("se_onehot_ready")
        grown = sem("se_grown")
        tables = sem("se_table_ready")
        looked = sem("se_looked")
        picked = sem("se_picked")
        matched = sem("se_matched")
        slots = sem("se_slots_ready")
        chain = sem("se_chain")
        begun = sem("se_scatter_begun")
        sent = [sem(f"se_sent{h}") for h in range(2)]
        with nc.Block() as block:
            @block.sync
            def _(sp):
                def load_rows(i, h):
                    wait_before_reuse(sp, matched, i, 2, h - 1)
                    chunk = S.key_rows[bass.ds(i * G2 + h * U, U), :, :]
                    sp.dma_start(rows[h][:, :, :, :].rearrange("p u k e -> p (u k e)"),
                                 row_bcast(chunk.rearrange("u k e -> (u k e)"))).then_inc(rows_in[h], 16)

                def step(i):
                    load_rows(i, 0)
                    load_rows(i, 1)

                each_step(sp, steps, step)
                load_rows(steps, 0)
                sp.wait_ge(rows_in[0], 16 * (steps + 1))

            @block.vector
            def _(dve):
                ch0 = Chain(dve, chain)
                ch0.link(nc.vector.tensor_copy(table[0][:, 0, :], S.start[:, :]))

                def onehots(i, h):
                    at = i * G2 + h * U
                    onehot(nc, C, low[h][:, :, :], S.lo[:, bass.ds(at, 1)], P)
                    onehot(nc, C, blk[h][:, :, :], S.hi[:, bass.ds(at, 1)], NBP)
                    dve.wait_ge(rows_in[h], i * 16 + 16)
                    nc.vector.tensor_scalar(low_t[h][:, :, :], rows[h][:, :, 1, :], C.part[:, 0:1], None,
                                            ALU.is_equal).then_inc(one, 1)

                def matches(i, h):
                    for u in range(U):
                        ins = nc.vector.scalar_tensor_tensor(
                            match[h][:, u, :], rows[h][:, u, 0, :], S.key[:, bass.ds(i * G2 + h * U + u, 1)],
                            C.before[:, :], ALU.is_equal, ALU.mult, accum_out=rank[h][:, u:u + 1])
                    ins.then_inc(matched, 1)

                def step(i):
                    ch = Chain(dve, chain, i, 4, 1)
                    for h in range(2):
                        onehots(*ahead(i, h))
                        dve.wait_ge(grown, i * 2 + h + 1)
                        ch.link(nc.vector.tensor_tensor(
                            table[h][:, 1:, :], grow[h][:, 0:U * NBP].rearrange("p (u b) -> p u b", b=NBP),
                            bc(table[h][:, 0, 0:1], [0, U], [1, NBP]), ALU.add))
                        nc.vector.tensor_copy(table[1 - h][:, 0, :], table[h][:, U, :]).then_inc(tables, 1)
                        matches(*ahead(i, h))
                        dve.wait_ge(looked, i * 2 + h + 1)
                        nc.vector.tensor_tensor(
                            pick[h][:, :, :], look[h][:, 0:U * NBP].rearrange("p (u b) -> p u b", b=NBP),
                            blk[h][:, :, :], ALU.mult).then_inc(picked, 1)
                        dve.wait_ge(picked, i * 2 + h + 1)
                        ch.link(nc.vector.tensor_reduce(base[h][:, :], pick[h][:, :, :], AX, ALU.add))
                        wait_before_reuse(dve, sent[h], i, 16 * U)
                        dve.wait_ge(matched, i * 2 + h + 1)
                        nc.vector.tensor_tensor(slot[h][:, :], base[h][:, :], rank[h][:, :], ALU.add)
                        nc.vector.tensor_copy(load[h][:, :], S.packed[:, bass.ds(i * G2 + h * U, U)]).then_inc(slots, 1)
                    ch.end()

                onehots(0, 0)
                matches(0, 0)
                each_step(dve, steps, step)

            @block.tensor
            def _(pe):
                def count(i, h):
                    pe.wait_ge(one, i * 2 + h + 1)
                    for u in range(U):
                        last = nc.tensor.matmul(grow[h][:, u * NBP:U * NBP], low[h][:, u, :],
                                                bc(blk[h][:, u, 0:1], [0, U - u], [1, NBP]),
                                                start=(u == 0), stop=(u == U - 1))
                    last.then_inc(grown, 1)

                def step(i):
                    for h in range(2):
                        pe.wait_ge(tables, i * 2 + h + 1)
                        for u in range(U):
                            last = nc.tensor.matmul(look[h][:, u * NBP:(u + 1) * NBP], low_t[h][:, u, :],
                                                    table[h][:, u, :], start=True, stop=True)
                        last.then_inc(looked, 1)
                        if h == 0:
                            count(i, 1)
                        else:
                            count(i + 1, 0)

                count(0, 0)
                each_step(pe, steps, step)

            @block.gpsimd
            def _(pool):
                def step(i):
                    for h in range(2):
                        pool.wait_ge(slots, i * 2 + h + 1)
                        pool.sem_inc(begun, 1)
                        for u in range(U):
                            nc.gpsimd.indirect_dma_start(
                                S.sorted, bass.IndirectOffsetOnAxis(ap=slot[h][:, u:u + 1], axis=0),
                                load[h][:, u:u + 1], None).then_inc(sent[h], 16)

                each_step(pool, steps, step)
                for h in range(2):
                    pool.wait_ge(sent[h], steps * U * 16)


def read_slots(nc, C, g, S):
    T = g.tiles
    W = T * P
    with stage(nc, g.name + "_") as (sb, ps, sem):
        packed = sb("rs_packed", [P, W], I32)
        row_i = sb("rs_row_i", [P, W], I32)
        key_i = sb("rs_key_i", [P, W], I32)
        typ_i = sb("rs_typ_i", [P, W], I32)
        row_f = sb("rs_row", [P, W])
        low_f = sb("rs_low", [P, W])
        typ_f = sb("rs_typ", [P, W])
        low_u = sb("rs_low_u", [P, T, P], U16)
        turned = [ps(f"rs_turned{i}", [P, 512]) for i in range(6)]
        loaded = sem("rs_loaded")
        chain = sem("rs_chain")
        split = sem("rs_split")
        stored = sem("rs_stored")
        turn_done = sem("rs_turn_done")
        turn_used = sem("rs_turn_used")
        groups = turns(T, 3 if g is REL else 2)
        with nc.Block() as block:
            @block.sync
            def _(sp):
                sp.dma_start(packed[:, :].rearrange("p (t e) -> p t e", e=P),
                             S.sorted.rearrange("(t p e) o -> p t (e o)", p=P, e=P)).then_inc(loaded, 16)
                sp.wait_ge(split, 1)
                sp.dma_start(S.low_rows.rearrange("(t p) e -> p t e", p=P), low_u[:, :, :]).then_inc(stored, 16)
                sp.wait_ge(stored, 16)

            @block.vector
            def _(dve):
                ch = Chain(dve, chain)
                dve.wait_ge(loaded, 16)
                nc.vector.tensor_scalar(row_i[:, :], packed[:, :], 0x7fff, None, ALU.bitwise_and)
                ch.link(nc.vector.tensor_scalar(key_i[:, :], packed[:, :], 15, 255, ALU.logical_shift_right,
                                                ALU.bitwise_and))
                nc.vector.tensor_scalar(typ_i[:, :], row_i[:, :], g.rels - 1, None, ALU.bitwise_and)
                nc.vector.tensor_copy(row_f[:, :], row_i[:, :])
                nc.vector.tensor_copy(low_u[:, :, :], key_i[:, :].rearrange("p (t e) -> p t e", e=P))
                ch.link(nc.vector.tensor_copy(low_f[:, :], key_i[:, :]))
                nc.vector.tensor_copy(typ_f[:, :], typ_i[:, :]).then_inc(split, 1)
                for q, (k, t0, n) in enumerate(groups):
                    dve.wait_ge(turn_done, q + 1)
                    out = (S.slot_row, S.slot_low, S.slot_type)[k][:, t0 * P:(t0 + n) * P]
                    nc.vector.tensor_copy(out, turned[q % 6][:, 0:n * P]).then_inc(turn_used, 1)

            @block.tensor
            def _(pe):
                pe.wait_ge(split, 1)
                for q, (k, t0, n) in enumerate(groups):
                    if q >= 6:
                        pe.wait_ge(turn_used, q - 5)
                    for i in range(n):
                        last = nc.tensor.transpose(turned[q % 6][:, i * P:(i + 1) * P],
                                                   (row_f, low_f, typ_f)[k][:, (t0 + i) * P:(t0 + i + 1) * P],
                                                   C.ident[:, :])
                    last.then_inc(turn_done, 1)


def score_edges(nc, C, g, S):
    steps = g.slots // G2
    with stage(nc, g.name + "_") as (sb, ps, sem):
        index = [sb(f"sc_index{h}", [P, U], I32) for h in range(2)]
        got = [sb(f"sc_got{h}", [P, U, g.row]) for h in range(2)]
        rows = [sb(f"sc_rows{h}", [P, U, P], U16) for h in range(2)]
        low_t = [sb(f"sc_low_t{h}", [P, U, P]) for h in range(2)]
        type1 = [sb(f"sc_type{h}", [P, U, R]) for h in range(2)]
        pick = [sb(f"sc_pick{h}", [P, U, g.rels, H]) for h in range(2)]
        dest = [sb(f"sc_dest{h}", [P, U, H]) for h in range(2)]
        both = [sb(f"sc_sum{h}", [P, U, H]) for h in range(2)]
        score = [sb(f"sc_score{h}", [P, U * H]) for h in range(2)]
        turned = [sb(f"sc_turned{h}", [U * H, P]) for h in range(2)]
        look = [ps(f"sc_look{h}", [P, 512]) for h in range(2)]
        turn = [ps(f"sc_turn{h}", [P, 512]) for h in range(2)]
        index_ready = sem("sc_index_ready")
        begun = sem("sc_begun")
        gathered = [sem(f"sc_gathered{h}") for h in range(2)]
        got_used = sem("sc_got_used")
        rows_in = [sem(f"sc_rows_in{h}") for h in range(2)]
        low_ready = sem("sc_low_ready")
        looked = sem("sc_looked")
        chain = sem("sc_chain")
        scored = sem("sc_scored")
        turn_done = sem("sc_turn_done")
        kept = sem("sc_kept")
        turn_copied = sem("sc_turn_copied")
        stored = [sem(f"sc_stored{h}") for h in range(2)]
        ended = sem("sc_ended")
        with nc.Block() as block:
            @block.sync
            def _(sp):
                def load_rows(i, h):
                    sp.dma_start(rows[h][:, :, :].rearrange("p u e -> p (u e)"), row_bcast(
                        S.low_rows[bass.ds(i * G2 + h * U, U), :].rearrange("u e -> (u e)"))).then_inc(rows_in[h], 16)

                def step(i):
                    for h in range(2):
                        wait_before_reuse(sp, low_ready, i, 2, h - 1)
                        load_rows(i, h)

                live = live_steps(sp, S, steps)
                each_step(sp, steps, step, live)
                sp.wait_ge(low_ready, live * 2)
                load_rows(live, 0)
                sp.wait_ge(rows_in[0], live * 16 + 16)
                sp.sem_inc(ended, 1)

            @block.gpsimd
            def _(pool):
                def step(i):
                    for h in range(2):
                        pool.wait_ge(index_ready, i * 2 + h + 1)
                        pool.sem_inc(begun, 1)
                        for u in range(U):
                            nc.gpsimd.indirect_dma_start(
                                got[h][:, u, :], None, S.score_table,
                                bass.IndirectOffsetOnAxis(ap=index[h][:, u:u + 1], axis=0)).then_inc(gathered[h], 16)

                each_step(pool, steps, step, live_steps(pool, S, steps))

            @block.vector
            def _(dve):
                def next_index(i, h):
                    nc.vector.tensor_copy(index[h][:, :],
                                          S.slot_row[:, bass.ds(i * G2 + h * U, U)]).then_inc(index_ready, 1)

                def compare(i, h):
                    if g is REL:
                        onehot(nc, C, type1[h][:, :, :], S.slot_type[:, bass.ds(i * G2 + h * U, 1)], R)
                    dve.wait_ge(rows_in[h], i * 16 + 16)
                    nc.vector.tensor_scalar(low_t[h][:, :, :], rows[h][:, :, :], C.part[:, 0:1], None,
                                            ALU.is_equal).then_inc(low_ready, 1)

                def step(i):
                    ch = Chain(dve, chain, i, 4)
                    for h in range(2):
                        at = i * G2 + h * U
                        compare(*ahead(i, h))
                        dve.wait_ge(looked, i * 2 + h + 1)
                        found = look[h][:, 0:U * g.er]
                        if g is REL:
                            ch.link(nc.vector.tensor_tensor(
                                pick[h][:, :, :, :], found.rearrange("p (u r h) -> p u r h", r=R, h=H),
                                bc(type1[h][:, 0, 0:1], [R, U], [1, R], [0, H]), ALU.mult))
                            ch.link(nc.vector.tensor_reduce(
                                dest[h][:, :, :], pick[h][:, :, :, :].rearrange("p u r h -> p u h r"), AX, ALU.add))
                            found = dest[h][:, :, :]
                        else:
                            found = found.rearrange("p (u h) -> p u h", h=H)
                        dve.wait_ge(gathered[h], (i * 16 + 16) * U)
                        if g is ROUTE:
                            nc.vector.tensor_copy(S.kept[:, bass.ds(at, U), :], got[h][:, :, 0:g.feats])
                        nc.vector.tensor_tensor(both[h][:, :, :], found, got[h][:, :, g.row - H:g.row],
                                                ALU.add).then_inc(got_used, 1)
                        dve.wait_ge(got_used, i * 2 + h + 1)
                        next_index(i + 1, h)
                        wait_before_reuse(dve, turn_done, i, 2, h - 1)
                        wait_before_reuse(dve, kept, i, 2, h - 1)
                        nc.vector.scalar_tensor_tensor(
                            score[h][:, :], both[h][:, :, :].rearrange("p u h -> p (u h)"), SLOPE,
                            both[h][:, :, :].rearrange("p u h -> p (u h)"), ALU.mult, ALU.max).then_inc(scored, 1)
                    if g is REL:
                        ch.end()

                next_index(0, 0)
                next_index(0, 1)
                compare(0, 0)
                each_step(dve, steps, step, live_steps(dve, S, steps))

            @block.tensor
            def _(pe):
                def look_up(i, h):
                    at = places(pe, S, 0, i * G2 + h * U, g.er)
                    pe.wait_ge(low_ready, i * 2 + h + 1)
                    for u in range(U):
                        last = nc.tensor.matmul(look[h][:, u * g.er:(u + 1) * g.er], low_t[h][:, u, :],
                                                S.dest_table[:, bass.ds(at[u], g.er)], start=True, stop=True)
                    last.then_inc(looked, 1)

                def step(i):
                    for h in range(2):
                        look_up(*ahead(i, h))
                        pe.wait_ge(scored, i * 2 + h + 1)
                        wait_before_reuse(pe, turn_copied, i, 2, h - 1)
                        nc.tensor.transpose(turn[h][0:U * H, 0:P], score[h][:, :], C.ident[:, :]).then_inc(turn_done, 1)

                look_up(0, 0)
                each_step(pe, steps, step, live_steps(pe, S, steps))

            @block.scalar
            def _(act):
                def step(i):
                    for h in range(2):
                        at = i * G2 + h * U
                        act.wait_ge(scored, i * 2 + h + 1)
                        nc.scalar.copy(S.score[:, bass.ds(at * H, U * H)], score[h][:, :]).then_inc(kept, 1)
                        act.wait_ge(turn_done, i * 2 + h + 1)
                        wait_before_reuse(act, stored[h], i, 16)
                        nc.scalar.copy(turned[h][:, :], turn[h][0:U * H, 0:P]).then_inc(turn_copied, 1)
                        act.wait_ge(turn_copied, i * 2 + h + 1)
                        act.dma_start(S.score_rows[bass.ds(at, U), :, :].rearrange("u h e -> (u h) e"),
                                      turned[h][:, :]).then_inc(stored[h], 16)

                live = live_steps(act, S, steps)
                each_step(act, steps, step, live)
                for h in range(2):
                    act.wait_ge(stored[h], live * 16)
                    act.sem_inc(ended, 1)


def node_maxima(nc, C, g, S):
    T, L = g.tiles, g.lane
    full, part = divmod(g.slots, T)
    with stage(nc, g.name + "_") as (sb, ps, sem):
        packed = sb("nm_packed", [P, L], I32)
        key = sb("nm_key", [P, L])
        fresh = sb("nm_fresh", [P, L])
        score = sb("nm_score", [P, H, L])
        peak = sb("nm_peak", [P, L, H])
        ends = sb("nm_ends", [P, H + 1])
        diag = sb("nm_diag", [P, H + 1, P])
        same = sb("nm_same", [P, P])
        reach = sb("nm_reach", [P, H, P])
        carry = sb("nm_carry", [P, H])
        index = sb("nm_index", [P, NBP], I32)
        across = [ps(f"nm_across{i}", [P, 512]) for i in range(2)]
        cleared = sem("nm_cleared")
        loaded = sem("nm_loaded")
        chain = sem("nm_chain")
        diag_ready = sem("nm_diag_ready")
        spread = sem("nm_spread")
        peaks = sem("nm_peaks_ready")
        stored = sem("nm_stored")
        gathered = sem("nm_gathered")
        with nc.Block() as block:
            @block.gpsimd
            def _(pool):
                nc.gpsimd.memset(score[:, :, :], 0.0).then_inc(cleared, 1)
                pool.wait_ge(stored, 16)
                for b in range(NB):
                    nc.gpsimd.indirect_dma_start(
                        S.peak[:, b * H:(b + 1) * H], None, S.peak_table,
                        bass.IndirectOffsetOnAxis(ap=S.last[:, b:b + 1], axis=0)).then_inc(gathered, 16)
                pool.wait_ge(gathered, NB * 16)

            @block.sync
            def _(sp):
                sp.dma_start(packed[:, :], S.sorted.rearrange("(p l) o -> p (l o)", p=P)).then_inc(loaded, 16)
                sp.wait_ge(cleared, 1)
                for h in range(H):
                    sp.dma_start(score[0:full, h, :].rearrange("p (t e) -> p t e", e=P),
                                 S.score_rows[0:full * T, h, :].rearrange("(p t) e -> p t e", t=T)).then_inc(loaded, 16)
                    if part:
                        sp.dma_start(score[full:full + 1, h, 0:part * P].rearrange("p (t e) -> p t e", e=P),
                                     S.score_rows[full * T:g.slots, h, :].rearrange(
                                         "(p t) e -> p t e", p=1)).then_inc(loaded, 16)
                sp.wait_ge(peaks, 1)
                sp.dma_start(S.peak_table.rearrange("(p l) h -> p (l h)", p=P),
                             peak[:, :, :].rearrange("p l h -> p (l h)")).then_inc(stored, 16)

            @block.vector
            def _(dve):
                ch = Chain(dve, chain)
                dve.wait_ge(loaded, 16 * (1 + H * (2 if part else 1)))
                ch.link(nc.vector.tensor_scalar(packed[:, :], packed[:, :], 15, None, ALU.logical_shift_right))
                ch.link(nc.vector.tensor_copy(key[:, :], packed[:, :]))
                ch.link(nc.vector.tensor_tensor(fresh[:, 1:L], key[:, 1:L], key[:, 0:L - 1], ALU.is_equal))
                ch.link(nc.vector.memset(fresh[:, 0:1], 0.0))
                ch.link(nc.vector.tensor_scalar(fresh[:, :], fresh[:, :], 1.0, BIG, ALU.subtract, ALU.mult))
                for h in range(H):
                    ins = nc.vector.tensor_tensor_scan(peak[:, :, h], fresh[:, :], score[:, h, :], -BIG, ALU.add,
                                                       ALU.max)
                ch.link(ins)
                nc.vector.tensor_copy(ends[:, H:H + 1], key[:, L - 1:L])
                ch.link(nc.vector.tensor_copy(ends[:, 0:H], peak[:, L - 1, :]))
                nc.vector.tensor_tensor(diag[:, :, :], bc(ends[:, 0:1], [1, H + 1], [0, P]),
                                        bc(C.ident[:, 0:1], [0, H + 1], [1, P]), ALU.mult).then_inc(diag_ready, 1)
                dve.wait_ge(spread, 1)
                ch.link(nc.vector.scalar_tensor_tensor(same[:, :], across[1][:, 0:P], key[:, 0:1], C.before[:, :],
                                                       ALU.is_equal, ALU.mult))
                ch.link(nc.vector.tensor_scalar(same[:, :], same[:, :], 1.0, BIG, ALU.subtract, ALU.mult))
                ch.link(nc.vector.tensor_tensor(reach[:, :, :], across[0][:, :].rearrange("p (h q) -> p h q", h=H),
                                                bc(same[:, 0:1], [0, H], [1, P]), ALU.add))
                ch.link(nc.vector.memset(fresh[:, 0:1], 0.0))
                ch.link(nc.vector.tensor_reduce(carry[:, :], reach[:, :, :], AX, ALU.max))
                for h in range(H):
                    ins = nc.vector.tensor_tensor_scan(peak[:, :, h], fresh[:, :], score[:, h, :],
                                                       carry[:, h:h + 1], ALU.add, ALU.max)
                ins.then_inc(peaks, 1)

            @block.tensor
            def _(pe):
                pe.wait_ge(diag_ready, 1)
                nc.tensor.matmul(across[0][:, :], C.ones[:, :], diag[:, 0:H, :].rearrange("p h q -> p (h q)"),
                                 start=True, stop=True)
                nc.tensor.matmul(across[1][:, 0:P], C.ones[:, :], diag[:, H, :], start=True,
                                 stop=True).then_inc(spread, 1)


def sum_edges(nc, C, g, S):
    steps = g.slots // G2
    hd = g.feats // H
    own = 4 if g is REL else U
    banks = 6
    with stage(nc, g.name + "_") as (sb, ps, sem):
        index = [sb(f"su_index{h}", [P, U], I32) for h in range(2)]
        got = [sb(f"su_got{h}", [P, U, g.feats]) for h in range(2)] if g is REL else None
        rows = [sb(f"su_rows{h}", [P, U, P], U16) for h in range(2)]
        low_t = [sb(f"su_low_t{h}", [P, U, P]) for h in range(2)]
        low = [sb(f"su_low{h}", [P, U, P]) for h in range(2)]
        under = [sb(f"su_under{h}", [P, U * H]) for h in range(2)]
        weight = [sb(f"su_weight{h}", [P, U, H]) for h in range(2)]
        terms = [sb(f"su_terms{h}", [P, U, g.out]) for h in range(2)]
        none = sb("su_none", [P, U * H])
        look = [ps(f"su_look{h}", [P, 512]) for h in range(2)]
        if g is REL:
            total = [ps(f"su_total{b}", [P, 512]) for b in range(banks)]
        else:
            all_sums = ps("su_all", [P, 1024])
        index_ready = sem("su_index_ready")
        begun = sem("su_begun")
        gathered = [sem(f"su_gathered{h}") for h in range(2)]
        rows_in = [sem(f"su_rows_in{h}") for h in range(2)]
        low_t_ready = sem("su_low_t_ready")
        low_ready = sem("su_low_ready")
        looked = sem("su_looked")
        chain = sem("su_chain")
        lowered = sem("su_lowered")
        weighed = sem("su_weighed")
        weights_ready = sem("su_weights_ready")
        dve_ready = sem("su_dve_terms_ready")
        act_ready = sem("su_act_terms_ready")
        totalled = sem("su_totalled")
        added = sem("su_added")
        cleared = sem("su_cleared")
        ended = sem("su_ended")
        with nc.Block() as block:
            @block.sync
            def _(sp):
                def load_rows(i, h):
                    wait_before_reuse(sp, low_t_ready, i, 2, h - 1)
                    sp.dma_start(rows[h][:, :, :].rearrange("p u e -> p (u e)"), row_bcast(
                        S.low_rows[bass.ds(i * G2 + h * U, U), :].rearrange("u e -> (u e)"))).then_inc(rows_in[h], 16)

                def step(i):
                    load_rows(i, 0)
                    load_rows(i, 1)

                live = live_steps(sp, S, steps)
                each_step(sp, steps + 1, step, live + 1)
                for h in range(2):
                    sp.wait_ge(rows_in[h], live * 16 + 16)
                    sp.sem_inc(ended, 1)

            def compare_rows(i, h, eng):
                eng.wait_ge(rows_in[h], i * 16 + 16)
                if g is ROUTE:
                    eng.sem_inc(begun, 1)
                tensor = nc.vector if g is REL else nc.gpsimd
                return tensor.tensor_scalar(low_t[h][:, :, :], rows[h][:, :, :], C.part[:, 0:1], None, ALU.is_equal)

            @block.gpsimd
            def _(pool):
                def gather(i):
                    for h in range(2):
                        wait_before_reuse(pool, act_ready, i, 2, h - 1)
                        pool.sem_inc(begun, 1)
                        pool.wait_ge(index_ready, i * 2 + h + 1)
                        pool.sem_inc(begun, 1)
                        for u in range(U):
                            nc.gpsimd.indirect_dma_start(
                                got[h][:, u, :], None, S.feature_table,
                                bass.IndirectOffsetOnAxis(ap=index[h][:, u:u + 1], axis=0)).then_inc(gathered[h], 16)

                def compare(i):
                    for h in range(2):
                        wait_before_reuse(pool, looked, i, 2, h - 1)
                        pool.sem_inc(begun, 1)
                        compare_rows(i, h, pool).then_inc(low_t_ready, 1)

                if g is REL:
                    nc.gpsimd.memset(S.sums[:, :], 0.0).then_inc(cleared, 1)
                    each_step(pool, steps, gather, live_steps(pool, S, steps))
                else:
                    each_step(pool, steps + 1, compare, live_steps(pool, S, steps) + 1)

            @block.vector
            def _(dve):
                def next_index(i, h):
                    nc.vector.tensor_copy(index[h][:, :],
                                          S.slot_row[:, bass.ds(i * G2 + h * U, U)]).then_inc(index_ready, 1)

                def compare_low(i, h, first, n):
                    return nc.vector.tensor_tensor(
                        low[h][:, first:first + n, :], bc(S.slot_low[:, bass.ds(i * G2 + h * U + first, 1)], [1, n], [0, P]),
                        bc(C.count[:, 0:1], [0, n], [1, P]), ALU.is_equal)

                def lower(i, h, ch):
                    at = i * G2 + h * U
                    dve.wait_ge(looked, i * 2 + h + 1)
                    ch.link(nc.vector.tensor_tensor(under[h][:, :], S.score[:, bass.ds(at * H, U * H)],
                                                    look[h][:, 0:U * H], ALU.subtract))
                    nc.vector.tensor_scalar(under[h][:, :], under[h][:, :], 0.0, None, ALU.min).then_inc(lowered, 1)

                def weigh(i, h):
                    if g is REL:
                        dve.wait_ge(gathered[h], (i * 16 + 16) * U)
                        feats = got[h][:, 0:own, :]
                    else:
                        feats = S.kept[:, bass.ds(i * G2 + h * U, U), :]
                    dve.wait_ge(weighed, i * 2 + h + 1)
                    nc.vector.tensor_tensor(
                        terms[h][:, 0:own, 0:g.feats].rearrange("p u (h d) -> p u h d", h=H),
                        feats.rearrange("p u (h d) -> p u h d", h=H),
                        bc(weight[h][:, 0, 0:1], [H, own], [1, H], [0, hd]), ALU.mult).then_inc(dve_ready, 1)

                def add_total(i, h, u, place):
                    n = h * U + u
                    dve.wait_ge(totalled, i * G2 + n + 1)
                    if not (isinstance(i, int) and n == 0):
                        dve.wait_ge(added, i * G2 + n)
                    sums = S.sums[:, bass.ds(place, g.out)]
                    nc.vector.tensor_tensor(sums, sums, total[n % banks][:, 0:g.out], ALU.add).then_inc(added, 1)

                def step(i):
                    ch = Chain(dve, chain, i, 2, 3)
                    for h in range(2):
                        weigh(i, h)
                        nxt = ahead(i, h)
                        lower(*nxt, ch)
                        if g is REL:
                            next_index(i + 1, h)
                            at = places(dve, S, 2, i * G2 + h * U, g.out)
                            for u in range(U):
                                if u == 3:
                                    compare_rows(i + 1, h, dve).then_inc(low_t_ready, 1)
                                if u % 2:
                                    ins = compare_low(*nxt, u - 1, 2)
                                if u == U - 1:
                                    ins.then_inc(low_ready, 1)
                                add_total(i, h, u, at[u])
                        else:
                            wait_before_reuse(dve, totalled, nxt[0], 2, nxt[1] - 1)
                            compare_low(*nxt, 0, U).then_inc(low_ready, 1)
                    ch.end()

                first = Chain(dve, chain)
                live = live_steps(dve, S, steps)
                first.link(nc.vector.memset(none[:, :], 0.0))
                first.link(nc.vector.tensor_copy(S.score[:, bass.ds(live * (G2 * H), U * H)], none[:, :]))
                if g is REL:
                    dve.wait_ge(cleared, 1)
                    next_index(0, 0)
                    next_index(0, 1)
                    compare_rows(0, 0, dve).then_inc(low_t_ready, 1)
                    compare_rows(0, 1, dve).then_inc(low_t_ready, 1)
                compare_low(0, 0, 0, U).then_inc(low_ready, 1)
                lower(0, 0, first)
                each_step(dve, steps, step, live)
                if g is ROUTE:
                    dve.wait_ge(totalled, live * 2 + 1)
                    nc.vector.tensor_copy(
                        S.sums[:, :].rearrange("p (b c) -> p b c", b=NB),
                        all_sums[:, :].rearrange("p (b c) -> p b c", c=PLACE)[:, 0:NB, 0:g.out])

            @block.tensor
            def _(pe):
                def look_up(i, h):
                    at = places(pe, S, 1, i * G2 + h * U, H)
                    pe.wait_ge(low_t_ready, i * 2 + h + 1)
                    for u in range(U):
                        last = nc.tensor.matmul(look[h][:, u * H:(u + 1) * H], low_t[h][:, u, :],
                                                S.peak[:, bass.ds(at[u], H)], start=True, stop=True)
                    last.then_inc(looked, 1)

                def step(i):
                    for h in range(2):
                        look_up(*ahead(i, h))
                        if g is ROUTE:
                            at = places(pe, S, 2, i * G2 + h * U, PLACE)
                        pe.wait_ge(low_ready, i * 2 + h + 1)
                        pe.wait_ge(dve_ready, i * 2 + h + 1)
                        pe.wait_ge(weights_ready, i * 2 + h + 1)
                        for u in range(U):
                            n = h * U + u
                            if u == own:
                                pe.wait_ge(act_ready, i * 2 + h + 1)
                            if g is REL:
                                if not (isinstance(i, int) and n < banks):
                                    pe.wait_ge(added, i * G2 + n - banks + 1)
                                nc.tensor.matmul(total[n % banks][:, 0:g.out], low[h][:, u, :], terms[h][:, u, :],
                                                 start=True, stop=True).then_inc(totalled, 1)
                            else:
                                last = nc.tensor.matmul(all_sums[:, bass.ds(at[u], g.out)], low[h][:, u, :],
                                                        terms[h][:, u, :], start=False, stop=False)
                        if g is ROUTE:
                            last.then_inc(totalled, 1)

                if g is ROUTE:
                    for b in range(2):
                        nc.tensor.matmul(all_sums[:, b * 512:(b + 1) * 512], C.zero_bf[:, :], C.zero_wide[:, :],
                                         start=True, stop=False)
                look_up(0, 0)
                each_step(pe, steps, step, live_steps(pe, S, steps))
                if g is ROUTE:
                    for b in range(2):
                        last = nc.tensor.matmul(all_sums[:, b * 512:(b + 1) * 512], C.zero_bf[:, :],
                                                C.zero_wide[:, :], start=False, stop=True)
                    last.then_inc(totalled, 1)

            @block.scalar
            def _(act):
                def step(i):
                    for h in range(2):
                        act.wait_ge(lowered, i * 2 + h + 1)
                        nc.scalar.activation(weight[h][:, :, :].rearrange("p u h -> p (u h)"), under[h][:, :],
                                             ACT.Exp).then_inc(weighed, 1)
                        act.wait_ge(weighed, i * 2 + h + 1)
                        if g is REL:
                            wait_before_reuse(act, totalled, i, G2, h * U - U)
                        else:
                            wait_before_reuse(act, totalled, i, 2, h - 1)
                        nc.scalar.copy(terms[h][:, :, g.feats:g.out], weight[h][:, :, :]).then_inc(weights_ready, 1)
                        if g is REL:
                            act.wait_ge(gathered[h], (i * 16 + 16) * U)
                        for u in range(own, U):
                            for k in range(H):
                                ins = nc.scalar.activation(terms[h][:, u, k * hd:(k + 1) * hd],
                                                           got[h][:, u, k * hd:(k + 1) * hd], ACT.Copy,
                                                           scale=weight[h][:, u, k:k + 1])
                        if g is REL:
                            ins.then_inc(act_ready, 1)

                each_step(act, steps, step, live_steps(act, S, steps))


PLACE = 32


def normalise(nc, C, S, name):
    with stage(nc) as (sb, ps, sem):
        square = sb(f"{name}_square", [P, NB, D])
        mean = sb(f"{name}_mean", [P, NB])
        var = sb(f"{name}_var", [P, NB])
        std = sb(f"{name}_std", [P, NB])
        chain = sem(f"{name}_chain")
        var_ready = sem(f"{name}_var_ready")
        std_ready = sem(f"{name}_std_ready")
        with nc.Block() as block:
            @block.vector
            def _(dve):
                ch = Chain(dve, chain)
                ch.link(nc.vector.tensor_reduce(mean[:, :], S.x[:, :, :], AX, ALU.add))
                ch.link(nc.vector.tensor_scalar(mean[:, :], mean[:, :], 1.0 / D, None, ALU.mult))
                ch.link(nc.vector.tensor_tensor(S.normed[:, :, :], S.x[:, :, :], bc(mean[:, 0:1], [1, NB], [0, D]),
                                                ALU.subtract))
                ch.link(nc.vector.tensor_tensor(square[:, :, :], S.normed[:, :, :], S.normed[:, :, :], ALU.mult))
                ch.link(nc.vector.tensor_reduce(var[:, :], square[:, :, :], AX, ALU.add))
                nc.vector.tensor_scalar(var[:, :], var[:, :], 1.0 / D, EPS, ALU.mult, ALU.add).then_inc(var_ready, 1)
                dve.wait_ge(std_ready, 1)
                ch.link(nc.vector.reciprocal(var[:, :], std[:, :]))
                ch.link(nc.vector.tensor_tensor(S.normed[:, :, :], S.normed[:, :, :], bc(var[:, 0:1], [1, NB], [0, D]),
                                                ALU.mult))

            @block.scalar
            def _(act):
                act.wait_ge(var_ready, 1)
                nc.scalar.activation(std[:, :], var[:, :], ACT.Sqrt).then_inc(std_ready, 1)


def load_nodes(nc, S, x_in):
    last = N - (NB - 1) * P
    with stage(nc) as (_, _, sem):
        cleared = sem("ln_cleared")
        loaded = sem("ln_loaded")
        with nc.Block() as block:
            @block.gpsimd
            def _(pool):
                nc.gpsimd.memset(S.x[:, NB - 1, :], 0.0).then_inc(cleared, 1)

            @block.sync
            def _(sp):
                sp.dma_start(S.x[:, 0:NB - 1, :],
                             x_in[0:(NB - 1) * P, :].rearrange("(t p) d -> p t d", p=P)).then_inc(loaded, 16)
                sp.wait_ge(cleared, 1)
                sp.dma_start(S.x[0:last, NB - 1, :], x_in[(NB - 1) * P:N, :]).then_inc(loaded, 16)
                sp.wait_ge(loaded, 32)


def relation_features(nc, C, S, w_in, left_in, right_in):
    RH = R * H
    with stage(nc) as (sb, ps, sem):
        w = sb("rf_w", [P, KC, R, H, HD])
        att = [sb(f"rf_att{s}", [P, R * D]) for s in range(2)]
        prod = sb("rf_prod", [P, KC, R * D])
        w_att = sb("rf_w_att", [P, KC, 2 * RH])
        tile = [sb(f"rf_tile{h}", [P, D]) for h in range(2)]
        turned = [sb(f"rf_turned{h}", [P, KC, P]) for h in range(2)]
        feats = [sb(f"rf_feats{h}", [P, R * D]) for h in range(2)]
        parts = [sb(f"rf_parts{h}", [P, RH]) for h in range(2)]
        turn = ps("rf_turn", [P, 512])
        banks = [ps(f"rf_bank{q}", [P, 512]) for q in range(4)]
        part = ps("rf_part", [P, 512])
        loaded = sem("rf_loaded")
        chain = sem("rf_chain")
        w_ready = sem("rf_w_ready")
        tile_ready = sem("rf_tile_ready")
        turn_done = sem("rf_turn_done")
        turn_copied = sem("rf_turn_copied")
        bank_done = sem("rf_bank_done")
        act_copied = sem("rf_act_copied")
        dve_copied = sem("rf_dve_copied")
        part_copied = sem("rf_part_copied")
        part_kept = sem("rf_part_kept")
        stored = [sem(f"rf_stored{h}") for h in range(2)]
        n_loads = KC + 2
        with nc.Block() as block:
            @block.sync
            def _(sp):
                for kc in range(KC):
                    sp.dma_start(w[:, kc, :, :, :].rearrange("p r h d -> p (r h) d"),
                                 w_in[:, :, kc * P:(kc + 1) * P, :].rearrange(
                                     "r h k d -> k (r h) d")).then_inc(loaded, 16)
                for s, a in enumerate((left_in, right_in)):
                    sp.dma_start(att[s][:, :], row_bcast(a.rearrange("r h d -> (r h d)"))).then_inc(loaded, 16)

                def step(i):
                    for h in range(2):
                        t = i * 2 + h
                        sp.wait_ge(act_copied, i * 4 + 2 * h + 2)
                        sp.wait_ge(dve_copied, i * 4 + 2 * h + 2)
                        sp.dma_start(S.feature_table[bass.ds(t * P * R, P * R), :].rearrange("(p r) d -> p (r d)", r=R),
                                     feats[h][:, :]).then_inc(stored[h], 16)
                        sp.wait_ge(part_copied, i * 2 + h + 1)
                        sp.dma_start(S.score_table[bass.ds(t * P * R, P * R), :].rearrange("(p r) h -> p (r h)", r=R),
                                     parts[h][:, :]).then_inc(stored[h], 16)

                each_step(sp, NB // 2, step)
                for h in range(2):
                    sp.wait_ge(stored[h], NB // 2 * 32)

            @block.gpsimd
            def _(pool):
                def step(i):
                    for h in range(2):
                        wait_before_reuse(pool, turn_done, i, 2, h - 1)
                        nc.gpsimd.tensor_copy(tile[h][:, :], S.normed[:, bass.ds(i * 2 + h, 1), :].rearrange(
                            "p t d -> p (t d)")).then_inc(tile_ready, 1)

                each_step(pool, NB // 2, step)

            @block.tensor
            def _(pe):
                pe.wait_ge(w_ready, 1)

                def step(i):
                    for h in range(2):
                        t = i * 2 + h
                        if not isinstance(t, int) or t:
                            pe.wait_ge(turn_copied, i * 2 + h)
                        pe.wait_ge(tile_ready, i * 2 + h + 1)
                        for kc in range(KC):
                            last = nc.tensor.transpose(turn[:, kc * P:(kc + 1) * P], tile[h][:, kc * P:(kc + 1) * P],
                                                       C.ident[:, :])
                        last.then_inc(turn_done, 1)
                        pe.wait_ge(turn_copied, i * 2 + h + 1)
                        for q in range(5):
                            if not isinstance(t, int) or t:
                                used, n = ((act_copied, 2), (dve_copied, 2), (part_kept, 1))[q // 2]
                                pe.wait_ge(used, i * 2 * n + n * h + (q % 2 + 1 - n if q < 4 else 0))
                            out = banks[q][:, :] if q < 4 else part[:, 0:2 * RH]
                            for kc in range(KC):
                                rhs = (w[:, kc, 2 * q:2 * q + 2, :, :].rearrange("p r h d -> p (r h d)") if q < 4
                                       else w_att[:, kc, :])
                                last = nc.tensor.matmul(out, turned[h][:, kc, :], rhs, start=(kc == 0),
                                                        stop=(kc == KC - 1))
                            last.then_inc(bank_done, 1)

                each_step(pe, NB // 2, step)

            @block.scalar
            def _(act):
                def step(i):
                    for h in range(2):
                        act.wait_ge(turn_done, i * 2 + h + 1)
                        nc.scalar.copy(turned[h][:, :, :].rearrange("p k n -> p (k n)"),
                                       turn[:, 0:KC * P]).then_inc(turn_copied, 1)
                        wait_before_reuse(act, stored[h], i, 32)
                        for q in range(2):
                            act.wait_ge(bank_done, i * 10 + 5 * h + q + 1)
                            nc.scalar.copy(feats[h][:, q * 512:(q + 1) * 512], banks[q][:, :]).then_inc(act_copied, 1)

                each_step(act, NB // 2, step)

            @block.vector
            def _(dve):
                ch = Chain(dve, chain)
                dve.wait_ge(loaded, 16 * n_loads)
                for s in range(2):
                    ch.link(nc.vector.tensor_tensor(prod[:, :, :], w[:, :, :, :, :].rearrange("p k r h d -> p k (r h d)"),
                                                    bc(att[s][:, 0:1], [0, KC], [1, R * D]), ALU.mult))
                    ch.link(nc.vector.tensor_reduce(w_att[:, :, s * RH:(s + 1) * RH],
                                                    prod[:, :, :].rearrange("p k (g d) -> p k g d", d=HD), AX, ALU.add))
                nc.vector.tensor_copy(parts[0][:, 0:1], w_att[:, 0, 0:1]).then_inc(w_ready, 1)

                def step(i):
                    for h in range(2):
                        wait_before_reuse(dve, stored[h], i, 32)
                        for q in range(2, 4):
                            dve.wait_ge(bank_done, i * 10 + 5 * h + q + 1)
                            nc.vector.tensor_copy(feats[h][:, q * 512:(q + 1) * 512],
                                                  banks[q][:, :]).then_inc(dve_copied, 1)
                        dve.wait_ge(bank_done, i * 10 + 5 * h + 5)
                        nc.vector.tensor_copy(parts[h][:, :], part[:, 0:RH]).then_inc(part_copied, 1)
                        nc.vector.tensor_copy(S.dest_table[:, bass.ds((i * 2 + h) * RH, RH)],
                                              part[:, RH:2 * RH]).then_inc(part_kept, 1)

                each_step(dve, NB // 2, step)


def add_attention(nc, C, S, bias_in):
    with stage(nc) as (sb, ps, sem):
        bias = sb("aa_bias", [P, D])
        inverse = sb("aa_inverse", [P, NB, H])
        loaded = sem("aa_loaded")
        chain = sem("aa_chain")
        with nc.Block() as block:
            @block.sync
            def _(sp):
                sp.dma_start(bias[:, :], row_bcast(bias_in)).then_inc(loaded, 16)

            @block.vector
            def _(dve):
                ch = Chain(dve, chain)
                sums = S.sums[:, :].rearrange("p (b c) -> p b c", b=NB)
                ch.link(nc.vector.tensor_scalar(inverse[:, :, :], sums[:, :, D:D + H], 0.5, None, ALU.max))
                ch.link(nc.vector.reciprocal(inverse[:, :, :], inverse[:, :, :]))
                heads = sums[:, :, 0:D].rearrange("p b (h d) -> p b h d", h=H)
                ch.link(nc.vector.tensor_tensor(heads, heads, bc(inverse[:, 0, 0:1], [H, NB], [1, H], [0, HD]), ALU.mult))
                dve.wait_ge(loaded, 16)
                ch.link(nc.vector.tensor_tensor(sums[:, :, 0:D], sums[:, :, 0:D], bc(bias[:, 0:1], [0, NB], [1, D]),
                                                ALU.add))
                ch.link(nc.vector.tensor_tensor(S.x[:, :, :], S.x[:, :, :], sums[:, :, 0:D], ALU.add))


def routing_features(nc, C, S, w_in, src_in, dst_in):
    XH = X * H
    WIDTH = XH + 2 * H
    with stage(nc) as (sb, ps, sem):
        w = sb("gf_w", [P, KC, WIDTH])
        att = sb("gf_att", [P, 2, XH])
        prod = sb("gf_prod", [P, KC, XH])
        tile = [sb(f"gf_tile{h}", [P, D]) for h in range(2)]
        turned = [sb(f"gf_turned{h}", [P, KC, P]) for h in range(2)]
        feats = [sb(f"gf_feats{h}", [P, XH + H]) for h in range(2)]
        turn = [ps(f"gf_turn{h}", [P, 512]) for h in range(2)]
        out = [ps(f"gf_out{h}", [P, 512]) for h in range(2)]
        loaded = sem("gf_loaded")
        chain = sem("gf_chain")
        w_ready = sem("gf_w_ready")
        tile_ready = sem("gf_tile_ready")
        turn_done = sem("gf_turn_done")
        turn_copied = sem("gf_turn_copied")
        out_done = sem("gf_out_done")
        copied = sem("gf_copied")
        kept = sem("gf_kept")
        stored = [sem(f"gf_stored{h}") for h in range(2)]
        with nc.Block() as block:
            @block.sync
            def _(sp):
                sp.dma_start(w[:, :, 0:XH], w_in.rearrange("(k p) c -> p k c", p=P)).then_inc(loaded, 16)
                for s, a in enumerate((src_in, dst_in)):
                    sp.dma_start(att[:, s, :], row_bcast(a.rearrange("h x -> (h x)"))).then_inc(loaded, 16)

                def step(i):
                    for h in range(2):
                        sp.wait_ge(copied, i * 2 + h + 1)
                        sp.dma_start(S.score_table[bass.ds((i * 2 + h) * P, P), :], feats[h][:, :]).then_inc(stored[h], 16)

                each_step(sp, NB // 2, step)
                for h in range(2):
                    sp.wait_ge(stored[h], NB // 2 * 16)

            @block.gpsimd
            def _(pool):
                def step(i):
                    for h in range(2):
                        wait_before_reuse(pool, turn_done, i, 2, h - 1)
                        nc.gpsimd.tensor_copy(tile[h][:, :], S.normed[:, bass.ds(i * 2 + h, 1), :].rearrange(
                            "p t d -> p (t d)")).then_inc(tile_ready, 1)

                each_step(pool, NB // 2, step)

            @block.tensor
            def _(pe):
                pe.wait_ge(w_ready, 1)

                def step(i):
                    for h in range(2):
                        wait_before_reuse(pe, turn_copied, i, 2, h - 1)
                        pe.wait_ge(tile_ready, i * 2 + h + 1)
                        for kc in range(KC):
                            last = nc.tensor.transpose(turn[h][:, kc * P:(kc + 1) * P],
                                                       tile[h][:, kc * P:(kc + 1) * P], C.ident[:, :])
                        last.then_inc(turn_done, 1)
                        pe.wait_ge(turn_copied, i * 2 + h + 1)
                        wait_before_reuse(pe, kept, i, 2, h - 1)
                        for kc in range(KC):
                            last = nc.tensor.matmul(out[h][:, 0:WIDTH], turned[h][:, kc, :], w[:, kc, :],
                                                    start=(kc == 0), stop=(kc == KC - 1))
                        last.then_inc(out_done, 1)

                each_step(pe, NB // 2, step)

            @block.scalar
            def _(act):
                def step(i):
                    for h in range(2):
                        act.wait_ge(turn_done, i * 2 + h + 1)
                        nc.scalar.copy(turned[h][:, :, :].rearrange("p k n -> p (k n)"),
                                       turn[h][:, 0:KC * P]).then_inc(turn_copied, 1)

                each_step(act, NB // 2, step)

            @block.vector
            def _(dve):
                ch = Chain(dve, chain)
                dve.wait_ge(loaded, 48)
                for s in range(2):
                    ch.link(nc.vector.tensor_tensor(prod[:, :, :], w[:, :, 0:XH], bc(att[:, s, 0:1], [0, KC], [1, XH]),
                                                    ALU.mult))
                    ch.link(nc.vector.tensor_reduce(w[:, :, XH + s * H:XH + (s + 1) * H],
                                                    prod[:, :, :].rearrange("p k (h x) -> p k h x", x=X), AX, ALU.add))
                nc.vector.tensor_copy(prod[:, 0, 0:1], w[:, 0, 0:1]).then_inc(w_ready, 1)

                def step(i):
                    for h in range(2):
                        dve.wait_ge(out_done, i * 2 + h + 1)
                        wait_before_reuse(dve, stored[h], i, 16)
                        nc.vector.tensor_copy(feats[h][:, :], out[h][:, 0:XH + H]).then_inc(copied, 1)
                        nc.vector.tensor_copy(S.dest_table[:, bass.ds((i * 2 + h) * H, H)],
                                              out[h][:, XH + H:WIDTH]).then_inc(kept, 1)

                each_step(dve, NB // 2, step)


def route(nc, C, S, bias_in, gamma_in, beta_in):
    XH = X * H
    with stage(nc) as (sb, ps, sem):
        rows = sb("ro_rows", [P, 3, XH])
        agg = sb("ro_agg", [P, NB, XH])
        square = sb("ro_square", [P, NB, XH])
        inverse = sb("ro_inverse", [P, NB, H])
        mean = sb("ro_mean", [P, NB])
        var = sb("ro_var", [P, NB])
        std = sb("ro_std", [P, NB])
        score = sb("ro_score", [P, NB, X])
        better = sb("ro_better", [P, NB, X])
        worse = sb("ro_worse", [P, NB])
        rank = sb("ro_rank", [P, NB, X])
        best = sb("ro_best", [P, NB])
        power = sb("ro_power", [P, NB, X])
        loaded = sem("ro_loaded")
        chain = sem("ro_chain")
        var_ready = sem("ro_var_ready")
        std_ready = sem("ro_std_ready")
        shifted = sem("ro_shifted")
        powered = sem("ro_powered")
        with nc.Block() as block:
            @block.sync
            def _(sp):
                for s, a in enumerate((bias_in, gamma_in, beta_in)):
                    sp.dma_start(rows[:, s, :], row_bcast(a)).then_inc(loaded, 16)

            @block.scalar
            def _(act):
                act.wait_ge(var_ready, 1)
                nc.scalar.activation(std[:, :], var[:, :], ACT.Sqrt).then_inc(std_ready, 1)
                act.wait_ge(shifted, 1)
                nc.scalar.activation(power[:, :, :].rearrange("p b x -> p (b x)"),
                                     score[:, :, :].rearrange("p b x -> p (b x)"), ACT.Exp).then_inc(powered, 1)

            @block.vector
            def _(dve):
                ch = Chain(dve, chain)
                sums = S.sums[:, :].rearrange("p (b c) -> p b c", b=NB)

                def row(s):
                    return bc(rows[:, s, 0:1], [0, NB], [1, XH])

                def per_node(ap, n=XH):
                    return bc(ap[:, 0:1], [1, NB], [0, n])

                ch.link(nc.vector.tensor_scalar(inverse[:, :, :], sums[:, :, XH:XH + H], 1e-16, None, ALU.add))
                ch.link(nc.vector.reciprocal(inverse[:, :, :], inverse[:, :, :]))
                ch.link(nc.vector.tensor_tensor(agg[:, :, :].rearrange("p b (h x) -> p b h x", h=H),
                                                sums[:, :, 0:XH].rearrange("p b (h x) -> p b h x", h=H),
                                                bc(inverse[:, 0, 0:1], [H, NB], [1, H], [0, X]), ALU.mult))
                dve.wait_ge(loaded, 48)
                ch.link(nc.vector.tensor_tensor(agg[:, :, :], agg[:, :, :], row(0), ALU.add))
                ch.link(nc.vector.tensor_reduce(mean[:, :], agg[:, :, :], AX, ALU.add))
                ch.link(nc.vector.tensor_scalar(mean[:, :], mean[:, :], 1.0 / XH, None, ALU.mult))
                ch.link(nc.vector.tensor_tensor(agg[:, :, :], agg[:, :, :], per_node(mean), ALU.subtract))
                ch.link(nc.vector.tensor_tensor(square[:, :, :], agg[:, :, :], agg[:, :, :], ALU.mult))
                ch.link(nc.vector.tensor_reduce(var[:, :], square[:, :, :], AX, ALU.add))
                nc.vector.tensor_scalar(var[:, :], var[:, :], 1.0 / XH, EPS, ALU.mult, ALU.add).then_inc(var_ready, 1)
                dve.wait_ge(std_ready, 1)
                ch.link(nc.vector.reciprocal(var[:, :], std[:, :]))
                ch.link(nc.vector.tensor_tensor(agg[:, :, :], agg[:, :, :], per_node(var), ALU.mult))
                ch.link(nc.vector.tensor_tensor(agg[:, :, :], agg[:, :, :], row(1), ALU.mult))
                ch.link(nc.vector.tensor_tensor(agg[:, :, :], agg[:, :, :], row(2), ALU.add))
                ch.link(nc.vector.tensor_reduce(score[:, :, :], agg[:, :, :].rearrange("p b (h x) -> p b x h", h=H), AX,
                                                ALU.add))
                ch.link(nc.vector.tensor_scalar(score[:, :, :], score[:, :, :], 1.0 / H, None, ALU.mult))
                for x in range(X):
                    one = bc(score[:, 0, x:x + 1], [X, NB], [0, X])
                    ch.link(nc.vector.tensor_tensor(better[:, :, :], score[:, :, :], one, ALU.is_gt))
                    if x:
                        ch.link(nc.vector.tensor_tensor(better[:, :, 0:x], score[:, :, 0:x],
                                                        bc(score[:, 0, x:x + 1], [X, NB], [0, x]), ALU.is_ge))
                    ch.link(nc.vector.tensor_reduce(rank[:, :, x], better[:, :, :], AX, ALU.add))
                ch.link(nc.vector.tensor_reduce(best[:, :], score[:, :, :], AX, ALU.max))
                nc.vector.tensor_tensor(score[:, :, :], score[:, :, :], per_node(best, X),
                                        ALU.subtract).then_inc(shifted, 1)
                dve.wait_ge(powered, 1)
                ch.link(nc.vector.tensor_scalar(rank[:, :, :], rank[:, :, :], 1.5, None, ALU.is_lt))
                ch.link(nc.vector.tensor_tensor(power[:, :, :], power[:, :, :], rank[:, :, :], ALU.mult))
                ch.link(nc.vector.tensor_reduce(worse[:, :], power[:, :, :], AX, ALU.add))
                ch.link(nc.vector.reciprocal(worse[:, :], worse[:, :]))
                ch.link(nc.vector.tensor_tensor(S.gate[:, :, :], power[:, :, :], per_node(worse, X), ALU.mult))


GT = 3


def experts(nc, C, S, w1_in, b1_in, w2_in, b2_in, out):
    FT = FF // P
    XF = X * FT
    GN = GT * P
    groups = NB // GT
    last = N - (NB - 1) * P
    with stage(nc) as (sb, ps, sem):
        w1 = sb("ex_w1", [P, KC, X, FF])
        w2 = sb("ex_w2", [P, XF, D])
        b1 = sb("ex_b1", [P, XF])
        b1_rows = sb("ex_b1_rows", [XF, P])
        b2 = sb("ex_b2", [1, X, D])
        tiles = sb("ex_tiles", [P, GT, D])
        turned = sb("ex_turned", [P, KC, GN])
        hidden = sb("ex_hidden", [P, XF, GN])
        turn = ps("ex_turn", [P, 512])
        up = [ps(f"ex_up{q}", [P, 512]) for q in range(3)]
        down = [ps(f"ex_down{q}", [P, 512]) for q in range(4)]
        loaded = sem("ex_loaded")
        b1_turned = sem("ex_b1_turned")
        b1_ready = sem("ex_b1_ready")
        tiles_ready = sem("ex_tiles_ready")
        turn_done = sem("ex_turn_done")
        turn_copied = sem("ex_turn_copied")
        up_done = sem("ex_up_done")
        gelu_done = sem("ex_gelu_done")
        down_done = sem("ex_down_done")
        added = sem("ex_added")
        stored = sem("ex_stored")
        with nc.Block() as block:
            @block.sync
            def _(sp):
                for kc in range(KC):
                    sp.dma_start(w1[:, kc, :, :], w1_in[:, kc * P:(kc + 1) * P, :].rearrange(
                        "x k f -> k x f")).then_inc(loaded, 16)
                sp.dma_start(w2[:, :, :], w2_in.rearrange("x (f p) d -> p (x f) d", p=P)).then_inc(loaded, 16)
                sp.dma_start(b1_rows[:, :], b1_in.rearrange("x (f p) -> (x f) p", p=P)).then_inc(loaded, 16)
                sp.dma_start(b2[:, :, :], b2_in.rearrange("(o x) d -> o x d", o=1)).then_inc(loaded, 16)
                sp.wait_ge(added, NB * X)
                sp.dma_start(out[0:(NB - 1) * P, :].rearrange("(t p) d -> p t d", p=P),
                             S.x[:, 0:NB - 1, :]).then_inc(stored, 16)
                sp.dma_start(out[(NB - 1) * P:N, :], S.x[0:last, NB - 1, :]).then_inc(stored, 16)
                sp.wait_ge(stored, 32)

            @block.gpsimd
            def _(pool):
                def step(i):
                    wait_before_reuse(pool, turn_done, i, KC)
                    nc.gpsimd.tensor_copy(tiles[:, :, :], S.normed[:, bass.ds(i * GT, GT), :]).then_inc(tiles_ready, 1)

                each_step(pool, groups, step)

            @block.tensor
            def _(pe):
                pe.wait_ge(loaded, 16 * (KC + 3))
                nc.tensor.transpose(turn[:, 0:XF], b1_rows[:, :], C.ident[0:XF, 0:XF]).then_inc(b1_turned, 1)
                pe.wait_ge(b1_ready, 1)

                def step(i):
                    pe.wait_ge(tiles_ready, i + 1)
                    for kc in range(KC):
                        if not (isinstance(i, int) and kc == 0):
                            pe.wait_ge(turn_copied, i * KC + kc)
                        for t in range(GT):
                            ins = nc.tensor.transpose(turn[:, t * P:(t + 1) * P], tiles[:, t, kc * P:(kc + 1) * P],
                                                      C.ident[:, :])
                        ins.then_inc(turn_done, 1)
                    pe.wait_ge(turn_copied, i * KC + KC)
                    for xf in range(XF):
                        if not (isinstance(i, int) and xf < 3):
                            pe.wait_ge(gelu_done, i * XF + xf - 2)
                        x, f = divmod(xf, FT)
                        for kc in range(KC):
                            ins = nc.tensor.matmul(up[xf % 3][:, 0:GN], w1[:, kc, x, f * P:(f + 1) * P],
                                                   turned[:, kc, :], start=(kc == 0), stop=(kc == KC - 1))
                        ins.then_inc(up_done, 1)
                    pe.wait_ge(gelu_done, i * XF + XF)
                    for n in range(GT * X):
                        t, x = divmod(n, X)
                        if not (isinstance(i, int) and n < 4):
                            pe.wait_ge(added, i * GT * X + n - 3)
                        for f in range(FT):
                            nc.tensor.matmul(down[n % 4][:, 0:D], hidden[:, x * FT + f, t * P:(t + 1) * P],
                                             w2[:, x * FT + f, :], start=(f == 0), stop=False)
                        nc.tensor.matmul(down[n % 4][:, 0:D], C.ones[0:1, :], b2[0:1, x, :], start=False,
                                         stop=True).then_inc(down_done, 1)

                each_step(pe, groups, step)

            @block.scalar
            def _(act):
                act.wait_ge(b1_turned, 1)
                nc.scalar.copy(b1[:, :], turn[:, 0:XF]).then_inc(b1_ready, 1)
                act.wait_ge(b1_ready, 1)

                def step(i):
                    for kc in range(KC):
                        act.wait_ge(turn_done, i * KC + kc + 1)
                        nc.scalar.copy(turned[:, kc, :], turn[:, 0:GN]).then_inc(turn_copied, 1)
                    for xf in range(XF):
                        act.wait_ge(up_done, i * XF + xf + 1)
                        nc.scalar.activation(hidden[:, xf, :], up[xf % 3][:, 0:GN], ACT.Gelu,
                                             bias=b1[:, xf:xf + 1]).then_inc(gelu_done, 1)

                each_step(act, groups, step)

            @block.vector
            def _(dve):
                def step(i):
                    for n in range(GT * X):
                        t, x = divmod(n, X)
                        dve.wait_ge(down_done, i * GT * X + n + 1)
                        if not (isinstance(i, int) and n == 0):
                            dve.wait_ge(added, i * GT * X + n)
                        row = S.x[:, bass.ds(i * GT + t, 1), :].rearrange("p t d -> p (t d)")
                        gate = S.gate[:, bass.ds(i * GT + t, 1), x:x + 1].rearrange("p t o -> p (t o)")
                        nc.vector.scalar_tensor_tensor(row, down[n % 4][:, 0:D], gate, row, ALU.mult,
                                                       ALU.add).then_inc(added, 1)

                each_step(dve, groups, step)


class Space:
    pass


def graph_space(nc, g):
    S = Space()

    def dram(name, shape, dt=F32):
        return nc.dram_tensor(f"{g.name}_{name}", shape, dt, kind="Internal").ap()

    S.key_rows = dram("key_rows", [g.raw_tiles * P, 2, P], U16)
    S.sorted = dram("sorted", [g.tiles * P * P, 1], I32)
    S.low_rows = dram("low_rows", [g.tiles * P, P], U16)
    S.place_dram = dram("place", [3, g.tiles * P], I32)
    S.live_dram = dram("live_steps", [1, 1], I32)
    S.score_table = dram("score_table", [NB * P * g.rels, g.row])
    S.feature_table = dram("feature_table", [NB * P * g.rels, g.feats]) if g is REL else None
    S.score_rows = dram("score_rows", [g.slots, H, P])
    S.peak_table = dram("peak_table", [g.tiles * P * P, H])
    return S


def attend(nc, C, g, S, src, dst, typ, features, finish):
    with stage(nc, g.name + "_") as (sb, _, _):
        S.counts = sb(f"counts", [P, NBP])
        S.start = sb(f"start", [P, NBP])
        S.last = sb(f"last", [P, NBP], I32)
        S.live = sb("live", [1, 1], I32)
        S.place_row = sb("place_row", [1, 3, g.tiles * P], I32)
        S.dest_table = sb(f"dest_table", [P, NB * g.er])
        S.sums = sb(f"sums", [P, NB * g.out])
        with stage(nc, g.name + "_") as (sb, _, _):
            W = g.raw_tiles * P
            S.lo, S.hi, S.key = (sb(f"{name}", [P, W]) for name in ("lo", "hi", "key"))
            S.packed = sb(f"packed", [P, W], I32)
            prepare_edges(nc, C, g, S, src, dst, typ)
            count_edges(nc, C, g, S)
            scatter_edges(nc, C, g, S)
        features(S)
        with stage(nc, g.name + "_") as (sb, _, _):
            W = g.tiles * P
            S.slot_row = sb(f"slot_row", [P, W], I32)
            S.slot_low = sb(f"slot_low", [P, W])
            S.slot_type = sb(f"slot_type", [P, W]) if g is REL else None
            S.score = sb("score", [P, (g.slots + U) * H])
            S.peak = sb(f"peak", [P, NB * H])
            S.kept = sb(f"kept", [P, g.slots, g.feats]) if g is ROUTE else None
            read_slots(nc, C, g, S)
            score_edges(nc, C, g, S)
            node_maxima(nc, C, g, S)
            sum_edges(nc, C, g, S)
        finish(S)


def gnn_moe_kernel(nc, x, src, dst, edge_type, conv_w, attn_l, attn_r, h_bias, w_gat, att_src, att_dst, b_gat,
                   ln_gamma, ln_beta, w1, b1, w2, b2, edge_index, out):
    rel, routing = graph_space(nc, REL), graph_space(nc, ROUTE)
    with stage(nc) as (sb, _, _):
        C = Space()
        C.ident = sb("ident", [P, P])
        C.before = sb("before", [P, P])
        C.after = sb("after", [P, P])
        C.ones = sb("ones", [P, P])
        C.zero_bf = sb("zero_bf", [P, P], BF16)
        C.zero_wide = sb("zero_wide", [P, 512], BF16)
        C.count_i = sb("count_i", [P, P], I32)
        C.part_i = sb("part_i", [P, 1], I32)
        C.count = sb("count", [P, P])
        C.part = sb("part", [P, 1])
        nodes = Space()
        nodes.x = sb("x_nodes", [P, NB, D])
        nodes.gate = sb("gate", [P, NB, X])
        constants(nc, C)
        load_nodes(nc, nodes, x)

        def with_normed(name, then):
            with ExitStack() as inner:
                nodes.normed = inner.enter_context(nc.sbuf_tensor(f"{name}_normed", [P, NB, D], F32))
                normalise(nc, C, nodes, name)
                then()

        def relation_stage(S):
            S.normed = nodes.normed
            relation_features(nc, C, S, conv_w, attn_l, attn_r)

        def routing_stage(S):
            S.normed = nodes.normed
            routing_features(nc, C, S, w_gat, att_src, att_dst)

        def finish_relations(S):
            S.x = nodes.x
            add_attention(nc, C, S, h_bias)

        def finish_routing(S):
            S.gate = nodes.gate
            route(nc, C, S, b_gat, ln_gamma, ln_beta)

        attend(nc, C, REL, rel, src, dst, edge_type,
               lambda S: with_normed("norm1", lambda: relation_stage(S)), finish_relations)
        attend(nc, C, ROUTE, routing, edge_index[0], edge_index[1], None,
               lambda S: with_normed("norm2", lambda: routing_stage(S)), finish_routing)
        with_normed("norm3", lambda: experts(nc, C, nodes, w1, b1, w2, b2, out))


_INS = ["x", "src", "dst", "edge_type_8", "L0_gnn_conv_weights", "L0_gnn_attn_l", "L0_gnn_attn_r", "L0_gnn_h_bias",
        "L0_ffn_W_gat", "L0_ffn_att_src", "L0_ffn_att_dst", "L0_ffn_b_gat", "L0_ffn_ln_gamma", "L0_ffn_ln_beta",
        "L0_ffn_W1", "L0_ffn_b1", "L0_ffn_W2", "L0_ffn_b2", "L0_ffn_edge_index"]


def kernel(**inputs):
    import numpy as _np
    import concourse.bacc as _bacc
    from concourse import mybir as _mybir
    from concourse.bass_utils import run_bass_kernel_spmd as _run

    nc = _bacc.Bacc("TRN2", target_bir_lowering=False, num_devices=1)
    arrays, args = {}, []
    for name in _INS:
        a = _np.ascontiguousarray(inputs[name])
        arrays[f"in_{name}_dram"] = a
        args.append(nc.dram_tensor(f"in_{name}_dram", a.shape, _mybir.dt.from_np(a.dtype), kind="ExternalInput").ap())
    out = nc.dram_tensor("out_0_dram", (N, D), F32, kind="ExternalOutput").ap()
    gnn_moe_kernel(nc, *args, out)
    r = _run(nc, [arrays], core_ids=[0])
    return r.results[0]["out_0_dram"]
```

```python
from contextlib import ExitStack, contextmanager

import concourse.bass as bass
from concourse import mybir

F32, BF16, I32, U16 = mybir.dt.float32, mybir.dt.bfloat16, mybir.dt.int32, mybir.dt.uint16
ALU = mybir.AluOpType
ACT = mybir.ActivationFunctionType
AX = mybir.AxisListType.X

P = 128
N = 3750
NB = -(-N // P)
NBP = 32
D = 256
KC = D // P
H = 4
R = 8
HD = D // H
E1 = 123750
E2 = 131072
X = 4
FF = 2 * D
XH = X * H
U = 8
G2 = 2 * U
Q = 4
PARTS = 3
EPS = 1e-5
SLOPE = 0.2
BIG = 1.0e30
FREE_LO, FREE_HI = 255, 31


class Graph:

    def __init__(self, name, chunks, types, feats):
        self.name = name
        self.raw = -(-chunks // G2) * G2
        self.raw_tiles = -(-self.raw // P)
        self.slots = -(-(self.raw + NB) // (Q * U)) * (Q * U)
        self.tiles = -(-(self.slots + Q * U) // P)
        self.rels = types
        self.er = types * H
        self.feats = feats
        self.out = feats + H


REL = Graph("rel", -(-E1 // P), R, D)
ROUTE = Graph("route", E2 // P + NB, 1, X * H)


def row_bcast(ap, parts=P):
    return bass.AP(ap.tensor, ap.offset, [[0, parts]] + [list(x) for x in ap.ap])


class Chain:

    def __init__(self, eng, sem, step=None, per_step=0, before=0):
        self.eng, self.sem, self.step, self.per_step, self.before, self.n = eng, sem, step, per_step, before, 0

    def give(self, ins):
        ins.then_inc(self.sem, 1)
        self.n += 1

    def take(self):
        at = self.before + self.n
        self.eng.wait_ge(self.sem, at if self.step is None else self.step * self.per_step + at)

    def link(self, ins):
        self.give(ins)
        self.take()

    def end(self):
        assert self.step is None or self.n == self.per_step, (self.n, self.per_step)


@contextmanager
def stage(nc, name=""):
    sems = []
    with ExitStack() as ctx:
        def sb(label, shape, dt=F32):
            return ctx.enter_context(nc.sbuf_tensor(name + label, shape, dt))

        def ps(label, shape, dt=F32):
            return ctx.enter_context(nc.psum_tensor(name + label, shape, dt))

        def sem(label):
            sems.append(nc.alloc_semaphore(name + label))
            return sems[-1]

        yield sb, ps, sem
        if sems:
            nc.clear_and_free_semaphores(sems)
            nc.all_engine_barrier()


def each_step(eng, steps, body, live=None):
    body(0)
    with eng.Fori(1, steps) as i:
        if live is None:
            body(i)
        else:
            with eng.If(i < live):
                body(i)


def live_steps(eng, S, steps):
    return eng.value_load(S.live[0:1, 0:1], min_val=1, max_val=steps)


def last_step(eng, S, steps):
    return eng.value_load(S.live[0:1, 1:2], min_val=0, max_val=steps - 1)


def wait_before_reuse(eng, sem, step, per_step, at=0):
    if not (isinstance(step, int) and step == 0):
        eng.wait_ge(sem, step * per_step + at)


def bc(ap, *dims):
    return bass.AP(ap.tensor, ap.offset, [list(ap.ap[0])] + [list(x) for x in dims])


def ahead(i, h):
    return (i, 1) if h == 0 else (i + 1, 0)


def later(i, h, n):
    return i + (h + n) // Q, (h + n) % Q


def places(eng, S, what, first, width, n=U):
    row = S.place_row[0:1, what, bass.ds(first, n)]
    _, values = eng.bass.values_load_multi_w_load_instructions(
        row, engines=[eng.engine], min_val=0, max_val=(NB - 1) * width,
        skip_runtime_bounds_check_because="count_edges makes them from blocks that it holds below NB")
    return values


def turns(tiles, arrays):
    return [(k, t, min(4, tiles - t)) for k in range(arrays) for t in range(0, tiles, 4)]


def constants(nc, C):
    with stage(nc) as (_, _, sem):
        filled = sem("const_filled")
        made = sem("const_made")
        with nc.Block() as block:
            @block.gpsimd
            def _(pool):
                nc.gpsimd.memset(C.ident[:, :], 0.0).then_inc(filled, 1)
                nc.gpsimd.memset(C.before[:, :], 1.0).then_inc(filled, 1)
                nc.gpsimd.memset(C.after[:, :], 1.0).then_inc(filled, 1)
                nc.gpsimd.memset(C.ones[:, :], 1.0).then_inc(filled, 1)
                nc.gpsimd.memset(C.zero_bf[:, :], 0.0).then_inc(filled, 1)
                pool.wait_ge(filled, 5)
                nc.gpsimd.affine_select(out=C.ident[:, :], in_=C.ident[:, :], compare_op=ALU.not_equal, fill=1.0,
                                        base=0, pattern=[[-1, P]], channel_multiplier=1).then_inc(made, 1)
                nc.gpsimd.affine_select(out=C.before[:, :], in_=C.before[:, :], compare_op=ALU.is_gt, fill=0.0,
                                        base=0, pattern=[[-1, P]], channel_multiplier=1).then_inc(made, 1)
                nc.gpsimd.affine_select(out=C.after[:, :], in_=C.after[:, :], compare_op=ALU.is_gt, fill=0.0,
                                        base=0, pattern=[[1, P]], channel_multiplier=-1).then_inc(made, 1)
                nc.gpsimd.iota(C.count_i[:, :], [[1, P]], base=0, channel_multiplier=0).then_inc(made, 1)
                nc.gpsimd.iota(C.part_i[:, :], [[0, 1]], base=0, channel_multiplier=1).then_inc(made, 1)
                pool.wait_ge(made, 5)

            @block.vector
            def _(dve):
                dve.wait_ge(made, 5)
                nc.vector.tensor_copy(C.count[:, :], C.count_i[:, :]).then_inc(filled, 1)
                nc.vector.tensor_copy(C.part[:, :], C.part_i[:, :]).then_inc(filled, 1)


def prepare_edges(nc, C, g, S, src_in, dst_in, type_in):
    T = g.raw_tiles
    W = T * P
    with stage(nc, g.name + "_") as (sb, ps, sem):
        src = sb("pe_src", [P, W], I32)
        dst = sb("pe_dst", [P, W], I32)
        typ = sb("pe_typ", [P, W], I32)
        lo_i = sb("pe_lo_i", [P, W], I32)
        hi_i = sb("pe_hi_i", [P, W], I32)
        a_f = sb("pe_a", [P, W])
        lo_f = sb("pe_lo", [P, W])
        hi_f = sb("pe_hi", [P, W])
        rows = sb("pe_rows", [P, T, 2, P], U16)
        a_ci = sb("pe_a_ci", [P, W], I32)
        k_ci = sb("pe_k_ci", [P, W], I32)
        turned = [ps(f"pe_turned{i}", [P, 512]) for i in range(6)]
        filled = sem("pe_filled")
        loaded = sem("pe_loaded")
        split = sem("pe_split")
        rows_out = sem("pe_rows_out")
        turn_done = sem("pe_turn_done")
        turn_used = sem("pe_turn_used")
        chain = sem("pe_chain")
        n_loads = []

        with nc.Block() as block:
            @block.gpsimd
            def _(pool):
                nc.gpsimd.memset(typ[:, :], 0).then_inc(filled, 1)
                if g is REL:
                    nc.gpsimd.memset(src[:, :], 0).then_inc(filled, 1)
                    nc.gpsimd.memset(dst[:, :], N).then_inc(filled, 1)
                else:
                    nc.gpsimd.iota(src[:, W - P:W], [[1, P]], base=0, channel_multiplier=P).then_inc(filled, 1)
                    nc.gpsimd.iota(dst[:, W - P:W], [[1, P]], base=0, channel_multiplier=P).then_inc(filled, 1)

            @block.sync
            def _(sp):
                sp.wait_ge(filled, 3)
                pairs = [(src, src_in), (dst, dst_in)] + ([(typ, type_in)] if g is REL else [])
                for sbuf, dram in pairs:
                    edges = E1 if g is REL else E2
                    tiles, rest = divmod(edges, P * P)
                    sp.dma_start(sbuf[:, 0:tiles * P].rearrange("p (t e) -> p t e", e=P),
                                 dram[0:tiles * P * P].rearrange("(t p e) -> p t e", p=P, e=P)).then_inc(loaded, 16)
                    n_loads.append(1)
                    full, last = divmod(rest, P)
                    if full:
                        sp.dma_start(sbuf[0:full, tiles * P:tiles * P + P],
                                     dram[tiles * P * P:tiles * P * P + full * P].rearrange(
                                         "(p e) -> p e", e=P)).then_inc(loaded, 16)
                        n_loads.append(1)
                    if last:
                        at = edges - last
                        sp.dma_start(sbuf[full:full + 1, tiles * P:tiles * P + last],
                                     dram[at:edges].rearrange("(p e) -> p e", p=1)).then_inc(loaded, 16)
                        n_loads.append(1)
                sp.wait_ge(split, 1)
                sp.dma_start(S.key_rows.rearrange("(t p) k e -> p t k e", p=P), rows[:, :, :, :]).then_inc(rows_out, 16)
                sp.wait_ge(rows_out, 16)

            @block.vector
            def _(dve):
                ch = Chain(dve, chain)
                dve.wait_ge(loaded, 16 * len(n_loads))
                dve.wait_ge(filled, 3)
                nc.vector.tensor_scalar(src[:, :], src[:, :], float(N - 1), None, ALU.min)
                ch.link(nc.vector.tensor_scalar(dst[:, :], dst[:, :], float(N), None, ALU.min))
                nc.vector.tensor_scalar(lo_i[:, :], dst[:, :], P - 1, None, ALU.bitwise_and)
                nc.vector.tensor_scalar(hi_i[:, :], dst[:, :], 7, None, ALU.logical_shift_right)
                ch.link(nc.vector.scalar_tensor_tensor(a_f[:, :], src[:, :], float(g.rels), typ[:, :], ALU.mult,
                                                       ALU.add))
                nc.vector.tensor_copy(lo_f[:, :], lo_i[:, :])
                ch.link(nc.vector.tensor_copy(hi_f[:, :], hi_i[:, :]))
                lo3 = lo_f[:, :].rearrange("p (t e) -> p t e", e=P)
                hi3 = hi_f[:, :].rearrange("p (t e) -> p t e", e=P)
                nc.vector.scalar_tensor_tensor(rows[:, :, 0, :], hi3, 256.0, lo3, ALU.mult, ALU.add)
                ch.link(nc.vector.tensor_copy(rows[:, :, 1, :], lo3))
                nc.vector.engine_nop().then_inc(split, 1)
                for q, (k, t0, n) in enumerate(turns(T, 3)):
                    dve.wait_ge(turn_done, q + 1)
                    out = (S.lo, S.hi, a_ci)[k][:, t0 * P:(t0 + n) * P]
                    nc.vector.tensor_copy(out, turned[q % 6][:, 0:n * P]).then_inc(turn_used, 1)
                dve.wait_ge(turn_used, len(turns(T, 3)))
                ch.link(nc.vector.scalar_tensor_tensor(S.key[:, :], S.hi[:, :], 256.0, S.lo[:, :], ALU.mult, ALU.add))
                ch.link(nc.vector.tensor_copy(k_ci[:, :], S.key[:, :]))
                ch.link(nc.vector.tensor_scalar(k_ci[:, :], k_ci[:, :], 15, None, ALU.logical_shift_left))
                ch.link(nc.vector.tensor_tensor(S.packed[:, :], k_ci[:, :], a_ci[:, :], ALU.bitwise_or))

            @block.tensor
            def _(pe):
                pe.wait_ge(split, 1)
                for q, (k, t0, n) in enumerate(turns(T, 3)):
                    if q >= 6:
                        pe.wait_ge(turn_used, q - 5)
                    for i in range(n):
                        last = nc.tensor.transpose(turned[q % 6][:, i * P:(i + 1) * P],
                                                   (lo_f, hi_f, a_f)[k][:, (t0 + i) * P:(t0 + i + 1) * P],
                                                   C.ident[:, :])
                    last.then_inc(turn_done, 1)


def onehot(nc, C, out, values, width):
    return nc.vector.tensor_tensor(out, bc(values, [1, U], [0, width]), bc(C.count[:, 0:1], [0, U], [1, width]),
                                   ALU.is_equal)


class Counting:

    def __init__(self, nc, C, g, S, lent=0):
        self.nc, self.C, self.g, self.S = nc, C, g, S
        self.steps = g.raw // G2
        self.own, self.lent = U - lent, lent

    def open(self, sb, ps, sem):
        self.low = [sb(f"{self.g.name}_co_low{h}", [P, U, P], BF16) for h in range(2)]
        self.blk = [sb(f"{self.g.name}_co_blk{h}", [P, U, NBP], BF16) for h in range(2)]
        self.counts = ps(self.g.name + "_co_counts", [P, 512])
        self.ready = sem(self.g.name + "_co_onehot_ready")
        if self.lent:
            self.minus = sb(self.g.name + "_co_minus", [P, self.steps * G2])
            self.square = [sb(f"{self.g.name}_co_square{h}", [P, self.lent, P]) for h in range(2)]
            self.minus_ready = sem(self.g.name + "_co_minus_ready")
            self.squared = sem(self.g.name + "_co_squared")
            self.lent_ready = sem(self.g.name + "_co_lent_ready")
        self.used = [sem(f"{self.g.name}_co_onehot_used{h}") for h in range(2)]
        self.counted = sem(self.g.name + "_co_counted")

    def vector_half(self, dve, i, h):
        wait_before_reuse(dve, self.used[h], i, 1)
        at = i * G2 + h * U
        self.nc.vector.tensor_tensor(self.low[h][:, 0:self.own, :], bc(self.S.lo[:, bass.ds(at, 1)], [1, self.own], [0, P]),
                                     bc(self.C.count[:, 0:1], [0, self.own], [1, P]), ALU.is_equal)
        onehot(self.nc, self.C, self.blk[h][:, :, :], self.S.hi[:, bass.ds(at, 1)], NBP).then_inc(self.ready, 1)

    def scalar_half(self, act, i, h):
        nc = self.nc
        for n in range(self.lent):
            ins = nc.scalar.activation(self.square[h][:, n, :], self.C.count[:, :], ACT.Square,
                                       bias=self.minus[:, bass.ds(i * G2 + h * U + self.own + n, 1)])
        ins.then_inc(self.squared, 1)
        act.wait_ge(self.squared, i * 2 + h + 1)
        wait_before_reuse(act, self.used[h], i, 1)
        nc.scalar.activation(self.low[h][:, self.own:U, :], self.square[h][:, :, :], ACT.Relu, scale=-1.0,
                             bias=self.C.ones[:, 0:1]).then_inc(self.lent_ready, 1)

    def vector_end(self, dve):
        dve.wait_ge(self.counted, 1)
        self.nc.vector.tensor_copy(self.S.counts[:, :], self.counts[:, 0:NBP])

    def tensor_start(self, pe):
        self.nc.tensor.matmul(self.counts[:, 0:NBP], self.C.zero_bf[:, :], self.C.zero_bf[:, 0:NBP], start=True,
                              stop=False)

    def tensor_half(self, pe, i, h):
        pe.wait_ge(self.ready, i * 2 + h + 1)
        if self.lent:
            pe.wait_ge(self.lent_ready, i * 2 + h + 1)
        for u in range(U):
            last = self.nc.tensor.matmul(self.counts[:, 0:NBP], self.low[h][:, u, :], self.blk[h][:, u, :],
                                         start=False, stop=False)
        last.then_inc(self.used[h], 1)

    def tensor_end(self, pe):
        self.nc.tensor.matmul(self.counts[:, 0:NBP], self.C.zero_bf[:, :], self.C.zero_bf[:, 0:NBP], start=False,
                              stop=True).then_inc(self.counted, 1)


def count_edges(nc, C, g, S, w, w_att, w_in, left_in, right_in):
    counting = Counting(nc, C, g, S, lent=2)
    RH = R * H
    with stage(nc, g.name + "_") as (sb, ps, sem):
        counting.open(sb, ps, sem)
        att = [sb(f"ce_att{s}", [P, R * D]) for s in range(2)]
        prod = [sb(f"ce_prod{s}", [P, R * D]) for s in range(2)]
        loaded = sem("ce_loaded")
        product = sem("ce_product")
        with nc.Block() as block:
            @block.sync
            def _(sp):
                for kc in range(KC):
                    sp.dma_start(w[:, kc, :, :, :].rearrange("p r h d -> p (r h) d"),
                                 w_in[:, :, kc * P:(kc + 1) * P, :].rearrange(
                                     "r h k d -> k (r h) d")).then_inc(loaded, 16)
                for s, a in enumerate((left_in, right_in)):
                    sp.dma_start(att[s][:, :], row_bcast(a.rearrange("r h d -> (r h d)"))).then_inc(loaded, 16)

            @block.scalar
            def _(act):
                def step(i):
                    for h in range(2):
                        counting.scalar_half(act, i, h)

                act.wait_ge(counting.minus_ready, 1)
                each_step(act, counting.steps, step)

            @block.gpsimd
            def _(pool):
                nc.gpsimd.tensor_scalar(counting.minus[:, :], S.lo[:, 0:counting.steps * G2], -1.0, None,
                                        ALU.mult).then_inc(counting.minus_ready, 1)
                pool.wait_ge(loaded, 16 * (KC + 2))
                for s in range(2):
                    for kc, out in ((0, prod[s]), (1, att[s])):
                        nc.gpsimd.tensor_tensor(out[:, :], w[:, kc, :, :, :].rearrange("p r h d -> p (r h d)"),
                                                att[s][:, :], ALU.mult).then_inc(product, 1)
                        pool.wait_ge(product, 2 * s + kc + 1)

            @block.vector
            def _(dve):
                def step(i):
                    for h in range(2):
                        counting.vector_half(dve, i, h)

                each_step(dve, counting.steps, step)
                counting.vector_end(dve)
                for s in range(2):
                    for kc, terms in ((0, prod[s]), (1, att[s])):
                        dve.wait_ge(product, 2 * s + kc + 1)
                        nc.vector.tensor_reduce(w_att[:, kc, s * RH:(s + 1) * RH],
                                                terms[:, :].rearrange("p (g d) -> p g d", d=HD), AX, ALU.add)

            @block.tensor
            def _(pe):
                def step(i):
                    for h in range(2):
                        counting.tensor_half(pe, i, h)

                counting.tensor_start(pe)
                each_step(pe, counting.steps, step)
                counting.tensor_end(pe)


def place_slots(nc, C, g, S):
    with stage(nc, g.name + "_") as (sb, ps, sem):
        size = sb("pl_size", [P, NBP])
        size_i = sb("pl_size_i", [P, NBP], I32)
        ends = sb("pl_ends", [P, NBP])
        zeros = sb("pl_zeros", [P, NBP])
        starts = sb("pl_starts", [P, NBP])
        chunk_i = sb("pl_chunk_i", [P, g.tiles], I32)
        chunk_f = sb("pl_chunk_f", [P, g.tiles])
        past = sb("pl_past", [P, g.tiles, NBP])
        blocks = sb("pl_blocks", [P, g.tiles])
        places_i = sb("pl_places_i", [P, 2, g.tiles], I32)
        free = sb("pl_free", [P, g.tiles * P], I32)
        live_i = sb("pl_live_i", [P, NBP, 2], I32)
        sums_ps = ps("pl_sums", [P, 512])
        summed = sem("pl_summed")
        chain = sem("pl_chain")
        stored = sem("pl_stored")
        numbered = sem("pl_numbered")
        numbers_ready = sem("pl_numbers_ready")
        with nc.Block() as block:
            @block.gpsimd
            def _(pool):
                nc.gpsimd.memset(free[:, :], (FREE_LO + 256 * FREE_HI) << 15).then_inc(numbered, 1)
                nc.gpsimd.iota(chunk_i[:, :], [[P * P, g.tiles]], base=0, channel_multiplier=P).then_inc(numbered, 1)

            @block.sync
            def _(sp):
                sp.wait_ge(numbered, 2)
                slots = g.tiles * P * P
                sp.dma_start(S.sorted[0:slots, :].rearrange("(p l) o -> p (l o)", p=P), free[:, :]).then_inc(stored, 16)
                sp.dma_start(S.sorted[slots:slots + 1, :], free[0:1, 0:1]).then_inc(stored, 16)
                sp.wait_ge(numbers_ready, 1)
                sp.dma_start(S.place_dram.rearrange("k (t p) -> p k t", p=P), places_i[:, :, :],
                             allow_slow_non_contiguous=True).then_inc(stored, 16)
                sp.dma_start(S.live_dram, live_i[N % P:N % P + 1, N // P, :]).then_inc(stored, 16)
                sp.wait_ge(stored, 64)
                sp.dma_start(S.place_row[0:1, :, :],
                             S.place_dram.rearrange("(o k) c -> o k c", o=1)).then_inc(stored, 16)
                sp.dma_start(S.live[0:1, :], S.live_dram).then_inc(stored, 16)
                sp.wait_ge(stored, 96)

            @block.vector
            def _(dve):
                ch = Chain(dve, chain)
                dve.wait_ge(summed, 1)
                ch.link(nc.vector.tensor_scalar(size_i[:, :], sums_ps[:, NBP:2 * NBP], float(P - 1), None, ALU.add))
                ch.link(nc.vector.tensor_scalar(size_i[:, :], size_i[:, :], 7, 7, ALU.logical_shift_right,
                                                ALU.logical_shift_left))
                nc.vector.memset(zeros[:, :], 0.0)
                ch.link(nc.vector.tensor_copy(size[:, :], size_i[:, :]))
                ch.link(nc.vector.tensor_tensor_scan(ends[:, :], size[:, :], zeros[:, :], 0.0, ALU.add, ALU.add))
                ch.link(nc.vector.tensor_tensor(starts[:, :], ends[:, :], size[:, :], ALU.subtract))
                ch.link(nc.vector.tensor_tensor(S.start[:, :], sums_ps[:, 0:NBP], starts[:, :], ALU.add))
                ch.link(nc.vector.tensor_scalar(live_i[:, :, 0], S.start[:, :], float(Q * U * P - 1), None, ALU.add))
                ch.link(nc.vector.tensor_scalar(live_i[:, :, 0], live_i[:, :, 0], (Q * U * P).bit_length() - 1, None,
                                                ALU.logical_shift_right))
                ch.link(nc.vector.tensor_scalar(live_i[:, :, 0], live_i[:, :, 0], 1.0, None, ALU.max))
                ch.link(nc.vector.tensor_scalar(live_i[:, :, 1], live_i[:, :, 0], -1.0, None, ALU.add))
                dve.wait_ge(numbered, 2)
                ch.link(nc.vector.tensor_copy(chunk_f[:, :], chunk_i[:, :]))
                ch.link(nc.vector.tensor_tensor(past[:, :, :], bc(ends[:, 0:1], [0, g.tiles], [1, NBP]),
                                                bc(chunk_f[:, 0:1], [1, g.tiles], [0, NBP]), ALU.is_le))
                ch.link(nc.vector.tensor_reduce(blocks[:, :], past[:, :, 0:NB], AX, ALU.add))
                for k, width in enumerate((PARTS * g.er, g.out)):
                    ins = nc.vector.tensor_scalar(places_i[:, k, :], blocks[:, :], float(NB - 1), float(width), ALU.min,
                                                  ALU.mult)
                ins.then_inc(numbers_ready, 1)

            @block.tensor
            def _(pe):
                nc.tensor.matmul(sums_ps[:, 0:NBP], C.after[:, :], S.counts[:, :], start=True, stop=True)
                nc.tensor.matmul(sums_ps[:, NBP:2 * NBP], C.ones[:, :], S.counts[:, :], start=True,
                                 stop=True).then_inc(summed, 1)


def prepared(S):
    return S.lo, S.hi, S.key, S.packed


class Beside:

    spans = []

    def open(self, sb, ps, sem): ...
    def sync_start(self, sp): ...
    def sync_end(self, sp): ...
    def tensor_start(self, pe): ...
    def tensor_first(self, pe, i, v): ...
    def tensor_middle(self, pe, i, v): ...
    def tensor_last(self, pe, i, v): ...
    def scalar_start(self, act): ...
    def scalar_step(self, act, i, v): ...
    def scalar_end(self, act): ...


def each_span(eng, spans, steps, body):
    for first, end, v in spans + [(spans[-1][1], steps, None)]:
        if first == 0:
            body(0, v)
        if end > first:
            with eng.Fori(max(first, 1), end) as i:
                body(i, v)


class RelationFeatures(Beside):

    def __init__(self, nc, C, S, w, w_att, other):
        self.nc, self.C, self.S, self.w, self.w_att, self.other = nc, C, S, w, w_att, other
        self.spans = [(0, NB, 0)]

    def open(self, sb, ps, sem):
        self.tile = sb("rf_tile", [P, D])
        self.nodes = sb("rf_nodes", [P, KC, P])
        self.feats = sb("rf_feats", [P, R, D + H])
        self.turn = ps("rf_turn", [P, 512])
        self.banks = [ps(f"rf_bank{q}", [P, 512]) for q in range(2)]
        self.tile_ready = sem("rf_tile_ready")
        self.turn_done = sem("rf_turn_done")
        self.nodes_ready = sem("rf_nodes_ready")
        self.bank_done = sem("rf_bank_done")
        self.copied = sem("rf_copied")
        self.feats_ready = sem("rf_feats_ready")
        self.stored = sem("rf_stored")
        self.put_by = sem("rf_put_by")

    def sync_start(self, sp):
        for k, edges in enumerate(prepared(self.other)):
            sp.dma_start(self.other.prepared_dram[k], edges[:, :].bitcast(I32) if k < 3 else edges[:, :]).then_inc(
                self.put_by, 16)

    def sync_end(self, sp):
        sp.wait_ge(self.put_by, 16 * len(prepared(self.other)))

    def tensor_first(self, pe, i, v):
        nc = self.nc
        pe.wait_ge(self.tile_ready, i + 1)
        for kc in range(KC):
            last = nc.tensor.transpose(self.turn[:, kc * P:(kc + 1) * P], self.tile[:, kc * P:(kc + 1) * P],
                                       self.C.ident[:, :])
        last.then_inc(self.turn_done, 1)

    def products(self, pe, i, q):
        nc = self.nc
        if q >= 2:
            pe.wait_ge(self.copied, i * 5 + q - 1)
        else:
            wait_before_reuse(pe, self.copied, i, 5)
        for kc in range(KC):
            out = self.banks[q % 2][:, :] if q < 4 else self.banks[q % 2][:, 0:2 * R * H]
            rhs = (self.w[:, kc, 2 * q:2 * q + 2, :, :].rearrange("p r h d -> p (r h d)") if q < 4
                   else self.w_att[:, kc, :])
            last = nc.tensor.matmul(out, self.nodes[:, kc, :], rhs, start=(kc == 0), stop=(kc == KC - 1))
        last.then_inc(self.bank_done, 1)

    def tensor_middle(self, pe, i, v):
        pe.wait_ge(self.nodes_ready, i + 1)
        for q in range(2):
            self.products(pe, i, q)

    def tensor_last(self, pe, i, v):
        for q in range(2, 5):
            self.products(pe, i, q)

    def scalar_step(self, act, i, v):
        nc, S = self.nc, self.S
        RH = R * H
        wait_before_reuse(act, self.turn_done, i, 1)
        nc.scalar.copy(self.tile[:, :], S.normed[:, bass.ds(i, 1), :].rearrange("p t d -> p (t d)")).then_inc(
            self.tile_ready, 1)
        act.wait_ge(self.turn_done, i + 1)
        wait_before_reuse(act, self.bank_done, i, 5)
        nc.scalar.copy(self.nodes[:, :, :].rearrange("p k n -> p (k n)"), self.turn[:, 0:KC * P]).then_inc(
            self.nodes_ready, 1)
        wait_before_reuse(act, self.stored, i, 16)
        for q in range(4):
            act.wait_ge(self.bank_done, i * 5 + q + 1)
            nc.scalar.copy(self.feats[:, 2 * q:2 * q + 2, 0:D],
                           self.banks[q % 2][:, :].rearrange("p (r d) -> p r d", r=2)).then_inc(self.copied, 1)
        act.wait_ge(self.bank_done, i * 5 + 5)
        nc.scalar.copy(self.feats[:, :, D:D + H],
                       self.banks[0][:, 0:RH].rearrange("p (r h) -> p r h", h=H)).then_inc(self.feats_ready, 1)
        nc.scalar.copy(S.dest_table[:, bass.ds(i * RH, RH)], self.banks[0][:, RH:2 * RH]).then_inc(self.copied, 1)
        act.wait_ge(self.copied, i * 5 + 5)
        act.dma_start(S.table[bass.ds(i * (P * R), P * R), :].rearrange("(p r) d -> p (r d)", r=R),
                      self.feats[:, :, :].rearrange("p r d -> p (r d)")).then_inc(self.stored, 16)

    def scalar_end(self, act):
        act.wait_ge(self.stored, NB * 16)


class Experts(Beside):

    PAIR = 2
    FT = FF // P

    def __init__(self, nc, C, S, w_route, w1_in, b1_in, w2_in, b2_in):
        self.nc, self.C, self.S, self.w_route = nc, C, S, w_route
        self.w1_in, self.b1_in, self.w2_in, self.b2_in = w1_in, b1_in, w2_in, b2_in
        self.spans = [(v * NB, (v + 1) * NB, v) for v in range(X // self.PAIR)]

    def open(self, sb, ps, sem):
        XF = X * self.FT
        self.w1 = sb("ex_w1", [P, KC, X, FF])
        self.w2 = sb("ex_w2", [P, XF, D])
        self.b1 = sb("ex_b1", [P, XF])
        self.b1_rows = sb("ex_b1_rows", [XF, P])
        self.b2 = sb("ex_b2", [1, X, D])
        self.tile = sb("ex_tile", [P, D])
        self.nodes = sb("ex_nodes", [P, KC, P])
        self.hidden = sb("ex_hidden", [P, self.PAIR * self.FT, P])
        self.feats = sb("ex_feats", [P, XH + H])
        self.result = sb("ex_result", [P, self.PAIR, D])
        self.turn = ps("ex_turn", [P, 512])
        self.up = [ps(f"ex_up{e}", [P, 512]) for e in range(self.PAIR)]
        self.down = ps("ex_down", [P, 512])
        self.loaded = sem("ex_loaded")
        self.b1_turned = sem("ex_b1_turned")
        self.b1_ready = sem("ex_b1_ready")
        self.tile_ready = sem("ex_tile_ready")
        self.turn_done = sem("ex_turn_done")
        self.nodes_ready = sem("ex_nodes_ready")
        self.route_done = sem("ex_route_done")
        self.feats_ready = sem("ex_feats_ready")
        self.table_stored = sem("ex_table_stored")
        self.up_done = sem("ex_up_done")
        self.gelu_done = sem("ex_gelu_done")
        self.down_done = sem("ex_down_done")
        self.result_ready = sem("ex_result_ready")
        self.stored = sem("ex_stored")

    def sync_start(self, sp):
        for kc in range(KC):
            sp.dma_start(self.w1[:, kc, :, :], self.w1_in[:, kc * P:(kc + 1) * P, :].rearrange(
                "x k f -> k x f")).then_inc(self.loaded, 16)
        sp.dma_start(self.w2[:, :, :], self.w2_in.rearrange("x (f p) d -> p (x f) d", p=P)).then_inc(self.loaded, 16)
        sp.dma_start(self.b1_rows[:, :], self.b1_in.rearrange("x (f p) -> (x f) p", p=P)).then_inc(self.loaded, 16)
        sp.dma_start(self.b2[:, :, :], self.b2_in.rearrange("(o x) d -> o x d", o=1)).then_inc(self.loaded, 16)

    def tensor_start(self, pe):
        XF = X * self.FT
        pe.wait_ge(self.loaded, 16 * (KC + 3))
        self.nc.tensor.transpose(self.turn[:, 0:XF], self.b1_rows[:, :], self.C.ident[0:XF, 0:XF]).then_inc(
            self.b1_turned, 1)
        pe.wait_ge(self.b1_ready, 1)

    def scalar_start(self, act):
        act.wait_ge(self.b1_turned, 1)
        self.nc.scalar.copy(self.b1[:, :], self.turn[:, 0:X * self.FT]).then_inc(self.b1_ready, 1)
        act.wait_ge(self.b1_ready, 1)

    def tensor_first(self, pe, i, v):
        nc = self.nc
        pe.wait_ge(self.tile_ready, i + 1)
        for kc in range(KC):
            last = nc.tensor.transpose(self.turn[:, kc * P:(kc + 1) * P], self.tile[:, kc * P:(kc + 1) * P],
                                       self.C.ident[:, :])
        last.then_inc(self.turn_done, 1)

    def tensor_middle(self, pe, i, v):
        nc, FT = self.nc, self.FT
        pe.wait_ge(self.nodes_ready, i + 1)
        if v == 0:
            for kc in range(KC):
                last = nc.tensor.matmul(self.turn[:, D:D + XH + 2 * H], self.nodes[:, kc, :], self.w_route[:, kc, :],
                                        start=(kc == 0), stop=(kc == KC - 1))
            last.then_inc(self.route_done, 1)
        for e in range(self.PAIR):
            for f in range(FT):
                for kc in range(KC):
                    last = nc.tensor.matmul(self.up[e][:, f * P:(f + 1) * P],
                                            self.w1[:, kc, v * self.PAIR + e, f * P:(f + 1) * P],
                                            self.nodes[:, kc, :], start=(kc == 0), stop=(kc == KC - 1))
            last.then_inc(self.up_done, 1)

    def tensor_last(self, pe, i, v):
        nc, FT = self.nc, self.FT
        wait_before_reuse(pe, self.result_ready, i, 1)
        for e in range(self.PAIR):
            pe.wait_ge(self.gelu_done, i * self.PAIR + e + 1)
            x = v * self.PAIR + e
            out = self.down[:, e * D:(e + 1) * D]
            for f in range(FT):
                nc.tensor.matmul(out, self.hidden[:, e * FT + f, :], self.w2[:, x * FT + f, :], start=(f == 0),
                                 stop=False)
            last = nc.tensor.matmul(out, self.C.ones[0:1, :], self.b2[0:1, x, :], start=False, stop=True)
        last.then_inc(self.down_done, 1)

    def scalar_step(self, act, i, v):
        nc, S, FT = self.nc, self.S, self.FT
        at = i - v * NB
        wait_before_reuse(act, self.turn_done, i, 1)
        nc.scalar.copy(self.tile[:, :], S.normed[:, bass.ds(at, 1), :].rearrange("p t d -> p (t d)")).then_inc(
            self.tile_ready, 1)
        act.wait_ge(self.turn_done, i + 1)
        nc.scalar.copy(self.nodes[:, :, :].rearrange("p k n -> p (k n)"), self.turn[:, 0:KC * P]).then_inc(
            self.nodes_ready, 1)
        if not (isinstance(i, int) and i == 0):
            self.store(act, i - 1)
        if v == 0:
            act.wait_ge(self.route_done, i + 1)
            wait_before_reuse(act, self.table_stored, i, 16)
            nc.scalar.copy(self.feats[:, :], self.turn[:, D:D + XH + H]).then_inc(self.feats_ready, 1)
            nc.scalar.copy(S.dest_table[:, bass.ds(i * H, H)], self.turn[:, D + XH + H:D + XH + 2 * H])
            act.wait_ge(self.feats_ready, i + 1)
            act.dma_start(S.table[bass.ds(i * P, P), :], self.feats[:, :]).then_inc(self.table_stored, 16)
        for e in range(self.PAIR):
            act.wait_ge(self.up_done, i * self.PAIR + e + 1)
            for f in range(FT):
                xf = (v * self.PAIR + e) * FT + f
                last = nc.scalar.activation(self.hidden[:, e * FT + f, :], self.up[e][:, f * P:(f + 1) * P], ACT.Gelu,
                                            bias=self.b1[:, xf:xf + 1])
            last.then_inc(self.gelu_done, 1)

    def store(self, act, i):
        act.wait_ge(self.down_done, i + 1)
        if not (isinstance(i, int) and i == 0):
            act.wait_ge(self.stored, i * 16)
        self.nc.scalar.copy(self.result[:, :, :].rearrange("p e d -> p (e d)"), self.down[:, :]).then_inc(
            self.result_ready, 1)
        act.wait_ge(self.result_ready, i + 1)
        act.dma_start(self.S.expert_out[bass.ds(i * P, P), :, :], self.result[:, :, :]).then_inc(self.stored, 16)

    def scalar_end(self, act):
        steps = self.spans[-1][1]
        self.store(act, steps - 1)
        act.wait_ge(self.stored, steps * 16)
        act.wait_ge(self.table_stored, NB * 16)


def scatter_edges(nc, C, g, S, beside, counting):
    steps = g.raw // G2
    with stage(nc, g.name + "_") as (sb, ps, sem):
        low = [sb(f"se_low{h}", [P, U, P], BF16) for h in range(2)]
        blk = [sb(f"se_blk{h}", [P, U, NBP], BF16) for h in range(2)]
        low_t = [sb(f"se_low_t{h}", [P, U, P]) for h in range(2)]
        rows = [sb(f"se_rows{h}", [P, U, 2, P], U16) for h in range(2)]
        table = [sb(f"se_table{h}", [P, U + 1, NBP]) for h in range(2)]
        match = [sb(f"se_match{h}", [P, U, P], BF16) for h in range(2)]
        rank = [sb(f"se_rank{h}", [P, U]) for h in range(2)]
        pick = [sb(f"se_pick{h}", [P, U, NBP]) for h in range(2)]
        base = [sb(f"se_base{h}", [P, U]) for h in range(2)]
        slot = [sb(f"se_slot{h}", [P, U], I32) for h in range(2)]
        load = [sb(f"se_load{h}", [P, U], I32) for h in range(2)]
        grow = [ps(f"se_grow{h}", [P, 512]) for h in range(2)]
        look = [ps(f"se_look{h}", [P, 512]) for h in range(2)]
        rows_in = [sem(f"se_rows_in{h}") for h in range(2)]
        one = sem("se_onehot_ready")
        grown = sem("se_grown")
        tables = sem("se_table_ready")
        looked = sem("se_looked")
        picked = sem("se_picked")
        matched = sem("se_matched")
        slots = sem("se_slots_ready")
        chain = sem("se_chain")
        begun = sem("se_scatter_begun")
        sent = [sem(f"se_sent{h}") for h in range(2)]
        beside.open(sb, ps, sem)
        if counting:
            counting.open(sb, ps, sem)
        with nc.Block() as block:
            @block.sync
            def _(sp):
                beside.sync_start(sp)

                def load_rows(i, h):
                    wait_before_reuse(sp, matched, i, 2, h - 1)
                    chunk = S.key_rows[bass.ds(i * G2 + h * U, U), :, :]
                    sp.dma_start(rows[h][:, :, :, :].rearrange("p u k e -> p (u k e)"),
                                 row_bcast(chunk.rearrange("u k e -> (u k e)"))).then_inc(rows_in[h], 16)

                def step(i):
                    load_rows(i, 0)
                    load_rows(i, 1)

                each_step(sp, steps, step)
                load_rows(steps, 0)
                sp.wait_ge(rows_in[0], 16 * (steps + 1))
                beside.sync_end(sp)

            @block.vector
            def _(dve):
                ch0 = Chain(dve, chain)
                ch0.link(nc.vector.tensor_copy(table[0][:, 0, :], S.start[:, :]))

                def onehots(i, h):
                    at = i * G2 + h * U
                    onehot(nc, C, low[h][:, :, :], S.lo[:, bass.ds(at, 1)], P)
                    onehot(nc, C, blk[h][:, :, :], S.hi[:, bass.ds(at, 1)], NBP)
                    dve.wait_ge(rows_in[h], i * 16 + 16)
                    nc.vector.tensor_scalar(low_t[h][:, :, :], rows[h][:, :, 1, :], C.part[:, 0:1], None,
                                            ALU.is_equal).then_inc(one, 1)

                def matches(i, h):
                    for u in range(U):
                        ins = nc.vector.scalar_tensor_tensor(
                            match[h][:, u, :], rows[h][:, u, 0, :], S.key[:, bass.ds(i * G2 + h * U + u, 1)],
                            C.before[:, :], ALU.is_equal, ALU.mult, accum_out=rank[h][:, u:u + 1])
                    ins.then_inc(matched, 1)

                def step(i):
                    ch = Chain(dve, chain, i, 4, 1)
                    for h in range(2):
                        onehots(*ahead(i, h))
                        dve.wait_ge(grown, i * 2 + h + 1)
                        ch.link(nc.vector.tensor_tensor(
                            table[h][:, 1:, :], grow[h][:, 0:U * NBP].rearrange("p (u b) -> p u b", b=NBP),
                            bc(table[h][:, 0, 0:1], [0, U], [1, NBP]), ALU.add))
                        nc.vector.tensor_copy(table[1 - h][:, 0, :], table[h][:, U, :]).then_inc(tables, 1)
                        matches(*ahead(i, h))
                        if counting:
                            counting.vector_half(dve, i, h)
                        dve.wait_ge(looked, i * 2 + h + 1)
                        nc.vector.tensor_tensor(
                            pick[h][:, :, :], look[h][:, 0:U * NBP].rearrange("p (u b) -> p u b", b=NBP),
                            blk[h][:, :, :], ALU.mult).then_inc(picked, 1)
                        dve.wait_ge(picked, i * 2 + h + 1)
                        ch.link(nc.vector.tensor_reduce(base[h][:, :], pick[h][:, :, :], AX, ALU.add))
                        wait_before_reuse(dve, sent[h], i, 16 * U)
                        dve.wait_ge(matched, i * 2 + h + 1)
                        nc.vector.tensor_tensor(slot[h][:, :], base[h][:, :], rank[h][:, :], ALU.add)
                        nc.vector.tensor_copy(load[h][:, :], S.packed[:, bass.ds(i * G2 + h * U, U)]).then_inc(slots, 1)
                    ch.end()

                onehots(0, 0)
                matches(0, 0)
                each_step(dve, steps, step)
                if counting:
                    for i in range(steps, counting.steps):
                        for h in range(2):
                            counting.vector_half(dve, i, h)
                    counting.vector_end(dve)

            @block.tensor
            def _(pe):
                def count(i, h):
                    pe.wait_ge(one, i * 2 + h + 1)
                    for u in range(U):
                        last = nc.tensor.matmul(grow[h][:, u * NBP:U * NBP], low[h][:, u, :],
                                                bc(blk[h][:, u, 0:1], [0, U - u], [1, NBP]),
                                                start=(u == 0), stop=(u == U - 1))
                    last.then_inc(grown, 1)

                def step(i, variant):
                    if variant is not None:
                        beside.tensor_first(pe, i, variant)
                    for h in range(2):
                        pe.wait_ge(tables, i * 2 + h + 1)
                        for u in range(U):
                            last = nc.tensor.matmul(look[h][:, u * NBP:(u + 1) * NBP], low_t[h][:, u, :],
                                                    table[h][:, u, :], start=True, stop=True)
                        last.then_inc(looked, 1)
                        if h == 0:
                            count(i, 1)
                        else:
                            count(i + 1, 0)
                        if counting:
                            counting.tensor_half(pe, i, h)
                        if variant is not None:
                            (beside.tensor_middle, beside.tensor_last)[h](pe, i, variant)

                beside.tensor_start(pe)
                count(0, 0)
                if counting:
                    counting.tensor_start(pe)
                each_span(pe, beside.spans, steps, step)
                if counting:
                    for i in range(steps, counting.steps):
                        for h in range(2):
                            counting.tensor_half(pe, i, h)
                    counting.tensor_end(pe)

            @block.scalar
            def _(act):
                def step(i, variant):
                    if variant is not None:
                        beside.scalar_step(act, i, variant)

                beside.scalar_start(act)
                each_span(act, beside.spans, beside.spans[-1][1], step)
                beside.scalar_end(act)

            @block.gpsimd
            def _(pool):
                def step(i):
                    for h in range(2):
                        pool.wait_ge(slots, i * 2 + h + 1)
                        pool.sem_inc(begun, 1)
                        for u in range(U):
                            nc.gpsimd.indirect_dma_start(
                                S.sorted, bass.IndirectOffsetOnAxis(ap=slot[h][:, u:u + 1], axis=0),
                                load[h][:, u:u + 1], None).then_inc(sent[h], 16)

                each_step(pool, steps, step)
                for h in range(2):
                    pool.wait_ge(sent[h], steps * U * 16)


def read_slots(nc, C, g, S):
    T = g.tiles
    W = T * P
    with stage(nc, g.name + "_") as (sb, ps, sem):
        packed = sb("rs_packed", [P, W], I32)
        after = sb("rs_after", [P, W], I32)
        cuts = sb("rs_cuts", [P, W])
        row_i = sb("rs_row_i", [P, W], I32)
        key_i = sb("rs_key_i", [P, W], I32)
        typ_i = sb("rs_typ_i", [P, W], I32)
        row_f = sb("rs_row", [P, W])
        low_f = sb("rs_low", [P, W])
        typ_f = sb("rs_typ", [P, W])
        low_u = sb("rs_low_u", [P, T, P], U16)
        turned = [ps(f"rs_turned{i}", [P, 512]) for i in range(6)]
        loaded = sem("rs_loaded")
        chain = sem("rs_chain")
        split = sem("rs_split")
        cut = sem("rs_cut")
        stored = sem("rs_stored")
        turn_done = sem("rs_turn_done")
        turn_used = sem("rs_turn_used")
        groups = turns(T, 3 if g is REL else 2)
        with nc.Block() as block:
            @block.sync
            def _(sp):
                for shift, to in ((0, packed), (1, after)):
                    sp.dma_start(to[:, :].rearrange("p (t e) -> p t e", e=P),
                                 S.sorted[shift:shift + W * P, :].rearrange("(t p e) o -> p t (e o)", p=P,
                                                                           e=P)).then_inc(loaded, 16)
                sp.wait_ge(split, 1)
                sp.dma_start(S.low_rows.rearrange("(t p) e -> p t e", p=P), low_u[:, :, :]).then_inc(stored, 16)
                sp.wait_ge(cut, 1)
                sp.dma_start(S.cuts[1:1 + W * P].rearrange("(t p e) -> p t e", p=P, e=P),
                             cuts[:, :].rearrange("p (t e) -> p t e", e=P)).then_inc(stored, 16)
                sp.dma_start(S.cuts[0:1].rearrange("(o e) -> o e", o=1), cuts[0:1, 0:1]).then_inc(stored, 16)
                sp.wait_ge(stored, 48)

            @block.vector
            def _(dve):
                ch = Chain(dve, chain)
                dve.wait_ge(loaded, 32)
                nc.vector.tensor_scalar(row_i[:, :], packed[:, :], 0x7fff, None, ALU.bitwise_and)
                ch.link(nc.vector.tensor_scalar(key_i[:, :], packed[:, :], 15, 255, ALU.logical_shift_right,
                                                ALU.bitwise_and))
                nc.vector.tensor_scalar(typ_i[:, :], row_i[:, :], g.rels - 1, None, ALU.bitwise_and)
                nc.vector.tensor_copy(row_f[:, :], row_i[:, :])
                nc.vector.tensor_copy(low_u[:, :, :], key_i[:, :].rearrange("p (t e) -> p t e", e=P))
                ch.link(nc.vector.tensor_copy(low_f[:, :], key_i[:, :]))
                nc.vector.tensor_copy(typ_f[:, :], typ_i[:, :]).then_inc(split, 1)
                nc.vector.tensor_scalar(packed[:, :], packed[:, :], 15, None, ALU.logical_shift_right)
                ch.link(nc.vector.tensor_scalar(after[:, :], after[:, :], 15, None, ALU.logical_shift_right))
                ch.link(nc.vector.tensor_tensor(cuts[:, :], packed[:, :], after[:, :], ALU.is_equal))
                nc.vector.tensor_scalar(cuts[:, :], cuts[:, :], 1.0, BIG, ALU.subtract, ALU.mult).then_inc(cut, 1)
                for q, (k, t0, n) in enumerate(groups):
                    dve.wait_ge(turn_done, q + 1)
                    out = (S.slot_row, S.slot_low, S.slot_type)[k][:, t0 * P:(t0 + n) * P]
                    nc.vector.tensor_copy(out, turned[q % 6][:, 0:n * P]).then_inc(turn_used, 1)

            @block.tensor
            def _(pe):
                pe.wait_ge(split, 1)
                for q, (k, t0, n) in enumerate(groups):
                    if q >= 6:
                        pe.wait_ge(turn_used, q - 5)
                    for i in range(n):
                        last = nc.tensor.transpose(turned[q % 6][:, i * P:(i + 1) * P],
                                                   (row_f, low_f, typ_f)[k][:, (t0 + i) * P:(t0 + i + 1) * P],
                                                   C.ident[:, :])
                    last.then_inc(turn_done, 1)


def attend_edges(nc, C, g, S):
    steps = g.slots // (Q * U)
    hd = g.feats // H
    cols = hd + 1
    own = 0 if g is REL else U
    lent = U - own
    banks = 4
    L = U * P
    BACK = U * R * H
    UH = U * H
    with stage(nc, g.name + "_") as (sb, ps, sem):
        index = [sb(f"ae_index{h}", [P, U], I32) for h in range(Q)]
        got = [sb(f"ae_got{h}", [P, U, g.out]) for h in range(Q)]
        rows = [sb(f"ae_rows{k}", [P, U, P], U16) for k in range(2)]
        low_t = [sb(f"ae_low_t{k}", [P, U, P], BF16) for k in range(2)]
        first1 = [sb(f"ae_first{k}", [P, 1]) for k in range(2)]
        dest_parts = sb("ae_dest_parts", [P, NB, PARTS, g.er], BF16)
        low = [sb(f"ae_low{k}", [P, U, P]) for k in range(2)]
        type1 = [sb(f"ae_type{k}", [P, U, R]) for k in range(2)]
        pick = sb("ae_pick", [P, U, g.rels, H])
        dest = sb("ae_dest", [P, U, H])
        both = sb("ae_both", [P, U, H])
        score = sb("ae_score", [P, UH])
        cuts = [sb(f"ae_cuts{k}", [H, L + 1]) for k in range(2)]
        upto = [sb(f"ae_upto{k}", [H, L]) for k in range(2)]
        peak = sb("ae_peak", [H, L])
        change = sb("ae_change", [H, 1])
        diag = sb("ae_diag", [H, H])
        under = sb("ae_under", [P, UH + H])
        weight = [sb(f"ae_weight{k}", [P, UH + H]) for k in range(2)]
        terms = [sb(f"ae_terms{k}", [P, U, H, cols]) for k in range(2)]
        turn = ps("ae_turn", [P, L])
        found = [ps(f"ae_found{k}", [P, 512]) for k in range(2)]
        total = [ps(f"ae_total{b}", [P, 512]) for b in range(banks)]
        index_ready = sem("ae_index_ready")
        begun = sem("ae_begun")
        gathered = [sem(f"ae_gathered{h}") for h in range(Q)]
        rows_in = [sem(f"ae_rows_in{k}") for k in range(2)]
        cuts_in = [sem(f"ae_cuts_in{k}") for k in range(2)]
        low_t_ready = sem("ae_low_t_ready")
        low_ready = sem("ae_low_ready")
        looked = sem("ae_looked")
        chain = sem("ae_chain")
        scored = sem("ae_scored")
        parts_ready = sem("ae_parts_ready")
        loading = sem("ae_loading")
        turning = sem("ae_turning")
        turned = sem("ae_turned")
        scanned = sem("ae_scanned")
        back_done = sem("ae_back_done")
        lowered = sem("ae_lowered")
        weighed = sem("ae_weighed")
        weights_ready = sem("ae_weights_ready")
        dve_ready = sem("ae_dve_terms_ready")
        act_ready = sem("ae_act_terms_ready")
        totalled = sem("ae_totalled")
        added = sem("ae_added")
        cleared = sem("ae_cleared")
        with nc.Block() as block:
            @block.sync
            def _(sp):
                def load_rows(i, h):
                    sp.dma_start(rows[h % 2][:, :, :].rearrange("p u e -> p (u e)"), row_bcast(
                        S.low_rows[bass.ds((i * Q + h) * U, U), :].rearrange(
                            "u e -> (u e)"))).then_inc(rows_in[h % 2], 16)

                def load_cuts(i, h):
                    sp.dma_start(cuts[h % 2][:, :], row_bcast(S.cuts[bass.ds((i * Q + h) * L, L + 1)],
                                                              H)).then_inc(cuts_in[h % 2], 16)

                def step(i):
                    for h in range(Q):
                        if not isinstance(i, int) or h >= 2:
                            sp.wait_ge(low_t_ready, i * Q + h - 1)
                            sp.sem_inc(loading, 1)
                            load_rows(i, h)
                            sp.wait_ge(scanned, i * Q + h - 1)
                            sp.sem_inc(loading, 1)
                            load_cuts(i, h)
                        else:
                            load_rows(i, h)
                            load_cuts(i, h)

                live = live_steps(sp, S, steps)
                each_step(sp, steps, step, live)
                sp.wait_ge(low_t_ready, live * Q)
                sp.sem_inc(loading, 1)
                load_rows(live, 0)
                load_rows(live, 1)
                sp.wait_ge(scanned, live * Q)
                sp.sem_inc(loading, 1)
                load_cuts(live, 0)
                for k in range(2):
                    sp.wait_ge(rows_in[k], live * (8 * Q) + 16)
                    sp.sem_inc(loading, 1)
                sp.wait_ge(cuts_in[0], live * (8 * Q) + 16)
                sp.sem_inc(loading, 1)

            @block.gpsimd
            def _(pool):
                nc.gpsimd.memset(S.sums[:, :], 0.0).then_inc(cleared, 1)

                def gather(h):
                    for u in range(U):
                        nc.gpsimd.indirect_dma_start(
                            got[h][:, u, :], None, S.table,
                            bass.IndirectOffsetOnAxis(ap=index[h][:, u:u + 1], axis=0)).then_inc(gathered[h], 16)

                def step(i):
                    for h in range(Q):
                        if g is REL:
                            wait_before_reuse(pool, act_ready, i, Q * lent, (h - Q + 1) * lent)
                            pool.sem_inc(begun, 1)
                        pool.wait_ge(index_ready, i * Q + h + 1)
                        pool.sem_inc(begun, 1)
                        gather(h)

                live = live_steps(pool, S, steps)
                each_step(pool, steps, step, live)
                if g is REL:
                    pool.wait_ge(act_ready, live * (Q * lent))
                    pool.sem_inc(begun, 1)
                pool.wait_ge(index_ready, live * Q + 1)
                pool.sem_inc(begun, 1)
                gather(0)

            @block.vector
            def _(dve):
                def next_index(i, h):
                    nc.vector.tensor_copy(index[h][:, :],
                                          S.slot_row[:, bass.ds((i * Q + h) * U, U)]).then_inc(index_ready, 1)

                def compare(i, h):
                    if g is REL:
                        onehot(nc, C, type1[h % 2][:, :, :], S.slot_type[:, bass.ds((i * Q + h) * U, 1)], R)
                    dve.wait_ge(rows_in[h % 2], i * (8 * Q) + h // 2 * 16 + 16)
                    nc.vector.tensor_scalar(first1[h % 2][:, :], rows[h % 2][:, 0, 0:1], C.part[:, 0:1], None,
                                            ALU.is_equal)
                    nc.vector.tensor_scalar(low_t[h % 2][:, :, :], rows[h % 2][:, :, :], C.part[:, 0:1], None,
                                            ALU.is_equal).then_inc(low_t_ready, 1)

                def compare_low(i, h, first, n):
                    return nc.vector.tensor_tensor(
                        low[h % 2][:, first:first + n, :],
                        bc(S.slot_low[:, bass.ds((i * Q + h) * U + first, 1)], [1, n], [0, P]),
                        bc(C.count[:, 0:1], [0, n], [1, P]), ALU.is_equal)

                def pick_own(i, h, ch):
                    dve.wait_ge(looked, i * Q + h + 1)
                    ch.give(nc.vector.tensor_tensor(
                        pick[:, :, :, :], found[h % 2][:, 0:U * g.er].rearrange("p (u r h) -> p u r h", r=R, h=H),
                        bc(type1[h % 2][:, 0, 0:1], [R, U], [1, R], [0, H]), ALU.mult))

                def sum_own(i, h, ch):
                    if g is REL:
                        ch.take()
                        terms = pick[:, :, :, :].rearrange("p u r h -> p u h r")
                    else:
                        dve.wait_ge(looked, i * Q + h + 1)
                        terms = found[h % 2][:, 0:U * PARTS * H].rearrange("p (u k h) -> p u h k", k=PARTS, h=H)
                    ch.give(nc.vector.tensor_reduce(dest[:, :, :], terms, AX, ALU.add))

                def add_source(i, h, ch):
                    dve.wait_ge(gathered[h], (i * 16 + 16) * U)
                    ch.take()
                    ch.give(nc.vector.tensor_tensor(both[:, :, :], dest[:, :, :], got[h][:, :, g.feats:g.out], ALU.add))

                def leak(ch):
                    ch.take()
                    flat = both[:, :, :].rearrange("p u h -> p (u h)")
                    nc.vector.scalar_tensor_tensor(score[:, :], flat, SLOPE, flat, ALU.mult, ALU.max).then_inc(scored, 1)

                def reverse(ap):
                    last = ap[:, L - 1:L]
                    return bass.AP(last.tensor, last.offset, [list(last.ap[0]), [-1, L]])

                def scan_on(i, h, ch):
                    k = h % 2
                    dve.wait_ge(turned, i * Q + h + 1)
                    dve.wait_ge(cuts_in[k], i * (8 * Q) + h // 2 * 16 + 16)
                    ch.give(nc.vector.tensor_tensor_scan(upto[k][:, :], cuts[k][:, 0:L], turn[0:H, :],
                                                         upto[1 - k][:, L - 1:L], ALU.add, ALU.max))

                def scan_back(h, ch):
                    ch.take()
                    k = h % 2
                    nc.vector.tensor_tensor_scan(reverse(peak[:, :]), reverse(cuts[k][:, 1:]), reverse(upto[k][:, :]),
                                                 -BIG, ALU.add, ALU.max).then_inc(scanned, 1)

                def compare_carry(i, h, ch):
                    dve.wait_ge(scanned, i * Q + h + 1)
                    ch.give(nc.vector.tensor_tensor(change[:, :], upto[1 - h % 2][:, L - 1:L], peak[:, 0:1],
                                                    ALU.subtract))

                def spread_carry(ch):
                    ch.take()
                    ch.give(nc.vector.tensor_scalar(diag[:, :], C.ident[0:H, 0:H], change[:, 0:1], 0.0, ALU.mult,
                                                    ALU.min))

                def lower(i, h):
                    dve.wait_ge(back_done, i * Q + h + 1)
                    back = found[h % 2][:, BACK:BACK + UH + H]
                    nc.vector.tensor_tensor(under[:, 0:UH], score[:, :], back[:, 0:UH], ALU.subtract)
                    nc.vector.tensor_scalar(under[:, UH:UH + H], back[:, UH:UH + H], first1[h % 2][:, 0:1], None,
                                            ALU.mult).then_inc(lowered, 1)

                def weigh(i, h):
                    dve.wait_ge(weighed, i * Q + h + 1)
                    nc.vector.tensor_tensor(
                        terms[h % 2][:, 0:own, :, 0:hd],
                        got[h][:, 0:own, 0:g.feats].rearrange("p u (h d) -> p u h d", h=H),
                        bc(weight[h % 2][:, 0:1], [H, own], [1, H], [0, hd]), ALU.mult).then_inc(dve_ready, 1)

                def rescale(i, h, place):
                    dve.wait_ge(weighed, i * Q + h + 1)
                    if not (isinstance(i, int) and h == 0):
                        dve.wait_ge(added, (i * Q + h) * (U + 1))
                    sums = S.sums[:, bass.ds(place, g.out)].rearrange("p (h c) -> p h c", h=H)
                    nc.vector.tensor_tensor(sums, sums, bc(weight[h % 2][:, UH:UH + 1], [1, H], [0, cols]),
                                            ALU.mult).then_inc(added, 1)

                def add(i, h, u, place):
                    n = h * U + u
                    dve.wait_ge(totalled, i * (Q * U) + n + 1)
                    dve.wait_ge(added, i * (Q * (U + 1)) + h * (U + 1) + u + 1)
                    sums = S.sums[:, bass.ds(place, g.out)]
                    nc.vector.tensor_tensor(sums, sums, total[n % banks][:, 0:g.out], ALU.add).then_inc(added, 1)

                links = 6 if g is REL else 5
                half = U // 2

                def step(i):
                    ch = Chain(dve, chain, i, Q * links, 1 + links)
                    for h in range(Q):
                        one, two = later(i, h, 1), later(i, h, 2)
                        last = later(i, h, -1)
                        late = not (isinstance(i, int) and h == 0)
                        if late:
                            at = places(dve, S, 1, (i * Q + h) * U - half, g.out)
                        else:
                            at = [None] * half + list(places(dve, S, 1, 0, g.out, half))
                        if own:
                            weigh(i, h)
                        if late and g is ROUTE:
                            add(*last, half, at[0])
                        dve.wait_ge(lowered, i * Q + h + 1)
                        compare(*two)
                        if late and g is REL:
                            add(*last, half, at[0])
                        if g is REL:
                            pick_own(*one, ch)
                        if late:
                            add(*last, half + 1, at[1])
                        sum_own(*one, ch)
                        if late:
                            add(*last, half + 2, at[2])
                        add_source(*one, ch)
                        next_index(i + 1, h)
                        if late and g is REL:
                            add(*last, half + 3, at[3])
                        leak(ch)
                        if late and g is ROUTE:
                            add(*last, half + 3, at[3])
                        rescale(i, h, at[half])
                        compare_low(*one, 0, U).then_inc(low_ready, 1)
                        scan_on(*one, ch)
                        add(i, h, 0, at[half])
                        scan_back(one[1], ch)
                        add(i, h, 1, at[half + 1])
                        compare_carry(*one, ch)
                        add(i, h, 2, at[half + 2])
                        spread_carry(ch)
                        add(i, h, 3, at[half + 3])
                        lower(*one)
                    ch.end()

                split = Chain(dve, parts_ready)
                whole = S.dest_table[:, :].rearrange("p (b r) -> p b r", b=NB)
                for k in range(PARTS):
                    split.link(nc.vector.tensor_copy(dest_parts[:, :, k, :], whole))
                    if k < PARTS - 1:
                        split.link(nc.vector.tensor_tensor(whole, whole, dest_parts[:, :, k, :], ALU.subtract))
                first = Chain(dve, chain)
                first.link(nc.vector.memset(upto[1][:, :], -BIG))
                for h in range(Q):
                    next_index(0, h)
                compare(0, 0)
                compare(0, 1)
                if g is REL:
                    pick_own(0, 0, first)
                sum_own(0, 0, first)
                add_source(0, 0, first)
                leak(first)
                scan_on(0, 0, first)
                scan_back(0, first)
                compare_carry(0, 0, first)
                spread_carry(first)
                lower(0, 0)
                compare_low(0, 0, 0, U).then_inc(low_ready, 1)
                dve.wait_ge(cleared, 1)
                each_step(dve, steps, step, live_steps(dve, S, steps))
                last = last_step(dve, S, steps)
                at = places(dve, S, 1, (last * Q + (Q - 1)) * U + half, g.out, half)
                for u in range(half):
                    add(last, Q - 1, half + u, at[u])

            @block.tensor
            def _(pe):
                def look_up(i, h):
                    width = g.er if g is REL else PARTS * g.er
                    at = places(pe, S, 0, (i * Q + h) * U, PARTS * g.er)
                    table = dest_parts[:, :, :, :].rearrange("p b k r -> p (b k r)")
                    pe.wait_ge(low_t_ready, i * Q + h + 1)
                    for u in range(U):
                        block_parts = table[:, bass.ds(at[u], PARTS * g.er)]
                        for k in range(0, PARTS * g.er, width):
                            last = nc.tensor.matmul(found[h % 2][:, u * width:(u + 1) * width], low_t[h % 2][:, u, :],
                                                    block_parts[:, k:k + width], start=(k == 0),
                                                    stop=(k + width == PARTS * g.er))
                    last.then_inc(looked, 1)

                def turn_scores(i, h):
                    pe.wait_ge(scored, i * Q + h + 1)
                    pe.sem_inc(turning, 1)
                    for u in range(U):
                        last = nc.tensor.transpose(turn[0:H, u * P:(u + 1) * P], score[:, u * H:(u + 1) * H],
                                                   C.ident[:, :])
                    last.then_inc(turned, 1)

                def turn_back(i, h, links):
                    pe.wait_ge(scanned, i * Q + h + 1)
                    pe.sem_inc(turning, 1)
                    back = found[h % 2][:, BACK:BACK + UH + H]
                    for u in range(U):
                        nc.tensor.transpose(back[:, u * H:(u + 1) * H], peak[:, u * P:(u + 1) * P],
                                            C.ident[0:H, 0:H])
                    pe.wait_ge(chain, links)
                    nc.tensor.matmul(back[:, UH:UH + H], C.ones[0:H, :], diag[:, :], start=True,
                                     stop=True).then_inc(back_done, 1)

                links = 6 if g is REL else 5

                def sum_chunks(i, h, first, n):
                    for u in range(first, first + n):
                        if u >= own:
                            pe.wait_ge(act_ready, i * (Q * lent) + h * lent + u - own + 1)
                        at = h * U + u
                        if not (isinstance(i, int) and at < banks):
                            before = at - banks
                            pe.wait_ge(added, i * (Q * (U + 1)) + before // U * (U + 1) + before % U + 2)
                        nc.tensor.matmul(total[at % banks][:, 0:g.out], low[h % 2][:, u, :],
                                         terms[h % 2][:, u, :, :].rearrange("p h c -> p (h c)"), start=True,
                                         stop=True).then_inc(totalled, 1)

                def step(i):
                    for h in range(Q):
                        one, two = later(i, h, 1), later(i, h, 2)
                        look_up(*two)
                        turn_scores(*one)
                        pe.wait_ge(low_ready, i * Q + h + 1)
                        if own:
                            pe.wait_ge(dve_ready, i * Q + h + 1)
                        pe.wait_ge(weights_ready, i * Q + h + 1)
                        sum_chunks(i, h, 0, U // 2)
                        turn_back(*one, i * (Q * links) + (h + 2) * links + 1)
                        sum_chunks(i, h, U // 2, U // 2)

                pe.wait_ge(parts_ready, 2 * PARTS - 1)
                look_up(0, 0)
                look_up(0, 1)
                turn_scores(0, 0)
                turn_back(0, 0, links + 1)
                each_step(pe, steps, step, live_steps(pe, S, steps))

            @block.scalar
            def _(act):
                def exponentials(i, h):
                    act.wait_ge(lowered, i * Q + h + 1)
                    nc.scalar.activation(weight[h % 2][:, :], under[:, :], ACT.Exp).then_inc(weighed, 1)

                def step(i):
                    for h in range(Q):
                        k = h % 2
                        act.wait_ge(weighed, i * Q + h + 1)
                        if not isinstance(i, int) or h >= 2:
                            act.wait_ge(totalled, i * (Q * U) + (h - 1) * U)
                        by_head = weight[k][:, 0:UH].rearrange("p (u h) -> p u h", h=H)
                        nc.scalar.copy(terms[k][:, :, :, hd], by_head).then_inc(weights_ready, 1)
                        if g is REL:
                            act.wait_ge(gathered[h], (i * 16 + 16) * U)
                            for u in range(own, U):
                                for a in range(H):
                                    ins = nc.scalar.activation(terms[k][:, u, a, 0:hd],
                                                               got[h][:, u, a * hd:(a + 1) * hd], ACT.Copy,
                                                               scale=weight[k][:, u * H + a:u * H + a + 1])
                                ins.then_inc(act_ready, 1)
                        exponentials(*later(i, h, 1))

                exponentials(0, 0)
                each_step(act, steps, step, live_steps(act, S, steps))


def normalise(nc, C, S, name, edges=None):
    half = NB // 2
    squares = NB - NB // 4
    scales = NB * 3 // 5
    with stage(nc) as (sb, ps, sem):
        square = sb(f"{name}_square", [P, NB - squares, D])
        scrap = [sb(f"{name}_scrap{k}", [P, D]) for k in range(2)]
        mean = sb(f"{name}_mean", [P, NB])
        var = sb(f"{name}_var", [P, NB])
        std = sb(f"{name}_std", [P, NB])
        inverse = sb(f"{name}_inverse", [P, NB])
        chain = sem(f"{name}_chain")
        summed = sem(f"{name}_summed")
        centred = sem(f"{name}_centred")
        squared = sem(f"{name}_squared")
        var_ready = sem(f"{name}_var_ready")
        std_ready = sem(f"{name}_std_ready")
        inverse_ready = sem(f"{name}_inverse_ready")
        loaded = sem(f"{name}_loaded")
        with nc.Block() as block:
            @block.sync
            def _(sp):
                if edges:
                    for k, to in enumerate(prepared(edges)):
                        sp.dma_start(to[:, :].bitcast(I32) if k < 3 else to[:, :],
                                     edges.prepared_dram[k]).then_inc(loaded, 16)
                    sp.wait_ge(loaded, 16 * len(prepared(edges)))

            @block.vector
            def _(dve):
                ch = Chain(dve, chain)

                def centre(first, n):
                    ch.link(nc.vector.tensor_scalar(mean[:, first:first + n], mean[:, first:first + n], 1.0 / D, None,
                                                    ALU.mult))
                    nc.vector.tensor_tensor(S.normed[:, first:first + n, :], S.x[:, first:first + n, :],
                                            bc(mean[:, first:first + 1], [1, n], [0, D]), ALU.subtract).then_inc(
                        centred, 1)

                ch.link(nc.vector.tensor_reduce(mean[:, 0:half], S.x[:, 0:half, :], AX, ALU.add))
                centre(0, half)
                dve.wait_ge(summed, NB - half)
                centre(half, NB - half)
                dve.wait_ge(centred, 2)
                ch.link(nc.vector.tensor_tensor(square[:, :, :], S.normed[:, squares:, :], S.normed[:, squares:, :],
                                                ALU.mult))
                ch.link(nc.vector.tensor_reduce(var[:, squares:], square[:, :, :], AX, ALU.add))
                dve.wait_ge(squared, squares)
                nc.vector.tensor_scalar(var[:, :], var[:, :], 1.0 / D, EPS, ALU.mult, ALU.add).then_inc(var_ready, 1)
                dve.wait_ge(std_ready, 1)
                nc.vector.reciprocal(inverse[:, :], std[:, :]).then_inc(inverse_ready, 1)
                dve.wait_ge(inverse_ready, 1)
                nc.vector.tensor_tensor(S.normed[:, 0:scales, :], S.normed[:, 0:scales, :],
                                        bc(inverse[:, 0:1], [1, scales], [0, D]), ALU.mult)

            @block.scalar
            def _(act):
                def scrap_for(n):
                    if n >= 2:
                        act.wait_ge(summed if n <= NB - half + 1 else squared, n - 1 if n <= NB - half + 1 else
                                    n - 1 - (NB - half))
                    return scrap[n % 2][:, :]

                for n in range(NB - half):
                    nc.scalar.activation(scrap_for(n), S.x[:, half + n, :], ACT.Copy,
                                         accum_out=mean[:, half + n:half + n + 1]).then_inc(summed, 1)
                for b in range(squares):
                    act.wait_ge(centred, 1 if b < half else 2)
                    nc.scalar.activation(scrap_for(NB - half + b), S.normed[:, b, :], ACT.Square,
                                         accum_out=var[:, b:b + 1]).then_inc(squared, 1)
                act.wait_ge(var_ready, 1)
                nc.scalar.activation(std[:, :], var[:, :], ACT.Sqrt).then_inc(std_ready, 1)
                act.wait_ge(inverse_ready, 1)
                for b in range(scales, NB):
                    nc.scalar.activation(S.normed[:, b, :], S.normed[:, b, :], ACT.Copy, scale=inverse[:, b:b + 1])


def load_nodes(nc, S, x_in):
    last = N - (NB - 1) * P
    with stage(nc) as (_, _, sem):
        cleared = sem("ln_cleared")
        loaded = sem("ln_loaded")
        with nc.Block() as block:
            @block.gpsimd
            def _(pool):
                nc.gpsimd.memset(S.x[:, NB - 1, :], 0.0).then_inc(cleared, 1)

            @block.sync
            def _(sp):
                sp.dma_start(S.x[:, 0:NB - 1, :],
                             x_in[0:(NB - 1) * P, :].rearrange("(t p) d -> p t d", p=P)).then_inc(loaded, 16)
                sp.wait_ge(cleared, 1)
                sp.dma_start(S.x[0:last, NB - 1, :], x_in[(NB - 1) * P:N, :]).then_inc(loaded, 16)
                sp.wait_ge(loaded, 32)


def add_attention(nc, C, S, bias_in):
    with stage(nc) as (sb, ps, sem):
        bias = sb("aa_bias", [P, D])
        inverse = sb("aa_inverse", [P, NB, H])
        loaded = sem("aa_loaded")
        chain = sem("aa_chain")
        with nc.Block() as block:
            @block.sync
            def _(sp):
                sp.dma_start(bias[:, :], row_bcast(bias_in)).then_inc(loaded, 16)

            @block.vector
            def _(dve):
                ch = Chain(dve, chain)
                sums = S.sums[:, :].rearrange("p (b h c) -> p b h c", b=NB, h=H)
                ch.link(nc.vector.tensor_scalar(inverse[:, :, :], sums[:, :, :, HD], 0.5, None, ALU.max))
                ch.link(nc.vector.reciprocal(inverse[:, :, :], inverse[:, :, :]))
                heads = sums[:, :, :, 0:HD]
                ch.link(nc.vector.tensor_tensor(heads, heads, bc(inverse[:, 0, 0:1], [H, NB], [1, H], [0, HD]), ALU.mult))
                dve.wait_ge(loaded, 16)
                ch.link(nc.vector.tensor_tensor(heads, heads, bc(bias[:, 0:1], [0, NB], [HD, H], [1, HD]), ALU.add))
                x = S.x[:, :, :].rearrange("p b (h d) -> p b h d", h=H)
                ch.link(nc.vector.tensor_tensor(x, x, heads, ALU.add))


def fold_routing(nc, w, w_in, src_in, dst_in):
    with stage(nc) as (sb, _, sem):
        att = sb("fr_att", [P, 2, XH])
        prod = sb("fr_prod", [P, KC, XH])
        loaded = sem("fr_loaded")
        chain = sem("fr_chain")
        with nc.Block() as block:
            @block.sync
            def _(sp):
                sp.dma_start(w[:, :, 0:XH], w_in.rearrange("(k p) c -> p k c", p=P)).then_inc(loaded, 16)
                for s, a in enumerate((src_in, dst_in)):
                    sp.dma_start(att[:, s, :], row_bcast(a.rearrange("h x -> (h x)"))).then_inc(loaded, 16)

            @block.vector
            def _(dve):
                ch = Chain(dve, chain)
                dve.wait_ge(loaded, 48)
                for s in range(2):
                    ch.link(nc.vector.tensor_tensor(prod[:, :, :], w[:, :, 0:XH], bc(att[:, s, 0:1], [0, KC], [1, XH]),
                                                    ALU.mult))
                    ch.link(nc.vector.tensor_reduce(w[:, :, XH + s * H:XH + (s + 1) * H],
                                                    prod[:, :, :].rearrange("p k (h x) -> p k h x", x=X), AX, ALU.add))


def route(nc, C, S, bias_in, gamma_in, beta_in):
    with stage(nc) as (sb, ps, sem):
        rows = sb("ro_rows", [P, 3, XH])
        agg = sb("ro_agg", [P, NB, XH])
        square = sb("ro_square", [P, NB, XH])
        inverse = sb("ro_inverse", [P, NB, H])
        mean = sb("ro_mean", [P, NB])
        var = sb("ro_var", [P, NB])
        std = sb("ro_std", [P, NB])
        score = sb("ro_score", [P, NB, X])
        better = sb("ro_better", [P, NB, X])
        worse = sb("ro_worse", [P, NB])
        rank = sb("ro_rank", [P, NB, X])
        best = sb("ro_best", [P, NB])
        power = sb("ro_power", [P, NB, X])
        loaded = sem("ro_loaded")
        chain = sem("ro_chain")
        var_ready = sem("ro_var_ready")
        std_ready = sem("ro_std_ready")
        shifted = sem("ro_shifted")
        powered = sem("ro_powered")
        with nc.Block() as block:
            @block.sync
            def _(sp):
                for s, a in enumerate((bias_in, gamma_in, beta_in)):
                    sp.dma_start(rows[:, s, :], row_bcast(a)).then_inc(loaded, 16)

            @block.scalar
            def _(act):
                act.wait_ge(var_ready, 1)
                nc.scalar.activation(std[:, :], var[:, :], ACT.Sqrt).then_inc(std_ready, 1)
                act.wait_ge(shifted, 1)
                nc.scalar.activation(power[:, :, :].rearrange("p b x -> p (b x)"),
                                     score[:, :, :].rearrange("p b x -> p (b x)"), ACT.Exp).then_inc(powered, 1)

            @block.vector
            def _(dve):
                ch = Chain(dve, chain)
                sums = S.sums[:, :].rearrange("p (b h c) -> p b h c", b=NB, h=H)

                def row(s):
                    return bc(rows[:, s, 0:1], [0, NB], [1, XH])

                def per_node(ap, n=XH):
                    return bc(ap[:, 0:1], [1, NB], [0, n])

                ch.link(nc.vector.tensor_scalar(inverse[:, :, :], sums[:, :, :, X], 1e-16, None, ALU.add))
                ch.link(nc.vector.reciprocal(inverse[:, :, :], inverse[:, :, :]))
                ch.link(nc.vector.tensor_tensor(agg[:, :, :].rearrange("p b (h x) -> p b h x", h=H),
                                                sums[:, :, :, 0:X],
                                                bc(inverse[:, 0, 0:1], [H, NB], [1, H], [0, X]), ALU.mult))
                dve.wait_ge(loaded, 48)
                ch.link(nc.vector.tensor_tensor(agg[:, :, :], agg[:, :, :], row(0), ALU.add))
                ch.link(nc.vector.tensor_reduce(mean[:, :], agg[:, :, :], AX, ALU.add))
                ch.link(nc.vector.tensor_scalar(mean[:, :], mean[:, :], 1.0 / XH, None, ALU.mult))
                ch.link(nc.vector.tensor_tensor(agg[:, :, :], agg[:, :, :], per_node(mean), ALU.subtract))
                ch.link(nc.vector.tensor_tensor(square[:, :, :], agg[:, :, :], agg[:, :, :], ALU.mult))
                ch.link(nc.vector.tensor_reduce(var[:, :], square[:, :, :], AX, ALU.add))
                nc.vector.tensor_scalar(var[:, :], var[:, :], 1.0 / XH, EPS, ALU.mult, ALU.add).then_inc(var_ready, 1)
                dve.wait_ge(std_ready, 1)
                ch.link(nc.vector.reciprocal(var[:, :], std[:, :]))
                ch.link(nc.vector.tensor_tensor(agg[:, :, :], agg[:, :, :], per_node(var), ALU.mult))
                ch.link(nc.vector.tensor_tensor(agg[:, :, :], agg[:, :, :], row(1), ALU.mult))
                ch.link(nc.vector.tensor_tensor(agg[:, :, :], agg[:, :, :], row(2), ALU.add))
                ch.link(nc.vector.tensor_reduce(score[:, :, :], agg[:, :, :].rearrange("p b (h x) -> p b x h", h=H), AX,
                                                ALU.add))
                ch.link(nc.vector.tensor_scalar(score[:, :, :], score[:, :, :], 1.0 / H, None, ALU.mult))
                for x in range(X):
                    one = bc(score[:, 0, x:x + 1], [X, NB], [0, X])
                    ch.link(nc.vector.tensor_tensor(better[:, :, :], score[:, :, :], one, ALU.is_gt))
                    if x:
                        ch.link(nc.vector.tensor_tensor(better[:, :, 0:x], score[:, :, 0:x],
                                                        bc(score[:, 0, x:x + 1], [X, NB], [0, x]), ALU.is_ge))
                    ch.link(nc.vector.tensor_reduce(rank[:, :, x], better[:, :, :], AX, ALU.add))
                ch.link(nc.vector.tensor_reduce(best[:, :], score[:, :, :], AX, ALU.max))
                nc.vector.tensor_tensor(score[:, :, :], score[:, :, :], per_node(best, X),
                                        ALU.subtract).then_inc(shifted, 1)
                dve.wait_ge(powered, 1)
                ch.link(nc.vector.tensor_scalar(rank[:, :, :], rank[:, :, :], 1.5, None, ALU.is_lt))
                ch.link(nc.vector.tensor_tensor(power[:, :, :], power[:, :, :], rank[:, :, :], ALU.mult))
                ch.link(nc.vector.tensor_reduce(worse[:, :], power[:, :, :], AX, ALU.add))
                ch.link(nc.vector.reciprocal(worse[:, :], worse[:, :]))
                ch.link(nc.vector.tensor_tensor(S.gate[:, :, :], power[:, :, :], per_node(worse, X), ALU.mult))


GT = 3


def add_experts(nc, S, out):
    last = N - (NB - 1) * P
    steps = NB // (2 * GT)
    with stage(nc) as (sb, _, sem):
        results = [sb(f"ax_results{h}", [P, GT, X, D]) for h in range(2)]
        loaded = [sem(f"ax_loaded{h}") for h in range(2)]
        added = sem("ax_added")
        stored = sem("ax_stored")
        with nc.Block() as block:
            @block.sync
            def _(sp):
                def step(i):
                    for h in range(2):
                        wait_before_reuse(sp, added, i, 2 * GT * X, (h - 1) * GT * X)
                        for v in range(X // 2):
                            rows = S.expert_out[bass.ds((i * 2 + h) * (GT * P) + v * (NB * P), GT * P), :, :]
                            sp.dma_start(results[h][:, :, 2 * v:2 * v + 2, :],
                                         rows.rearrange("(t p) x d -> p t x d", p=P)).then_inc(loaded[h], 16)

                    if not (isinstance(i, int) and i == 0):
                        sp.dma_start(out[bass.ds((i - 1) * (2 * GT * P), 2 * GT * P), :].rearrange(
                            "(t p) d -> p t d", p=P), S.x[:, bass.ds((i - 1) * (2 * GT), 2 * GT), :]).then_inc(stored, 16)

                each_step(sp, steps, step)
                sp.wait_ge(added, NB * X)
                first = NB - 2 * GT
                sp.dma_start(out[first * P:(NB - 1) * P, :].rearrange("(t p) d -> p t d", p=P),
                             S.x[:, first:NB - 1, :]).then_inc(stored, 16)
                sp.dma_start(out[(NB - 1) * P:N, :], S.x[0:last, NB - 1, :]).then_inc(stored, 16)
                sp.wait_ge(stored, 16 * (steps + 1))

            @block.vector
            def _(dve):
                def step(i):
                    for h in range(2):
                        dve.wait_ge(loaded[h], i * 32 + 32)
                        for x in range(X):
                            for t in range(GT):
                                n = h * GT * X + x * GT + t
                                if x:
                                    dve.wait_ge(added, i * (2 * GT * X) + n - GT + 1)
                                at = i * (2 * GT) + h * GT + t
                                row = S.x[:, bass.ds(at, 1), :].rearrange("p t d -> p (t d)")
                                gate = S.gate[:, bass.ds(at, 1), x:x + 1].rearrange("p t o -> p (t o)")
                                nc.vector.scalar_tensor_tensor(row, results[h][:, t, x, :], gate, row, ALU.mult,
                                                               ALU.add).then_inc(added, 1)

                each_step(dve, steps, step)


class Space:
    pass


def graph_space(nc, g):
    S = Space()

    def dram(name, shape, dt=F32):
        return nc.dram_tensor(f"{g.name}_{name}", shape, dt, kind="Internal").ap()

    S.key_rows = dram("key_rows", [g.raw_tiles * P, 2, P], U16)
    S.prepared_dram = dram("prepared", [4, P, g.raw_tiles * P], I32) if g is ROUTE else None
    S.sorted = dram("sorted", [g.tiles * P * P + 1, 1], I32)
    S.cuts = dram("cuts", [g.tiles * P * P + 1])
    S.low_rows = dram("low_rows", [g.tiles * P, P], U16)
    S.place_dram = dram("place", [2, g.tiles * P], I32)
    S.live_dram = dram("live_steps", [1, 2], I32)
    S.table = dram("table", [NB * P * g.rels, g.out])
    return S


def attend(nc, C, g, S, nodes, src, dst, typ, prepare, finish):
    with stage(nc, g.name + "_") as (sb, _, _):
        S.start = sb("start", [P, NBP])
        S.live = sb("live", [1, 2], I32)
        S.place_row = sb("place_row", [1, 2, g.tiles * P], I32)
        S.dest_table = sb("dest_table", [P, NB * g.er])
        S.sums = sb("sums", [P, NB * g.out])
        with stage(nc, g.name + "_") as (sb, _, _):
            S.normed = nodes.normed = sb("normed", [P, NB, D])
            if g is REL:
                normalise(nc, C, nodes, g.name)
            with stage(nc, g.name + "_") as (sb, _, _):
                W = g.raw_tiles * P
                S.lo, S.hi, S.key = (sb(name, [P, W]) for name in ("lo", "hi", "key"))
                S.packed = sb("packed", [P, W], I32)
                if g is REL:
                    prepare_edges(nc, C, g, S, src, dst, typ)
                else:
                    normalise(nc, C, nodes, g.name, edges=S)
                beside = prepare(S, sb)
                place_slots(nc, C, g, S)
                scatter_edges(nc, C, g, S, *beside)
        with stage(nc, g.name + "_") as (sb, _, _):
            W = g.tiles * P
            S.slot_row = sb("slot_row", [P, W], I32)
            S.slot_low = sb("slot_low", [P, W])
            S.slot_type = sb("slot_type", [P, W]) if g is REL else None
            read_slots(nc, C, g, S)
            attend_edges(nc, C, g, S)
        finish(S)


def gnn_moe_kernel(nc, x, src, dst, edge_type, conv_w, attn_l, attn_r, h_bias, w_gat, att_src, att_dst, b_gat,
                   ln_gamma, ln_beta, w1, b1, w2, b2, edge_index, out):
    rel, routing = graph_space(nc, REL), graph_space(nc, ROUTE)
    with stage(nc) as (sb, _, _):
        C = Space()
        C.ident = sb("ident", [P, P])
        C.before = sb("before", [P, P])
        C.after = sb("after", [P, P])
        C.ones = sb("ones", [P, P])
        C.zero_bf = sb("zero_bf", [P, P], BF16)
        C.count_i = sb("count_i", [P, P], I32)
        C.part_i = sb("part_i", [P, 1], I32)
        C.count = sb("count", [P, P])
        C.part = sb("part", [P, 1])
        nodes = Space()
        nodes.x = sb("x_nodes", [P, NB, D])
        nodes.gate = sb("gate", [P, NB, X])
        nodes.expert_out = nc.dram_tensor("expert_out", [X // 2 * NB * P, 2, D], F32, kind="Internal").ap()
        for S, g in ((rel, REL), (routing, ROUTE)):
            S.counts = sb(g.name + "_counts", [P, NBP])
        constants(nc, C)
        load_nodes(nc, nodes, x)

        def relation_work(S, sb):
            w = sb("w", [P, KC, R, H, HD])
            w_att = sb("w_att", [P, KC, 2 * R * H])
            count_edges(nc, C, REL, S, w, w_att, conv_w, attn_l, attn_r)
            W = ROUTE.raw_tiles * P
            routing.lo, routing.hi, routing.key = (sb("other_" + name, [P, W]) for name in ("lo", "hi", "key"))
            routing.packed = sb("other_packed", [P, W], I32)
            prepare_edges(nc, C, ROUTE, routing, edge_index[0], edge_index[1], None)
            return RelationFeatures(nc, C, S, w, w_att, routing), Counting(nc, C, ROUTE, routing)

        def expert_work(S, sb):
            S.expert_out = nodes.expert_out
            w_route = sb("w_route", [P, KC, XH + 2 * H])
            fold_routing(nc, w_route, w_gat, att_src, att_dst)
            return Experts(nc, C, S, w_route, w1, b1, w2, b2), None

        def finish_relations(S):
            S.x = nodes.x
            add_attention(nc, C, S, h_bias)

        def finish_routing(S):
            S.gate = nodes.gate
            route(nc, C, S, b_gat, ln_gamma, ln_beta)

        attend(nc, C, REL, rel, nodes, src, dst, edge_type, relation_work, finish_relations)
        attend(nc, C, ROUTE, routing, nodes, None, None, None, expert_work,
               finish_routing)
        add_experts(nc, nodes, out)


_INS = ["x", "src", "dst", "edge_type_8", "L0_gnn_conv_weights", "L0_gnn_attn_l", "L0_gnn_attn_r", "L0_gnn_h_bias",
        "L0_ffn_W_gat", "L0_ffn_att_src", "L0_ffn_att_dst", "L0_ffn_b_gat", "L0_ffn_ln_gamma", "L0_ffn_ln_beta",
        "L0_ffn_W1", "L0_ffn_b1", "L0_ffn_W2", "L0_ffn_b2", "L0_ffn_edge_index"]


def kernel(**inputs):
    import numpy as _np
    import concourse.bacc as _bacc
    from concourse import mybir as _mybir
    from concourse.bass_utils import run_bass_kernel_spmd as _run

    nc = _bacc.Bacc("TRN2", target_bir_lowering=False, num_devices=1)
    arrays, args = {}, []
    for name in _INS:
        a = _np.ascontiguousarray(inputs[name])
        arrays[f"in_{name}_dram"] = a
        args.append(nc.dram_tensor(f"in_{name}_dram", a.shape, _mybir.dt.from_np(a.dtype), kind="ExternalInput").ap())
    out = nc.dram_tensor("out_0_dram", (N, D), F32, kind="ExternalOutput").ap()
    gnn_moe_kernel(nc, *args, out)
    r = _run(nc, [arrays], core_ids=[0])
    return r.results[0]["out_0_dram"]
```
